# Optimizing a Trainium2 kernel written in Bass

```python
import numpy as np
import jax
import jax.numpy as jnp

def _softmax(x, axis=-1):
    return jax.nn.softmax(x, axis=axis)

def _gelu(x):
    return jax.nn.gelu(x, approximate=True)

def _silu(x):
    return jax.nn.silu(x)

def _sigmoid(x):
    return jax.nn.sigmoid(x)

def _layernorm(x, axis=-1, eps=1e-05):
    m = jnp.mean(x, axis=axis, keepdims=True)
    v = jnp.var(x, axis=axis, keepdims=True)
    return (x - m) / jnp.sqrt(v + eps)

def _scatter_add(tgt, idx, src, axis=0):
    return tgt.at[idx].add(src)

def _segment_sum(src, seg, n):
    return jax.ops.segment_sum(src, seg, n)
kernel_name = 'mk_gps_d1_gnn_r32_dfda1d'

def setup_inputs(seed: int=0):
    np.random.seed(seed)
    _w = jnp.asarray

    def _rec_inputs():
        import jax
        import jax.numpy as jnp
        _gk = jax.random.key(seed)
        x = -6.415e-05 + 1 * jax.random.normal(jax.random.fold_in(_gk, 1), (625, 512), jnp.float32)
        _s = jax.random.randint(jax.random.fold_in(_gk, 2), (10000,), 0, 625, jnp.int32)
        _d = jax.random.randint(jax.random.fold_in(_gk, 3), (10000,), 0, 625, jnp.int32)
        _loop = jnp.arange(625, dtype=jnp.int32)
        src = jnp.concatenate([_s, _d, _loop])
        dst = jnp.concatenate([_d, _s, _loop])
        _o = jnp.argsort(dst, stable=True)
        src = src[_o]
        dst = dst[_o]
        return (x, src, dst)
    x, src, dst = _rec_inputs()

    def _L0_gnn_setup():
        import jax, jax.numpy as jnp
        import numpy as np
        N, E, H = (625, 5000, 512)
        EPS = 1e-07

        def _ln(x, g, b, eps=1e-05):
            mu = jnp.mean(x, axis=-1, keepdims=True)
            var = jnp.mean((x - mu) ** 2, axis=-1, keepdims=True)
            return (x - mu) * jax.lax.rsqrt(var + eps) * g + b

        def _genconv(x, src, dst, t, w1, b1, lg, lb, w2, b2):
            m = jax.nn.relu(x[src]) + EPS
            z = m * t
            zmax = jax.lax.stop_gradient(jax.ops.segment_max(z, dst, num_segments=N))
            zmax = jnp.where(jnp.isfinite(zmax), zmax, 0.0)
            e = jnp.exp(z - zmax[dst])
            denom = jax.ops.segment_sum(e, dst, num_segments=N)
            alpha = e / (denom[dst] + 1e-16)
            agg = jax.ops.segment_sum(alpha * m, dst, num_segments=N)
            h = agg + x
            h = jax.nn.relu(_ln(h @ w1 + b1, lg, lb))
            return h @ w2 + b2

        def _forward(x, edge_index, p):
            src, dst = (edge_index[0], edge_index[1])
            x1 = _genconv(x, src, dst, *p['c0'])
            x2 = x1 + jax.nn.relu(_ln(_genconv(x1, src, dst, *p['c1']), p['lng_1'], p['lnb_1']))
            x3 = x2 + jax.nn.relu(_ln(_genconv(x2, src, dst, *p['c2']), p['lng_2'], p['lnb_2']))
            return jnp.concatenate([x1, x2, x3], axis=1) @ p['cw'] + p['cb']
        key = jax.random.key(seed)
        ks = iter(jax.random.split(key, 16))
        s = 0.05
        d = {'x': jax.random.normal(next(ks), (N, H), jnp.float32), 'edge_index': jax.random.randint(next(ks), (2, E), 0, N, jnp.int32)}
        for i in range(3):
            d[f't{i}'] = jnp.ones((1,), jnp.float32)
            d[f'mw1_{i}'] = jax.random.normal(next(ks), (H, 2 * H), jnp.float32) * s
            d[f'mb1_{i}'] = jnp.zeros((2 * H,), jnp.float32)
            d[f'mlg_{i}'] = jnp.ones((2 * H,), jnp.float32)
            d[f'mlb_{i}'] = jnp.zeros((2 * H,), jnp.float32)
            d[f'mw2_{i}'] = jax.random.normal(next(ks), (2 * H, H), jnp.float32) * s
            d[f'mb2_{i}'] = jnp.zeros((H,), jnp.float32)
        for i in (1, 2):
            d[f'lng_{i}'] = jnp.ones((H,), jnp.float32)
            d[f'lnb_{i}'] = jnp.zeros((H,), jnp.float32)
        d['cw'] = jax.random.normal(next(ks), (3 * H, H), jnp.float32) * s
        d['cb'] = jnp.zeros((H,), jnp.float32)
        return d
    _L0_gnn_all = _L0_gnn_setup()
    _L0_gnn_in = {k: v for k, v in _L0_gnn_all.items() if k in ('t0', 'mw1_0', 'mb1_0', 'mlg_0', 'mlb_0', 'mw2_0', 'mb2_0', 't1', 'mw1_1', 'mb1_1', 'mlg_1', 'mlb_1', 'mw2_1', 'mb2_1', 't2', 'mw1_2', 'mb1_2', 'mlg_2', 'mlb_2', 'mw2_2', 'mb2_2', 'lng_1', 'lnb_1', 'lng_2', 'lnb_2', 'cw', 'cb')}
    del _L0_gnn_all

    def _L0_mix_setup():
        import jax, jax.numpy as jnp
        import numpy as np
        B, S, D, H, R, P = (4, 256, 512, 8, 64, 4)
        HD = D // H
        EPS = 1e-06

        def _sketch_p4(z, G1, G2):
            inv_sqrt_r = 1.0 / np.sqrt(R).astype(np.float32)
            half = inv_sqrt_r * (z @ G1 * (z @ G2))
            return half * half
        key = jax.random.key(seed)
        ks = jax.random.split(key, 16)
        lin = lambda k: jax.random.normal(k, (D, D), jnp.float32) * (1.0 / np.sqrt(D))
        g = lambda k: jax.random.normal(k, (HD, R), jnp.float32) * (1.0 / np.sqrt(R))
        return {'x': jax.random.normal(ks[0], (B, S, D), jnp.float32), 'Wq': lin(ks[1]), 'bq': jnp.zeros((D,), jnp.float32), 'Wk': lin(ks[2]), 'bk': jnp.zeros((D,), jnp.float32), 'Wv': lin(ks[3]), 'bv': jnp.zeros((D,), jnp.float32), 'Wp': lin(ks[4]), 'bp': jnp.zeros((D,), jnp.float32), 'gamma_q': jnp.ones((1,), jnp.float32), 'beta_q': jnp.zeros((1,), jnp.float32), 'gamma_k': jnp.ones((1,), jnp.float32), 'beta_k': jnp.zeros((1,), jnp.float32), 'qG1': g(ks[5]), 'qG2': g(ks[6]), 'kG1': g(ks[7]), 'kG2': g(ks[8])}
    _L0_mix_all = _L0_mix_setup()
    _L0_mix_in = {k: v for k, v in _L0_mix_all.items() if k in ('Wq', 'bq', 'Wk', 'bk', 'Wv', 'bv', 'Wp', 'bp', 'gamma_q', 'beta_q', 'gamma_k', 'beta_k', 'qG1', 'qG2', 'kG1', 'kG2')}
    del _L0_mix_all

    def _L0_ffn_setup():
        import jax, jax.numpy as jnp
        import numpy as np
        TOP_K = 6
        CAP_FACTOR = 2.0
        key = jax.random.key(seed)
        ks = jax.random.split(key, 9)
        B, S, D, F, E, SH = (4, 64, 512, 256, 64, 2)
        return {'x': jax.random.normal(ks[0], (B, S, D), jnp.float32), 'router_w': jax.random.normal(ks[1], (E, D), jnp.float32) * 0.02, 'bias': jnp.zeros((E,), jnp.float32), 'shared_w_gate': jax.random.normal(ks[2], (SH, F, D), jnp.float32) * 0.02, 'shared_w_up': jax.random.normal(ks[3], (SH, F, D), jnp.float32) * 0.02, 'shared_w_down': jax.random.normal(ks[4], (SH, D, F), jnp.float32) * 0.02, 'w_gate': jax.random.normal(ks[5], (E, F, D), jnp.float32) * 0.02, 'w_up': jax.random.normal(ks[6], (E, F, D), jnp.float32) * 0.02, 'w_down': jax.random.normal(ks[7], (E, D, F), jnp.float32) * 0.02}
    _L0_ffn_all = _L0_ffn_setup()
    _L0_ffn_in = {k: v for k, v in _L0_ffn_all.items() if k in ('router_w', 'bias', 'shared_w_gate', 'shared_w_up', 'shared_w_down', 'w_gate', 'w_up', 'w_down')}
    del _L0_ffn_all
    return {'x': x, 'src': src, 'dst': dst, 'L0_gnn_t0': _L0_gnn_in['t0'], 'L0_gnn_mw1_0': _L0_gnn_in['mw1_0'], 'L0_gnn_mb1_0': _L0_gnn_in['mb1_0'], 'L0_gnn_mlg_0': _L0_gnn_in['mlg_0'], 'L0_gnn_mlb_0': _L0_gnn_in['mlb_0'], 'L0_gnn_mw2_0': _L0_gnn_in['mw2_0'], 'L0_gnn_mb2_0': _L0_gnn_in['mb2_0'], 'L0_gnn_t1': _L0_gnn_in['t1'], 'L0_gnn_mw1_1': _L0_gnn_in['mw1_1'], 'L0_gnn_mb1_1': _L0_gnn_in['mb1_1'], 'L0_gnn_mlg_1': _L0_gnn_in['mlg_1'], 'L0_gnn_mlb_1': _L0_gnn_in['mlb_1'], 'L0_gnn_mw2_1': _L0_gnn_in['mw2_1'], 'L0_gnn_mb2_1': _L0_gnn_in['mb2_1'], 'L0_gnn_t2': _L0_gnn_in['t2'], 'L0_gnn_mw1_2': _L0_gnn_in['mw1_2'], 'L0_gnn_mb1_2': _L0_gnn_in['mb1_2'], 'L0_gnn_mlg_2': _L0_gnn_in['mlg_2'], 'L0_gnn_mlb_2': _L0_gnn_in['mlb_2'], 'L0_gnn_mw2_2': _L0_gnn_in['mw2_2'], 'L0_gnn_mb2_2': _L0_gnn_in['mb2_2'], 'L0_gnn_lng_1': _L0_gnn_in['lng_1'], 'L0_gnn_lnb_1': _L0_gnn_in['lnb_1'], 'L0_gnn_lng_2': _L0_gnn_in['lng_2'], 'L0_gnn_lnb_2': _L0_gnn_in['lnb_2'], 'L0_gnn_cw': _L0_gnn_in['cw'], 'L0_gnn_cb': _L0_gnn_in['cb'], 'L0_mix_Wq': _L0_mix_in['Wq'], 'L0_mix_bq': _L0_mix_in['bq'], 'L0_mix_Wk': _L0_mix_in['Wk'], 'L0_mix_bk': _L0_mix_in['bk'], 'L0_mix_Wv': _L0_mix_in['Wv'], 'L0_mix_bv': _L0_mix_in['bv'], 'L0_mix_Wp': _L0_mix_in['Wp'], 'L0_mix_bp': _L0_mix_in['bp'], 'L0_mix_gamma_q': _L0_mix_in['gamma_q'], 'L0_mix_beta_q': _L0_mix_in['beta_q'], 'L0_mix_gamma_k': _L0_mix_in['gamma_k'], 'L0_mix_beta_k': _L0_mix_in['beta_k'], 'L0_mix_qG1': _L0_mix_in['qG1'], 'L0_mix_qG2': _L0_mix_in['qG2'], 'L0_mix_kG1': _L0_mix_in['kG1'], 'L0_mix_kG2': _L0_mix_in['kG2'], 'L0_ffn_router_w': _L0_ffn_in['router_w'], 'L0_ffn_bias': _L0_ffn_in['bias'], 'L0_ffn_shared_w_gate': _L0_ffn_in['shared_w_gate'], 'L0_ffn_shared_w_up': _L0_ffn_in['shared_w_up'], 'L0_ffn_shared_w_down': _L0_ffn_in['shared_w_down'], 'L0_ffn_w_gate': _L0_ffn_in['w_gate'], 'L0_ffn_w_up': _L0_ffn_in['w_up'], 'L0_ffn_w_down': _L0_ffn_in['w_down']}

def reference(x, src, dst, L0_gnn_t0, L0_gnn_mw1_0, L0_gnn_mb1_0, L0_gnn_mlg_0, L0_gnn_mlb_0, L0_gnn_mw2_0, L0_gnn_mb2_0, L0_gnn_t1, L0_gnn_mw1_1, L0_gnn_mb1_1, L0_gnn_mlg_1, L0_gnn_mlb_1, L0_gnn_mw2_1, L0_gnn_mb2_1, L0_gnn_t2, L0_gnn_mw1_2, L0_gnn_mb1_2, L0_gnn_mlg_2, L0_gnn_mlb_2, L0_gnn_mw2_2, L0_gnn_mb2_2, L0_gnn_lng_1, L0_gnn_lnb_1, L0_gnn_lng_2, L0_gnn_lnb_2, L0_gnn_cw, L0_gnn_cb, L0_mix_Wq, L0_mix_bq, L0_mix_Wk, L0_mix_bk, L0_mix_Wv, L0_mix_bv, L0_mix_Wp, L0_mix_bp, L0_mix_gamma_q, L0_mix_beta_q, L0_mix_gamma_k, L0_mix_beta_k, L0_mix_qG1, L0_mix_qG2, L0_mix_kG1, L0_mix_kG2, L0_ffn_router_w, L0_ffn_bias, L0_ffn_shared_w_gate, L0_ffn_shared_w_up, L0_ffn_shared_w_down, L0_ffn_w_gate, L0_ffn_w_up, L0_ffn_w_down):
    import jax
    import jax.numpy as jnp

    def _L0_gnn_ref(x, edge_index, t0, mw1_0, mb1_0, mlg_0, mlb_0, mw2_0, mb2_0, t1, mw1_1, mb1_1, mlg_1, mlb_1, mw2_1, mb2_1, t2, mw1_2, mb1_2, mlg_2, mlb_2, mw2_2, mb2_2, lng_1, lnb_1, lng_2, lnb_2, cw, cb):
        import jax, jax.numpy as jnp
        import numpy as np
        N, E, H = (625, 5000, 512)
        EPS = 1e-07

        def _ln(x, g, b, eps=1e-05):
            mu = jnp.mean(x, axis=-1, keepdims=True)
            var = jnp.mean((x - mu) ** 2, axis=-1, keepdims=True)
            return (x - mu) * jax.lax.rsqrt(var + eps) * g + b

        def _genconv(x, src, dst, t, w1, b1, lg, lb, w2, b2):
            m = jax.nn.relu(x[src]) + EPS
            z = m * t
            zmax = jax.lax.stop_gradient(jax.ops.segment_max(z, dst, num_segments=N))
            zmax = jnp.where(jnp.isfinite(zmax), zmax, 0.0)
            e = jnp.exp(z - zmax[dst])
            denom = jax.ops.segment_sum(e, dst, num_segments=N)
            alpha = e / (denom[dst] + 1e-16)
            agg = jax.ops.segment_sum(alpha * m, dst, num_segments=N)
            h = agg + x
            h = jax.nn.relu(_ln(h @ w1 + b1, lg, lb))
            return h @ w2 + b2

        def _forward(x, edge_index, p):
            src, dst = (edge_index[0], edge_index[1])
            x1 = _genconv(x, src, dst, *p['c0'])
            x2 = x1 + jax.nn.relu(_ln(_genconv(x1, src, dst, *p['c1']), p['lng_1'], p['lnb_1']))
            x3 = x2 + jax.nn.relu(_ln(_genconv(x2, src, dst, *p['c2']), p['lng_2'], p['lnb_2']))
            return jnp.concatenate([x1, x2, x3], axis=1) @ p['cw'] + p['cb']
        p = {'c0': (t0, mw1_0, mb1_0, mlg_0, mlb_0, mw2_0, mb2_0), 'c1': (t1, mw1_1, mb1_1, mlg_1, mlb_1, mw2_1, mb2_1), 'c2': (t2, mw1_2, mb1_2, mlg_2, mlb_2, mw2_2, mb2_2), 'lng_1': lng_1, 'lnb_1': lnb_1, 'lng_2': lng_2, 'lnb_2': lnb_2, 'cw': cw, 'cb': cb}
        return _forward(x, edge_index, p)

    def _L0_mix_ref(x, Wq, bq, Wk, bk, Wv, bv, Wp, bp, gamma_q, beta_q, gamma_k, beta_k, qG1, qG2, kG1, kG2):
        import jax, jax.numpy as jnp
        import numpy as np
        B, S, D, H, R, P = (4, 256, 512, 8, 64, 4)
        HD = D // H
        EPS = 1e-06

        def _sketch_p4(z, G1, G2):
            inv_sqrt_r = 1.0 / np.sqrt(R).astype(np.float32)
            half = inv_sqrt_r * (z @ G1 * (z @ G2))
            return half * half
        b, s, d = x.shape
        split = lambda t: t.reshape(b, s, H, HD).transpose(0, 2, 1, 3)
        q = split(x @ Wq + bq)
        k = split(x @ Wk + bk)
        v = split(x @ Wv + bv)
        q = gamma_q * q + beta_q
        k = gamma_k * k + beta_k
        phi_q = _sketch_p4(q, qG1, qG2)
        phi_k = _sketch_p4(k, kG1, kG2)
        kv = jnp.einsum('bhsr,bhsd->bhrd', phi_k, v)
        ksum = phi_k.sum(axis=2)
        num = jnp.einsum('bhqr,bhrd->bhqd', phi_q, kv)
        den = jnp.einsum('bhqr,bhr->bhq', phi_q, ksum) + EPS
        out = num / den[..., None]
        out = out.transpose(0, 2, 1, 3).reshape(b, s, d)
        return out @ Wp + bp

    def _L0_ffn_ref(x, router_w, bias, shared_w_gate, shared_w_up, shared_w_down, w_gate, w_up, w_down):
        import jax, jax.numpy as jnp
        import numpy as np
        TOP_K = 6
        CAP_FACTOR = 2.0
        B, S, D = x.shape
        E = router_w.shape[0]
        K = TOP_K
        N = B * S
        C = max(1, int(N * K * CAP_FACTOR / E))
        router_logits = jnp.einsum('bsd,ed->bse', x, router_w) + bias
        hg = jnp.einsum('bsd,efd->bsef', x, shared_w_gate)
        hu = jnp.einsum('bsd,efd->bsef', x, shared_w_up)
        shared_out = jnp.einsum('bsef,edf->bsd', jax.nn.silu(hg) * hu, shared_w_down)
        shared_out = shared_out / shared_w_gate.shape[0]
        router_probs = jax.nn.softmax(router_logits, axis=-1)
        topk_p, topk_i = jax.lax.top_k(router_probs, K)
        topk_p = topk_p / (jnp.sum(topk_p, axis=-1, keepdims=True) + 1e-09)
        x_flat = x.reshape(N, D)
        flat_e = topk_i.reshape(-1)
        flat_g = topk_p.reshape(-1)
        token_ids = jnp.repeat(jnp.arange(N), K)
        order = jnp.argsort(flat_e)
        se = flat_e[order]
        st = token_ids[order]
        sg = flat_g[order]
        M = se.shape[0]
        pos = jnp.arange(M)
        is_first = jnp.concatenate([jnp.ones((1,), bool), se[1:] != se[:-1]])
        group_starts = jax.lax.cummax(pos * is_first.astype(pos.dtype))
        slot = pos - group_starts
        valid = slot < C
        safe_slot = jnp.where(valid, slot, C)
        expert_in = jnp.zeros((E, C + 1, D), x.dtype).at[se, safe_slot].set(x_flat[st])
        expert_gate = jnp.zeros((E, C + 1), x.dtype).at[se, safe_slot].set(sg)
        expert_tok = jnp.full((E, C + 1), N, jnp.int32).at[se, safe_slot].set(st.astype(jnp.int32))
        expert_mask = jnp.zeros((E, C + 1), bool).at[se, safe_slot].set(valid)
        expert_in = expert_in[:, :C]
        expert_gate = expert_gate[:, :C]
        expert_tok = expert_tok[:, :C]
        expert_mask = expert_mask[:, :C]
        hg = jnp.einsum('ecd,efd->ecf', expert_in, w_gate)
        hu = jnp.einsum('ecd,efd->ecf', expert_in, w_up)
        expert_out = jnp.einsum('ecf,edf->ecd', jax.nn.silu(hg) * hu, w_down)
        fm = expert_mask.reshape(-1)
        dst = jnp.where(fm, expert_tok.reshape(-1), N)
        fg = jnp.where(fm, expert_gate.reshape(-1), jnp.zeros((), x.dtype))
        sparse = jax.ops.segment_sum(fg[:, None] * expert_out.reshape(-1, D), dst, num_segments=N + 1)[:N]
        return shared_out + sparse.reshape(B, S, D)
    edge_index = jnp.stack([src, dst])
    xn = _layernorm(x, axis=-1)
    x = x + _L0_gnn_ref(xn, edge_index, L0_gnn_t0, L0_gnn_mw1_0, L0_gnn_mb1_0, L0_gnn_mlg_0, L0_gnn_mlb_0, L0_gnn_mw2_0, L0_gnn_mb2_0, L0_gnn_t1, L0_gnn_mw1_1, L0_gnn_mb1_1, L0_gnn_mlg_1, L0_gnn_mlb_1, L0_gnn_mw2_1, L0_gnn_mb2_1, L0_gnn_t2, L0_gnn_mw1_2, L0_gnn_mb1_2, L0_gnn_mlg_2, L0_gnn_mlb_2, L0_gnn_mw2_2, L0_gnn_mb2_2, L0_gnn_lng_1, L0_gnn_lnb_1, L0_gnn_lng_2, L0_gnn_lnb_2, L0_gnn_cw, L0_gnn_cb) + _L0_mix_ref(xn[None], L0_mix_Wq, L0_mix_bq, L0_mix_Wk, L0_mix_bk, L0_mix_Wv, L0_mix_bv, L0_mix_Wp, L0_mix_bp, L0_mix_gamma_q, L0_mix_beta_q, L0_mix_gamma_k, L0_mix_beta_k, L0_mix_qG1, L0_mix_qG2, L0_mix_kG1, L0_mix_kG2)[0]
    x = x + _L0_ffn_ref(_layernorm(x, axis=-1)[None], L0_ffn_router_w, L0_ffn_bias, L0_ffn_shared_w_gate, L0_ffn_shared_w_up, L0_ffn_shared_w_down, L0_ffn_w_gate, L0_ffn_w_up, L0_ffn_w_down)[0]
    return x

_drawn_inputs = setup_inputs


def setup_inputs(seed=0):
    import zlib

    import numpy as np

    out = dict(_drawn_inputs(seed))
    spreads = {'L0_gnn_mb1_0': (0.0, 0.1),
     'L0_gnn_mlg_0': (1.0, 0.2),
     'L0_gnn_mlb_0': (0.0, 0.1),
     'L0_gnn_mb2_0': (0.0, 0.1),
     'L0_gnn_mb1_1': (0.0, 0.427),
     'L0_gnn_mlg_1': (1.0, 0.2),
     'L0_gnn_mlb_1': (0.0, 0.1),
     'L0_gnn_mb2_1': (0.0, 0.1),
     'L0_gnn_mb1_2': (0.0, 0.8),
     'L0_gnn_mlg_2': (1.0, 0.2),
     'L0_gnn_mlb_2': (0.0, 0.313),
     'L0_gnn_mb2_2': (0.0, 0.363),
     'L0_gnn_lng_1': (1.0, 0.2),
     'L0_gnn_lnb_1': (0.0, 0.1),
     'L0_gnn_lng_2': (1.0, 0.2),
     'L0_gnn_lnb_2': (0.0, 0.286),
     'L0_gnn_cb': (0.0, 0.1),
     'L0_mix_bq': (0.0, 0.8),
     'L0_mix_bk': (0.0, 0.8),
     'L0_mix_bv': (0.0, 0.1),
     'L0_mix_bp': (0.0, 0.1),
     'L0_ffn_bias': (0.0, 0.8)}
    factors = {'L0_mix_Wq': 4.815,
     'L0_mix_Wk': 4.261,
     'L0_mix_Wv': 3.032,
     'L0_mix_qG1': 5.637,
     'L0_mix_qG2': 5.565,
     'L0_mix_kG1': 5.139,
     'L0_mix_kG2': 5.135,
     'L0_ffn_router_w': 8.0,
     'L0_ffn_shared_w_gate': 7.401,
     'L0_ffn_shared_w_up': 7.447,
     'L0_ffn_shared_w_down': 7.239,
     'L0_ffn_w_gate': 8.0,
     'L0_ffn_w_up': 8.0,
     'L0_ffn_w_down': 8.0}
    for name, (base, spread) in spreads.items():
        noise = np.random.default_rng([zlib.crc32(name.encode()), seed]).standard_normal(out[name].shape)
        drawn = base * np.exp(spread * noise) if base else spread * noise
        out[name] = jnp.asarray(drawn.astype(out[name].dtype))
    for name, factor in factors.items():
        out[name] = (out[name] * factor).astype(out[name].dtype)
    return out
```

```python
from contextlib import ExitStack

import concourse.bass as bass
from concourse import mybir

F32 = mybir.dt.float32
F32R = mybir.dt.float32r
BF16 = mybir.dt.bfloat16
F16 = mybir.dt.float16
I32 = mybir.dt.int32
ACT = mybir.ActivationFunctionType
ALU = mybir.AluOpType
AX = mybir.AxisListType
RMAX = bass.bass_isa.ReduceOp.max

N = 625
T = 125
NT = N // T
D = 512
H = 1024
P = 128
KD = D // P
KH = H // P
TP = N + 1
HALVES = [(0, 314), (314, 312)]
NL = 3
EDGES = 20625
CH = EDGES // T
G = 3
NG = CH // G
E = 64
F = 256
TOPK = 6
CAP = int(N * TOPK * 2.0 / E)
WE = KD * 2 * F + (F // P) * D
FAR = 200.0
SKIP = 100000.0
UNROLL = 4
PKU = 4 * NT
NSH = 2 * NT
NW = 63

COL_LG, COL_LB, COL_BQ, COL_BK, COL_S = 0, 24, 48, 52, 56


def gps_kernel(nc, x, src, dst, cols, rows, w1, w2, cw, wmix, gmix, router, rbias, shared, experts, out):
    xn2 = nc.dram_tensor("xn2_scratch", (N, D), F32, kind="Internal").ap()
    yrow = nc.dram_tensor("yrow_scratch", (N * TOPK, D), F32, kind="Internal").ap()

    with ExitStack() as ctx:
        base = [16512]

        def sb(name, shape, dt, at=None):
            size = {F32: 4, F32R: 4, I32: 4, BF16: 2, F16: 2}[dt]
            for s in shape[1:]:
                size *= s
            if at is None:
                at = base[0]
                base[0] += -(-size // 32) * 32
                assert base[0] <= 229344, (name, base[0])
            return nc.alloc_sbuf_tensor_at(name, shape, dt, offset=at)

        sems = {}

        def S(name):
            if name not in sems:
                sems[name] = ctx.enter_context(nc.semaphore(name))
            return sems[name]

        RG_WORDS = 5008 + 8192 + 4096 + 10240 + 6250
        rg_at = base[0]
        RG = sb("split_operands", [P, RG_WORDS], F32R)
        o_xt, o_w1, o_cw, o_e, o_at = 0, 5008, 13200, 17296, 27536

        def rg(o, *dims, p=P):
            n = 1
            for q in dims:
                n *= q
            v = RG[0:p, o:o + n]
            if len(dims) == 2:
                v = v.rearrange("p (a b) -> p a b", a=dims[0])
            if len(dims) == 3:
                v = v.rearrange("p (a b c) -> p a b c", a=dims[0], b=dims[1])
            return v

        def pair(o, *dims, p=P):
            n = 1
            for q in dims:
                n *= q
            return rg(o, *dims, p=p), rg(o + n, *dims, p=p)

        XT = pair(o_xt, KD, TP)
        HT = [pair(o_xt + 1000 * i, 4 * T) for i in range(2)]
        RT = pair(o_xt + 2000, 8 * T)
        XI = pair(o_xt + 4000, 4 * T)
        W1 = pair(o_w1, KD, H)
        CW = pair(o_cw, KD, D)
        W2 = pair(o_e, KH, D)
        EX = pair(o_e, NT, D, p=T)
        EM = pair(o_e + 5120, NT, D, p=T)
        AT_hi = rg(o_at, NT, N, p=T)
        AT_lo = rg(o_at + 3125, NT, N, p=T)
        WMA, WMB = pair(o_cw, KD, D), pair(o_at, KD, D)
        VV = pair(o_e, NT, D, p=T)
        KT = pair(o_e + 5120, KD, TP)
        QT = KT
        PK = pair(o_w1, NT, D, p=T)
        PQ = pair(o_e, KD, TP)
        OT = pair(o_w1, KD, TP)
        KV = pair(o_w1 + 5120, KD, 256)
        GM = pair(o_w1 + 7168, 4, P)
        RW = pair(o_at + 0, KD, E)
        SG = [pair(o_w1 + 6144 * s, KD, 2 * F) for s in range(2)]
        SD = [pair(o_w1 + 6144 * s + 4096, 2, D) for s in range(2)]
        ST = pair(o_at + 3125, 2 * T)
        RING = [sb(f"expert_weights{r}", [P, WE], F32, at=rg_at + 4 * (17296 + r * WE)) for r in range(UNROLL)]

        XO = sb("x_out", [T, NT, D], F32)
        XC = sb("x_cur", [T, NT, D], F32)
        fg_at = base[0]
        FG = sb("work", [P, 13312], F32)

        def fg(o, *dims, p=P):
            n = 1
            for q in dims:
                n *= q
            v = FG[0:p, o:o + n]
            if len(dims) == 2:
                v = v.rearrange("p (a b) -> p a b", a=dims[0])
            if len(dims) == 3:
                v = v.rearrange("p (a b c) -> p a b c", a=dims[0], b=dims[1])
            return v

        HN = fg(0, NT, D, p=T)
        STG = [fg(2560 + 2048 * i, 2048) for i in range(2)]
        BC1 = fg(6656, H, p=T)
        BC2, BCG, BCB = [fg(7680 + 512 * i, D, p=T) for i in range(3)]
        YY = [fg(9216 + 1024 * i, H, p=T) for i in range(2)]
        RR = fg(11264, 8 * T)
        EE = [fg(11264 + 512 * i, D, p=T) for i in range(2)]
        EP = fg(12288, D, p=T)
        LN = fg(12288, D, p=T)
        LN2 = fg(12800, D, p=T)
        MT = [fg(9216 + 1024 * i, 512) for i in range(2)]
        MT2 = [fg(9728 + 1024 * i, 512) for i in range(2)]
        MT3 = [fg(11264 + 512 * i, 512) for i in range(2)]
        one_hot_src = FG[0:T, 2560:2560 + G * 313].bitcast(BF16).rearrange("p (g n) -> p g n", g=G)
        one_hot_dst = FG[0:T, 3520:3520 + G * 63].bitcast(BF16).rearrange("p (g n) -> p g n", g=G)
        iota_h = FG[0:T, 3720:3720 + 313].bitcast(F16)
        member = FG[0:T, 4040:4040 + 413].bitcast(BF16)
        srcf = fg(4460, 2 * CH, p=T)
        dstrel = fg(4800, NT, 2 * CH, p=T)
        srci = fg(9216, CH, p=T).bitcast(I32)
        dsti = fg(9400, CH, p=T).bitcast(I32)
        adj = fg(10240, 2, N, p=T)
        ge = fg(9600, CH, p=T)
        rge = fg(11600, 1000, p=1)
        cnt, los, his = [rge[:, i * 275:(i + 1) * 275].rearrange("p (a b) -> p a b", a=NT) for i in range(3)]
        gidx = rge[:, 825:935].rearrange("p (a b) -> p a b", a=2)
        gidx_i = rge[:, 940:995].bitcast(I32)
        zero_b = FG[0:T, 12700:12956].bitcast(BF16)
        iota_i = fg(6656, N + 1, p=T).bitcast(I32)
        LOG, PRB, MSK, KRK, POS, GAT = [fg(320 * i, NT, E, p=T) for i in range(6)]
        SELT = [FG[0:T, 2560 + 320 * i:2560 + 320 * i + 293].bitcast(BF16)[:, 0:NT * CAP].rearrange("p (t s) -> p t s", t=NT) for i in range(4)]
        MTAB = FG[0:T, 3840:3840 + NT * E * 4].bitcast(BF16).rearrange("p (t e c) -> p t e c", t=NT, e=E)
        MSKB = FG[0:T, 5120:5120 + 160].bitcast(BF16).rearrange("p (t e) -> p t e", t=NT)
        POSB = FG[0:T, 5280:5280 + 160].bitcast(BF16).rearrange("p (t e) -> p t e", t=NT)
        TAB = fg(5440, E, 7, p=CAP)
        GR = fg(6656, 3, NT * E, p=T)
        RBC = fg(7640, E, p=T)
        SIL = [fg(7720 + 256 * i, F, p=P) for i in range(2)]
        HG = [fg(8232 + 256 * i, F, p=P) for i in range(2)]
        HTF = [fg(8744 + 256 * i, 2 * CAP) for i in range(2)]
        XE = [fg(9256 + 480 * i, KD * CAP) for i in range(2)]
        XG = [fg(10216 + 512 * i, D, p=CAP) for i in range(4)]
        OS = [fg(0 + 512 * i, D, p=CAP) for i in range(4)]
        YL = [fg(2560 + 3072 * i, TOPK, D, p=T) for i in range(2)]
        ZB = fg(10216, D)

        pnum_i = fg(12300, 1, p=T).bitcast(I32)
        pnum = fg(12302, 1, p=T)
        snum_i = fg(12310, CAP + 1, p=T).bitcast(I32)
        ysum = fg(9216, D, p=T)
        ones_f = fg(12288, P, p=T)

        ident = sb("ident", [P, P], F32)
        colp = sb("colp", [P, NW], F32)
        ones_r = sb("ones_r", [T, P], F32R)
        gb = sb("gb", [P, 8], F32)
        mhalf = sb("mhalf", [T, NT], F32)
        stats = sb("stats", [T, NT, 2, 6], F32)
        mv = sb("mv", [T, NT, 2], F32)
        rstd = sb("rstd", [T, NT], F32)
        st_m = sb("st_m", [T, 2, 6], F32)
        mv_m = sb("mv_m", [T, 4], F32)
        st_o = sb("st_o", [T, 1, 6], F32)
        mv_o = sb("mv_o", [T, 4], F32)
        zmx = sb("zmx", [T, NT + 3], F32)
        lohi = sb("lohi", [1, 2, NT], F32)
        lohi_i = sb("lohi_i", [1, 2, NT], I32)
        tri = sb("tri", [T, T], BF16)
        ones_b = sb("ones_b", [T, P], BF16)
        iota_s = sb("iota_s", [T, CAP + 1], BF16)
        gat_s = sb("gat_s", [CAP, E], F32)
        tok_i = sb("tok_i", [CAP, E], I32)
        row_i = sb("row_i", [CAP, E], I32)
        tok_c = sb("tok_c", [CAP, UNROLL], I32)
        row_c = sb("row_c", [CAP, UNROLL], I32)
        r8 = sb("r8", [T, NT, 8], F32)
        rsm = sb("rsm", [T, 4, NT], F32)
        tokf = fg(12500, 2, E, p=CAP)

        ps = ctx.enter_context(nc.psum_tensor("ps", [P, 8, 512], F32))

        pe, dve, act, pool, sp = nc.tensor, nc.vector, nc.scalar, nc.gpsimd, nc.sync

        def f(ap):
            return ap.bitcast(F32)

        def mm3(o, a, b, start, stop):
            pe.matmul(o, a[1], b[0], start=start, stop=False)
            pe.matmul(o, a[0], b[1], start=False, stop=False)
            return pe.matmul(o, a[0], b[0], start=False, stop=stop)

        def sub(p, *ix):
            return (p[0][ix], p[1][ix])

        kv_bank = ps[:, 0:2, :].rearrange("p b (c n) -> p (b c) n", c=2)

        def kv_block(v, h):
            return v[64 * h:64 * h + 64].rearrange("p c (a n) -> p c a n", a=2)[:, :, :, 64 * h:64 * h + 64]

        A_ = slice(None)

        def cut(o, n):
            return slice(o, o + n)

        vstep = [0]

        def v1(ins):
            vstep[0] += 1
            ins.then_inc(S("vector_step"), 1)
            dve.wait_ge(S("vector_step"), vstep[0])

        astep = [0]

        def a1(ins):
            astep[0] += 1
            ins.then_inc(S("scalar_step"), 1)
            act.wait_ge(S("scalar_step"), astep[0])

        gstep = [0]

        def g1(ins):
            gstep[0] += 1
            ins.then_inc(S("pool_step"), 1)
            pool.wait_ge(S("pool_step"), gstep[0])

        w1v = [w1[L].rearrange("(k p) n -> p k n", p=P) for L in range(NL)]
        w2v = [w2[L].rearrange("(k p) n -> p k n", p=P) for L in range(NL)]
        cwv = [cw[L * D:(L + 1) * D, :].rearrange("(k p) n -> p k n", p=P) for L in range(NL)]
        wmv = [wmix[i].rearrange("(k p) n -> p k n", p=P) for i in range(4)]
        plan = []

        def piece(name, source, parts, free=None):
            plan.append((name, source, parts, free))

        piece("wv", wmv[2], WMA)
        piece("wk", wmv[1], WMB)
        piece("g", None, GM)
        piece("wq", wmv[0], WMA, ("v_ps", NT))
        piece("wp", wmv[3], WMB, ("kt_ps", 8))
        for L in range(NL):
            gone = ("mix_out_ps", NT) if L == 0 else ("w1_ps", NT * L)
            for k in range(2):
                piece(f"w1_{L}{k}", w1v[L][:, 2 * k:2 * k + 2, :], sub(W1, A_, cut(2 * k, 2), A_), gone)
            piece(f"cw_{L}", cwv[L], CW, ("mix_out_ps", NT) if L == 0 else ("cw_ps", NT * L))
            for k in range(2):
                piece(f"w2_{L}{k}", w2v[L][:, 4 * k:4 * k + 4, :], sub(W2, A_, cut(4 * k, 4), A_), ("agg_ps", NT * (L + 1)))
        piece("rw", router.rearrange("(k p) n -> p k n", p=P), RW, ("agg_ps", NT * NL))
        for s in range(2):
            gone = ("cw_ps", NT * NL)
            piece(f"sg{s}", shared[s, :, 0:KD * 2 * F].rearrange("p (k n) -> p k n", k=KD), SG[s], gone)
            piece(f"sd{s}", shared[s, :, KD * 2 * F:WE].rearrange("p (k n) -> p k n", k=2), SD[s], gone)
        order = {n: i for i, (n, _, _, _) in enumerate(plan)}

        def staged(i):
            parts = plan[i][2][0]
            n = 1
            for q in parts.shape[1:]:
                n *= q
            v = STG[i % 2][:, 0:n]
            return v.rearrange("p (k n) -> p k n", k=parts.shape[1])

        def split_hi(name):
            i = order[name]
            act.wait_ge(S(f"stage_in{i % 2}"), 16 * (i // 2 + 1) + (16 if i >= order["g"] and i % 2 == order["g"] % 2 else 0))
            free = plan[i][3]
            if free:
                act.wait_ge(S(free[0]), free[1])
            act.activation(plan[i][2][0], staged(i), ACT.Copy).then_inc(S("weight_hi"), 1)

        def split_lo(name):
            i = order[name]
            dve.wait_ge(S("weight_hi"), i + 1)
            dve.tensor_tensor(plan[i][2][1], staged(i), f(plan[i][2][0]), ALU.subtract).then_inc(S("weight_lo"), 1)

        def weights(name):
            pe.wait_ge(S("weight_lo"), order[name] + 1)


        block = ctx.enter_context(nc.Block())

        @block.sync
        def _(eng):
            sp.dma_start(XO[:], x.rearrange("(t p) f -> p t f", p=T)).then_inc(S("x_in"), 16)
            sp.dma_start(colp[:], cols).then_inc(S("cols_in"), 16)
            sp.dma_start(BC1[:, 0:D], rows[0:D].partition_broadcast(T)).then_inc(S("mixrow_in"), 16)
            sp.dma_start(BC1[:, D:H], rows[D:2 * D].partition_broadcast(T)).then_inc(S("mixrow_in"), 16)
            sp.dma_start(BC2, rows[2 * D:3 * D].partition_broadcast(T)).then_inc(S("mixrow_in"), 16)

            def load(name):
                i = order[name]
                if i >= 2:
                    sp.wait_ge(S("weight_lo"), i - 1)
                if name == "g":
                    sp.wait_ge(S("stage_zero"), 1)
                    gv = staged(i)
                    sp.dma_start(gv[0:64, :, 0:64], gmix.rearrange("g p n -> p g n")).then_inc(S(f"stage_in{i % 2}"), 16)
                    sp.dma_start(gv[64:128, :, 64:128], gmix.rearrange("g p n -> p g n")).then_inc(S(f"stage_in{i % 2}"), 16)
                else:
                    sp.dma_start(staged(i), plan[i][1]).then_inc(S(f"stage_in{i % 2}"), 16)

            for n in ("wv", "wk", "g", "wq", "wp"):
                load(n)
            sp.wait_ge(S("mix_out_add"), NT)
            sp.dma_start(srci, src).then_inc(S("edges_in"), 16)
            sp.dma_start(dsti, dst).then_inc(S("edges_in"), 16)
            sp.wait_ge(S("adj_lo"), NT)
            r = 3 * D
            for L in range(NL):
                if L:
                    sp.wait_ge(S("x_next"), NT * L)
                sp.dma_start(BC1, rows[r:r + H].partition_broadcast(T)).then_inc(S("rows_in"), 16)
                sp.dma_start(BC2, rows[r + H:r + H + D].partition_broadcast(T)).then_inc(S("rows_in"), 16)
                r += H + D
                if L:
                    sp.dma_start(BCG, rows[r:r + D].partition_broadcast(T)).then_inc(S("rows_in"), 16)
                    sp.dma_start(BCB, rows[r + D:r + 2 * D].partition_broadcast(T)).then_inc(S("rows_in"), 16)
                    r += 2 * D
                for n in (f"w1_{L}0", f"w1_{L}1", f"cw_{L}", f"w2_{L}0", f"w2_{L}1"):
                    load(n)
            sp.wait_ge(S("x_next"), NT * NL)
            sp.dma_start(RBC, rbias.partition_broadcast(T)).then_inc(S("rbias_in"), 16)
            sp.wait_ge(S("zeros_made"), 1)
            for q in range(NT):
                sp.dma_start(yrow[750 * q:750 * (q + 1), :].rearrange("(p a) n -> p a n", p=T),
                             ZB[0:T, :].unsqueeze(1).to_broadcast([T, TOPK, D])).then_inc(S("y_zero"), 16)
            for n in ("rw", "sg0", "sd0", "sg1", "sd1"):
                load(n)
            sp.wait_ge(S("fin_norm"), NT)
            sp.dma_start(xn2.rearrange("(t p) f -> p t f", p=T), XC[:]).then_inc(S("xn2_out"), 16)
            sp.wait_ge(S("w2_ps"), NT * NL)

            def load_expert(e, r):
                sp.dma_start(RING[r][:], experts[e].rearrange("a p n -> (a p) n")).then_inc(S(f"ring_in{r}"), 16)

            for r in range(UNROLL):
                if r == UNROLL - 1:
                    sp.wait_ge(S("router_ps"), NT)
                load_expert(cut(r, 1), r)
            with sp.Fori(1, E // UNROLL) as i:
                for r in range(UNROLL):
                    sp.wait_ge(S("o_ps"), UNROLL * i + r - 3)
                    load_expert(bass.ds(UNROLL * i + r, 1), r)
            for r in range(UNROLL):
                sp.wait_ge(S(f"y_out{r}"), 16 * (E // UNROLL))
            for t in range(NT):
                if t >= 2:
                    sp.wait_ge(S("y_sum"), t - 1)
                sp.dma_start(YL[t % 2], yrow[750 * t:750 * (t + 1), :].rearrange("(p a) n -> p a n", p=T)).then_inc(S(f"y_in{t % 2}"), 16)
                if t >= 1:
                    sp.wait_ge(S("y_sum"), t)
                    sp.dma_start(out[T * (t - 1):T * t, :], XO[:, t - 1, :]).then_inc(S("out_done"), 16)
            sp.wait_ge(S("y_sum"), NT)
            sp.dma_start(out[T * (NT - 1):, :], XO[:, NT - 1, :]).then_inc(S("out_done"), 16)
            sp.wait_ge(S("out_done"), 16 * NT)

        @block.gpsimd
        def _(eng):
            g1(pool.memset(ident[:], 0.0))
            pool.affine_select(out=ident[:], in_=ident[:], compare_op=ALU.not_equal, fill=1.0, base=0,
                               pattern=[[-1, P]], channel_multiplier=1).then_inc(S("ident"), 1)
            g1(pool.memset(mhalf[:], -0.5))
            pool.memset(f(XT[0][:, :, N:TP]), 0.0)
            pool.memset(f(XT[1][:, :, N:TP]), 0.0)
            pool.memset(f(KV[0]), 0.0)
            pool.memset(f(KV[1]), 0.0).then_inc(S("pads_zero"), 1)
            g1(pool.memset(tri[:], 1.0))
            pool.affine_select(out=tri[:], in_=tri[:], compare_op=ALU.is_gt, fill=0.0, base=0,
                               pattern=[[1, T]], channel_multiplier=-1)
            pool.memset(ones_b[:], 1.0).then_inc(S("consts"), 1)

            def rsqrt(o, i, n, wait, value, done):
                pool.wait_ge(S(wait), value)
                pool.tensor_tensor(o, i, mhalf[:, 0:n], ALU.pow).then_inc(S(done), 1)

            rsqrt(rstd[:], mv[:, :, 1], NT, "in_var", 1, "in_rstd")
            pool.wait_ge(S("weight_lo"), 1)
            pool.memset(STG[order["g"] % 2][:, 0:4 * P], 0.0).then_inc(S("stage_zero"), 1)
            pool.wait_ge(S("in_norm"), NT)
            pool.wait_ge(S("mixrow_in"), 48)
            for t in range(NT):
                g1(pool.tensor_tensor(XO[:, t, :], XO[:, t, :], BC1[:, D:H], ALU.add))
                pool.tensor_tensor(XO[:, t, :], XO[:, t, :], BC2, ALU.add).then_inc(S("x_rows"), 1)
            for t in range(NT):
                pool.wait_ge(S("v_hi"), t + 1)
                pool.tensor_tensor(VV[1][:, t, :], MT[t % 2][0:T, :], f(VV[0][:, t, :]), ALU.subtract).then_inc(S("v_lo"), 1)
            pool.wait_ge(S("mix_out_add"), NT)
            pool.iota(iota_i, pattern=[[1, N + 1]], base=0, channel_multiplier=0).then_inc(S("iota"), 1)
            pool.iota(gidx_i, pattern=[[1, NG]], base=0, channel_multiplier=0).then_inc(S("iota"), 1)
            for L in range(NL):
                pool.wait_ge(S("zmax"), L + 1)
                pool.partition_all_reduce(zmx[:, NT + 1:NT + 2], zmx[:, NT:NT + 1], T, RMAX).then_inc(S("zmax_all"), 1)
                for t in range(NT):
                    n = NT * L + t
                    pool.wait_ge(S("exp"), n + 1)
                    if n >= 1:
                        pool.wait_ge(S("em_lo"), n)
                    g1(pool.tensor_tensor(EP, EE[t % 2], HN[:, t, :], ALU.mult))
                    pool.tensor_copy(EM[0][:, t, :], EP).then_inc(S("em_hi"), 1)
                for i in range(NT + 1):
                    n = NT * L + i
                    if i < NT:
                        rsqrt(mv_m[:, 2:3], mv_m[:, 1:2], 1, "mlp_var", n + 1, "mlp_rstd")
                    if L and i >= 1:
                        m = NT * (L - 1) + i
                        rsqrt(mv_o[:, 2:3], mv_o[:, 1:2], 1, "out_var", m, "out_rstd")
                        pool.wait_ge(S("out_norm"), m)
                        g1(pool.tensor_tensor(LN2, LN, BCG, ALU.mult))
                        pool.tensor_tensor(LN2, LN2, BCB, ALU.add).then_inc(S("out_affine"), 1)
                    if i < NT:
                        for h in range(2):
                            pool.wait_ge(S("relu"), 2 * n + h + 1)
                            if n >= 1 and h == 0:
                                pool.wait_ge(S("w2_ps"), n)
                            pool.tensor_copy(RT[0][:, cut(500 * h, 500)], RR[:, cut(500 * h, 500)]).then_inc(S("r_hi"), 1)
            pool.wait_ge(S("x_next"), NT * NL)
            pool.wait_ge(S("r_lo"), 2 * NT * NL)
            pool.memset(ZB, 0.0).then_inc(S("zeros_made"), 1)
            rsqrt(rstd[:], mv[:, :, 1], NT, "fin_var", 1, "fin_rstd")
            pool.iota(pnum_i, pattern=[[0, 1]], base=0, channel_multiplier=1)
            pool.iota(snum_i, pattern=[[1, CAP + 1]], base=0, channel_multiplier=0).then_inc(S("iota"), 1)
            pool.wait_ge(S("y_zero"), 16 * NT)
            for r in range(UNROLL):
                last = pool.memset(XG[r], 0.0)
            last.then_inc(S("xg_zero"), 1)
            pool.wait_ge(S("xg_zero"), 1)
            pool.wait_ge(S("xn2_out"), 16)
            pool.wait_ge(S("tables"), 1)

            last_token = pool.to_reg(N - 1)
            last_row = pool.to_reg(N * TOPK - 1)

            def gather(n, r):
                pool.wait_ge(S("tok_col"), n + 1)
                pool.sem_inc(S("pool_turns"), 1)
                pool.indirect_dma_start(XG[r], None, xn2, bass.IndirectOffsetOnAxis(ap=tok_c[:, cut(r, 1)], axis=0),
                                        bounds_check=last_token, oob_is_err=False).then_inc(S(f"xg_in{r}"), 16)

            def scatter(n, r):
                pool.wait_ge(S("scaled"), n + 1)
                pool.sem_inc(S("pool_turns"), 1)
                pool.indirect_dma_start(yrow, bass.IndirectOffsetOnAxis(ap=row_c[:, cut(r, 1)], axis=0), OS[r], None,
                                        bounds_check=last_row, oob_is_err=False).then_inc(S(f"y_out{r}"), 16)

            for e in range(3):
                gather(e, e)
            for e in range(UNROLL):
                gather(e + 3, (e + 3) % UNROLL)
                scatter(e, e)
            with pool.Fori(1, E // UNROLL - 1) as i:
                for r in range(UNROLL):
                    e = UNROLL * i + r
                    gather(e + 3, (r + 3) % UNROLL)
                    scatter(e, r)
            for r in range(UNROLL):
                e = E - UNROLL + r
                if r == 0:
                    gather(e + 3, 3)
                scatter(e, r)

        @block.scalar
        def _(eng):
            def tr_hi(which):
                for t in range(NT):
                    act.wait_ge(S(which + "_tr"), t + 1)
                    act.activation(XT[0][:, :, cut(t * T, T)], ps[:, t % 2, 0:KD * T].rearrange("p (k n) -> p k n", k=KD),
                                   ACT.Copy).then_inc(S(which + "_hi"), 1)

            split_hi("wv")
            tr_hi("in")
            split_hi("wk")
            for t in range(NT):
                act.wait_ge(S("v_sb"), t + 1)
                act.activation(VV[0][:, t, :], MT[t % 2][0:T, :], ACT.Copy).then_inc(S("v_hi"), 1)
                if t == 1:
                    split_hi("g")
            act.wait_ge(S("cols_in"), 16)
            act.wait_ge(S("gb"), 1)

            def proj(u):
                q = u >= 8
                c, h = divmod(u % 8, 2)
                n0, nn = HALVES[h]
                act.wait_ge(S("kt_ps"), u + 1)
                if u >= 2:
                    act.wait_ge(S("kt_lo"), u - 1)
                act.activation(MT2[u % 2][:, 0:nn], ps[:, 4 + u % 2, 0:nn], ACT.Identity,
                               bias=gb[:, cut((0 if q else 4) + c, 1)],
                               scale=colp[:, cut(COL_S + (0 if q else 2), 1)]).then_inc(S("kt_sb"), 1)
                act.wait_ge(S("kt_sb"), u + 1)
                if u == 8:
                    act.wait_ge(S("pk_ps"), 4 * NT)
                act.activation(KT[0][:, c, cut(n0, nn)], MT2[u % 2][:, 0:nn], ACT.Copy).then_inc(S("kt_hi"), 1)

            for u in range(8):
                proj(u)
                if u == 3:
                    split_hi("wq")
            act.wait_ge(S("v_lo"), NT)

            def pk_scale(u):
                act.wait_ge(S("pk_ps"), u + 1)
                if u >= 2:
                    act.wait_ge(S("pk_lo"), u - 1)
                act.activation(MT[u % 2][0:T, 0:P], ps[0:T, 6 + u % 2, 0:P], ACT.Copy, scale=0.125).then_inc(S("pk_a"), 1)

            def pk_square(u):
                t, c = divmod(u, KD)
                act.wait_ge(S("pk_ab"), u + 1)
                a1(act.activation(MT[u % 2][0:T, 2 * P:3 * P], MT[u % 2][0:T, P:2 * P], ACT.Square))
                act.activation(PK[0][:, t, cut(c * P, P)], MT[u % 2][0:T, 2 * P:3 * P], ACT.Copy).then_inc(S("pk_hi"), 1)

            pk_scale(0)
            for u in range(4 * NT):
                if u + 1 < 4 * NT:
                    pk_scale(u + 1)
                pk_square(u)
            act.wait_ge(S("kv_ps"), 1)
            for h in range(2):
                last = act.activation(kv_block(KV[0], h), kv_block(kv_bank, h), ACT.Copy)
            last.then_inc(S("kv_hi"), 1)
            split_hi("wp")
            for u in range(8, 16):
                proj(u)

            def pq_scale(u):
                nn = HALVES[u % 2][1]
                act.wait_ge(S("pk_ps"), PKU + u + 1)
                if u >= 2:
                    act.wait_ge(S("pk_lo"), PKU + u - 1)
                act.activation(MT[u % 2][:, 0:nn], ps[:, 2 + u % 2, 0:nn], ACT.Copy, scale=0.125).then_inc(S("pk_a"), 1)

            def pq_square(u):
                c, h = divmod(u, 2)
                n0, nn = HALVES[h]
                act.wait_ge(S("pk_ab"), PKU + u + 1)
                a1(act.activation(MT[u % 2][:, 0:nn], MT3[u % 2][:, 0:nn], ACT.Square))
                act.activation(PQ[0][:, c, cut(n0, nn)], MT[u % 2][:, 0:nn], ACT.Copy).then_inc(S("pk_hi"), 1)

            pq_scale(0)
            for u in range(8):
                if u + 1 < 8:
                    pq_scale(u + 1)
                pq_square(u)
            for u in range(8):
                c, h = divmod(u, 2)
                n0, nn = HALVES[h]
                act.wait_ge(S("attn"), u + 1)
                act.activation(OT[0][:, c, cut(n0, nn)], MT[u % 2][:, 0:nn], ACT.Copy).then_inc(S("attn_hi"), 1)

            for j in range(NT):
                act.wait_ge(S("adj_tr"), j + 1)
                act.activation(AT_hi[:, 0:3, cut(j * T, T)], ps[0:T, 4, 0:3 * T].rearrange("p (s n) -> p s n", s=3), ACT.Copy)
                act.activation(AT_hi[:, 3:5, cut(j * T, T)], ps[0:T, 5, 0:2 * T].rearrange("p (s n) -> p s n", s=2),
                               ACT.Copy).then_inc(S("adj_hi"), 1)

            for L in range(NL):
                act.wait_ge(S("zmax_neg"), L + 1)
                for t in range(NT):
                    n = NT * L + t
                    if n >= 2:
                        act.wait_ge(S("e_lo"), n - 1)
                        act.wait_ge(S("em_hi"), n - 1)
                    act.activation(EE[t % 2], HN[:, t, :], ACT.Exp, scale=colp[0:T, cut(COL_S + 4 + L, 1)],
                                   bias=zmx[:, NT + 2:NT + 3]).then_inc(S("exp"), 1)
                    act.wait_ge(S("exp"), n + 1)
                    act.activation(EX[0][:, t, :], EE[t % 2], ACT.Copy).then_inc(S("e_hi"), 1)
                for nme in (f"w1_{L}0", f"w1_{L}1", f"cw_{L}"):
                    split_hi(nme)

                def h_hi(i):
                    act.wait_ge(S("h_tr"), NT * L + i + 1)
                    act.activation(HT[i % 2][0], ps[:, 4, 0:4 * T], ACT.Copy).then_inc(S("ht_hi"), 1)

                h_hi(0)
                for i in range(NT + 2):
                    n = NT * L + i
                    if i + 1 < NT:
                        h_hi(i + 1)
                    if i == 0:
                        split_hi(f"w2_{L}0")
                        split_hi(f"w2_{L}1")
                    if i >= 2:
                        act.wait_ge(S("x_tr"), n - 1)
                        act.activation(XI[0], ps[:, 6, 0:4 * T], ACT.Copy).then_inc(S("xi_hi"), 1)
                    if i < NT:
                        act.wait_ge(S("mlp_nmr"), n + 1)
                        act.activation(YY[i % 2], YY[i % 2], ACT.Identity, bias=mv_m[:, 3:4], scale=mv_m[:, 2:3]).then_inc(S("y_norm"), 1)
                        act.wait_ge(S("y_tr"), n + 1)
                        if n >= 1:
                            act.wait_ge(S("r_lo"), 2 * n)
                        for k in range(KH):
                            last = act.activation(RR[:, cut(k * T, T)], ps[:, 2 + k // 4, cut((k % 4) * T, T)], ACT.Relu,
                                                  bias=colp[:, cut(COL_LB + 8 * L + k, 1)], scale=colp[:, cut(COL_LG + 8 * L + k, 1)])
                            if k % 4 == 3:
                                last.then_inc(S("relu"), 1)
            split_hi("rw")
            tr_hi("fin")
            for nme in ("sg0", "sd0", "sg1", "sd1"):
                split_hi(nme)
            for t in range(NT):
                act.wait_ge(S("log_max"), t + 1)
                act.activation(PRB[:, t, :], LOG[:, t, :], ACT.Exp, bias=rsm[:, 0, cut(t, 1)],
                               accum_out=rsm[:, 1, cut(t, 1)]).then_inc(S("log_exp"), 1)

            def shared_silu(n):
                act.wait_ge(S("gu_ps"), n + 1)
                if n >= 2:
                    act.wait_ge(S("hg"), n - 1)
                act.activation(SIL[n % 2][0:T, :], ps[0:T, 2 + n % 2, 0:F], ACT.Silu).then_inc(S("silu"), 1)

            def shared_hi(n):
                act.wait_ge(S("ht_ps"), n + 1)
                act.activation(ST[0], ps[:, 6, 0:2 * T], ACT.Copy).then_inc(S("s_t_hi"), 1)

            shared_silu(0)
            for n in range(2 * NT):
                if n + 1 < 2 * NT:
                    shared_silu(n + 1)
                shared_hi(n)

            def after(name, value):
                if not isinstance(value, int) or value > 0:
                    act.wait_ge(S(name), value)

            def xe_copy(e, r):
                act.wait_ge(S("xe_ps"), e + 1)
                after("gu_ps", NSH + e - 1)
                act.activation(XE[r % 2], ps[:, r % 2, 0:KD * CAP], ACT.Copy).then_inc(S("xe_sb"), 1)

            def silu(e, r):
                act.wait_ge(S("gu_ps"), NSH + e + 1)
                after("hg", NSH + e - 1)
                act.activation(SIL[r % 2][0:CAP, :], ps[0:CAP, 2 + r % 2, 0:F], ACT.Silu).then_inc(S("silu"), 1)

            def scale(e, col, r):
                act.wait_ge(S("o_ps"), e + 1)
                act.wait_ge(S("row_col"), e + 1)
                act.activation(OS[r], ps[0:CAP, 6 + r % 2, 0:D], ACT.Copy, scale=gat_s[:, col]).then_inc(S("scaled"), 1)

            act.wait_ge(S("tables"), 1)
            xe_copy(0, 0)
            for r in range(UNROLL):
                xe_copy(r + 1, (r + 1) % UNROLL)
                silu(r, r)
                if r >= 1:
                    scale(r - 1, cut(r - 1, 1), r - 1)
            with act.Fori(1, E // UNROLL - 1) as i:
                for r in range(UNROLL):
                    e = UNROLL * i + r
                    xe_copy(e + 1, (r + 1) % UNROLL)
                    silu(e, r)
                    scale(e - 1, bass.ds(e - 1, 1), (r - 1) % UNROLL)
            for r in range(UNROLL):
                e = E - UNROLL + r
                if e + 1 < E:
                    xe_copy(e + 1, (r + 1) % UNROLL)
                silu(e, r)
                scale(e - 1, cut(e - 1, 1), (r - 1) % UNROLL)
            scale(E - 1, cut(E - 1, 1), UNROLL - 1)

        @block.vector
        def _(eng):
            def row_stats(var, rs, norm):
                for t in range(NT):
                    if var == "fin_var":
                        dve.wait_ge(S("cw_add"), NT * (NL - 1) + t + 1)
                    last = dve.bn_stats(stats[:, t, 0, :], XO[:, t, :])
                v1(last)
                for t in range(NT):
                    last = dve.bn_aggr(mv[:, t, :], stats[:, t, 0, :])
                v1(last)
                dve.tensor_scalar(mv[:, :, 1], mv[:, :, 1], 1e-5, None, ALU.add).then_inc(S(var), 1)
                dve.wait_ge(S(rs), 1)
                for t in range(NT):
                    dve.tensor_scalar(XC[:, t, :], XO[:, t, :], mv[:, t, 0:1], rstd[:, cut(t, 1)],
                                      ALU.subtract, ALU.mult).then_inc(S(norm), 1)

            def tr_lo(which):
                for t in range(NT):
                    dve.wait_ge(S(which + "_hi"), t + 1)
                    dve.tensor_tensor(XT[1][:, :, cut(t * T, T)], ps[:, t % 2, 0:KD * T].rearrange("p (k n) -> p k n", k=KD),
                                      f(XT[0][:, :, cut(t * T, T)]), ALU.subtract).then_inc(S(which + "_lo"), 1)

            def message(L, t):
                v1(dve.tensor_scalar(HN[:, t, :], XC[:, t, :], 0.0, 1e-7, ALU.max, ALU.add))
                v1(dve.tensor_scalar(LN2, HN[:, t, :], colp[0:T, cut(COL_S + 4 + L, 1)], -3.0e38, ALU.mult, ALU.max,
                                     accum_out=zmx[:, cut(t, 1)]))
                if t == NT - 1:
                    dve.tensor_reduce(zmx[:, NT:NT + 1], zmx[:, 0:NT], axis=AX.X, op=ALU.max).then_inc(S("zmax"), 1)

            dve.memset(ones_f, 1.0).then_inc(S("ones_f"), 1)
            dve.wait_ge(S("ones_f"), 1)
            dve.tensor_copy(ones_r[:], ones_f).then_inc(S("ones_r"), 1)
            dve.wait_ge(S("x_in"), 16)
            row_stats("in_var", "in_rstd", "in_norm")
            split_lo("wv")
            tr_lo("in")
            split_lo("wk")
            dve.wait_ge(S("cols_in"), 16)
            dve.tensor_scalar(gb[:, 0:4], colp[:, COL_BQ:COL_BQ + 4], colp[:, COL_S:COL_S + 1], colp[:, COL_S + 1:COL_S + 2], ALU.mult, ALU.add)
            dve.tensor_scalar(gb[:, 4:8], colp[:, COL_BK:COL_BK + 4], colp[:, COL_S + 2:COL_S + 3], colp[:, COL_S + 3:COL_S + 4],
                              ALU.mult, ALU.add).then_inc(S("gb"), 1)
            dve.wait_ge(S("mixrow_in"), 48)
            for t in range(NT):
                dve.wait_ge(S("v_ps"), t + 1)
                if t >= 2:
                    dve.wait_ge(S("v_lo"), t - 1)
                dve.tensor_tensor(MT[t % 2][0:T, :], ps[0:T, 2 + t % 2, :], BC1[:, 0:D], ALU.add).then_inc(S("v_sb"), 1)
                if t == 1:
                    split_lo("g")

            def proj_lo(u):
                c, h = divmod(u % 8, 2)
                n0, nn = HALVES[h]
                dve.wait_ge(S("kt_hi"), u + 1)
                dve.tensor_tensor(KT[1][:, c, cut(n0, nn)], MT2[u % 2][:, 0:nn], f(KT[0][:, c, cut(n0, nn)]),
                                  ALU.subtract).then_inc(S("kt_lo"), 1)

            for u in range(8):
                proj_lo(u)
                if u == 3:
                    split_lo("wq")

            def pk_mul(u):
                dve.wait_ge(S("pk_a"), u + 1)
                dve.tensor_tensor(MT[u % 2][0:T, P:2 * P], ps[0:T, 6 + u % 2, P:2 * P], MT[u % 2][0:T, 0:P], ALU.mult).then_inc(S("pk_ab"), 1)

            pk_mul(0)
            for u in range(4 * NT):
                t, c = divmod(u, KD)
                if u + 1 < 4 * NT:
                    pk_mul(u + 1)
                dve.wait_ge(S("pk_hi"), u + 1)
                dve.tensor_tensor(PK[1][:, t, cut(c * P, P)], MT[u % 2][0:T, 2 * P:3 * P], f(PK[0][:, t, cut(c * P, P)]),
                                  ALU.subtract).then_inc(S("pk_lo"), 1)
            dve.wait_ge(S("kv_hi"), 1)
            for h in range(2):
                last = dve.tensor_tensor(kv_block(KV[1], h), kv_block(kv_bank, h), f(kv_block(KV[0], h)), ALU.subtract)
            last.then_inc(S("kv_lo"), 1)
            split_lo("wp")
            for u in range(8, 16):
                proj_lo(u)

            def pq_mul(u):
                nn = HALVES[u % 2][1]
                dve.wait_ge(S("pk_a"), PKU + u + 1)
                dve.tensor_tensor(MT3[u % 2][:, 0:nn], ps[:, 6 + u % 2, 0:nn], MT[u % 2][:, 0:nn], ALU.mult).then_inc(S("pk_ab"), 1)

            pq_mul(0)
            for u in range(8):
                c, h = divmod(u, 2)
                n0, nn = HALVES[h]
                if u + 1 < 8:
                    pq_mul(u + 1)
                dve.wait_ge(S("pk_hi"), PKU + u + 1)
                dve.tensor_tensor(PQ[1][:, c, cut(n0, nn)], MT[u % 2][:, 0:nn], f(PQ[0][:, c, cut(n0, nn)]),
                                  ALU.subtract).then_inc(S("pk_lo"), 1)
            for u in range(8):
                c, h = divmod(u, 2)
                n0, nn = HALVES[h]
                dve.wait_ge(S("attn_ps"), u + 1)
                v1(dve.tensor_scalar(MT3[u % 2][:, 0:nn], ps[:, u % 2, 0:nn], 1e-6, None, ALU.add))
                v1(dve.reciprocal(MT3[u % 2][:, 0:nn], MT3[u % 2][:, 0:nn]))
                dve.tensor_tensor(MT[u % 2][:, 0:nn], ps[:, 4 + u % 2, 0:nn], MT3[u % 2][:, 0:nn], ALU.mult).then_inc(S("attn"), 1)
                dve.wait_ge(S("attn_hi"), u + 1)
                dve.tensor_tensor(OT[1][:, c, cut(n0, nn)], MT[u % 2][:, 0:nn], f(OT[0][:, c, cut(n0, nn)]),
                                  ALU.subtract).then_inc(S("attn_lo"), 1)
            for t in range(NT):
                dve.wait_ge(S("mix_out_ps"), t + 1)
                dve.wait_ge(S("x_rows"), t + 1)
                dve.tensor_tensor(XO[:, t, :], XO[:, t, :], ps[0:T, 2 + t % 2, :], ALU.add).then_inc(S("mix_out_add"), 1)

            for t in range(NT):
                message(0, t)
            dve.wait_ge(S("iota"), 2)
            dve.memset(zero_b, 0.0)
            dve.tensor_copy(iota_h, iota_i)
            v1(dve.tensor_copy(gidx[:, 0, :], gidx_i))
            v1(dve.tensor_scalar(gidx[:, 1, :], gidx[:, 0, :], 1.0, None, ALU.add))
            v1(dve.tensor_scalar(gidx[:, 0, :], gidx[:, 0, :], -100.0, None, ALU.add))
            dve.wait_ge(S("edges_in"), 32)
            dve.tensor_copy(srcf[:, 0:CH], srci)
            v1(dve.tensor_copy(dstrel[:, 0, 0:CH], dsti))
            for j in range(1, NT):
                last = dve.tensor_scalar(dstrel[:, j, 0:CH], dstrel[:, 0, 0:CH], float(-T * j), None, ALU.add)
            v1(last)
            for j in range(NT):
                v1(dve.tensor_scalar(ge, dstrel[:, j, 0:CH], 0.0, None, ALU.is_ge))
                v1(dve.scalar_tensor_tensor(out=member[:, cut(j * CH, CH)], in0=dstrel[:, j, 0:CH], scalar=float(T), in1=ge,
                                            op0=ALU.is_lt, op1=ALU.mult))
            dve.sem_inc(S("member"), 1)
            dve.wait_ge(S("member_ps"), 1)
            for j in range(NT):
                b, q = (6, j) if j < 3 else (7, j - 3)
                last = dve.tensor_reduce(cnt[:, j, :], ps[0:1, b, cut(q * CH, CH)].rearrange("p (g c) -> p g c", c=G), axis=AX.X, op=ALU.add)
            v1(last)
            for j in range(NT):
                dve.scalar_tensor_tensor(out=los[:, j, :], in0=cnt[:, j, :], scalar=0.5, in1=gidx[:, 0, :], op0=ALU.is_gt, op1=ALU.mult)
                last = dve.scalar_tensor_tensor(out=his[:, j, :], in0=cnt[:, j, :], scalar=0.5, in1=gidx[:, 1, :], op0=ALU.is_gt, op1=ALU.mult)
            v1(last)
            dve.tensor_reduce(lohi[:, 0, :], los, axis=AX.X, op=ALU.min)
            v1(dve.tensor_reduce(lohi[:, 1, :], his, axis=AX.X, op=ALU.max))
            v1(dve.tensor_scalar(lohi[:, 0, :], lohi[:, 0, :], 100.0, float(NG - 1), ALU.add, ALU.min))
            v1(dve.tensor_tensor(lohi[:, 1, :], lohi[:, 1, :], lohi[:, 0, :], ALU.subtract))
            v1(dve.tensor_scalar(lohi[:, 1, :], lohi[:, 1, :], 1.0, None, ALU.max))
            dve.tensor_copy(lohi_i[:], lohi[:]).then_inc(S("ranges"), 1)
            dve.wait_ge(S("ranges"), 1)

            def adj_out(j):
                dve.wait_ge(S("adj_ps"), j + 1)
                if j >= 2:
                    dve.wait_ge(S("adj_tr"), j - 1)
                dve.tensor_copy(adj[:, j % 2, 0:313], ps[0:T, 2 * (j % 2), 0:313])
                dve.tensor_copy(adj[:, j % 2, 313:N], ps[0:T, 2 * (j % 2) + 1, 0:312]).then_inc(S("adj_sb"), 1)
                dve.wait_ge(S("adj_hi"), j + 1)
                dve.tensor_tensor(AT_lo[:, 0:3, cut(j * T, T)], ps[0:T, 4, 0:3 * T].rearrange("p (s n) -> p s n", s=3),
                                  f(AT_hi[:, 0:3, cut(j * T, T)]), ALU.subtract)
                dve.tensor_tensor(AT_lo[:, 3:5, cut(j * T, T)], ps[0:T, 5, 0:2 * T].rearrange("p (s n) -> p s n", s=2),
                                  f(AT_hi[:, 3:5, cut(j * T, T)]), ALU.subtract).then_inc(S("adj_lo"), 1)

            for j in range(NT):
                lo = dve.value_load(lohi_i[0:1, 0, j:j + 1], min_val=0, max_val=NG - 1)
                steps = dve.value_load(lohi_i[0:1, 1, j:j + 1], min_val=1, max_val=NG)
                with dve.Fori(0, steps) as q:
                    for i in range(G):
                        dve.wait_ge(S(f"one_hot_free{j}"), q * G + i + 1)
                        dve.tensor_scalar(one_hot_src[:, i, :], iota_h, srcf[:, bass.ds((lo + q) * G + i, 1)], None, ALU.is_equal)
                        dve.tensor_scalar(one_hot_dst[:, i, :], iota_h[:, 0:T + 1], dstrel[:, j, bass.ds((lo + q) * G + i, 1)], None,
                                          ALU.is_equal).then_inc(S(f"one_hot{j}"), 1)
                if j >= 1:
                    adj_out(j - 1)
            adj_out(NT - 1)

            for L in range(NL):
                dve.wait_ge(S("zmax_all"), L + 1)
                dve.tensor_scalar(zmx[:, NT + 2:NT + 3], zmx[:, NT + 1:NT + 2], -1.0, None, ALU.mult).then_inc(S("zmax_neg"), 1)
                for t in range(NT):
                    n = NT * L + t
                    dve.wait_ge(S("e_hi"), n + 1)
                    dve.tensor_tensor(EX[1][:, t, :], EE[t % 2], f(EX[0][:, t, :]), ALU.subtract).then_inc(S("e_lo"), 1)
                    dve.wait_ge(S("em_hi"), n + 1)
                    dve.tensor_tensor(EM[1][:, t, :], EP, f(EM[0][:, t, :]), ALU.subtract).then_inc(S("em_lo"), 1)
                for d in range(NT):
                    n = NT * L + d
                    dve.wait_ge(S("agg_ps"), n + 1)
                    v1(dve.tensor_scalar(LN, ps[0:T, 2 * (d % 2), :], 1e-30, None, ALU.max))
                    v1(dve.reciprocal(LN, LN))
                    v1(dve.tensor_tensor(LN2, ps[0:T, 2 * (d % 2) + 1, :], LN, ALU.mult))
                    dve.tensor_tensor(HN[:, d, :], LN2, XC[:, d, :], ALU.add).then_inc(S("h"), 1)
                    if d < 3:
                        split_lo((f"w1_{L}0", f"w1_{L}1", f"cw_{L}")[d])

                def h_lo(i):
                    dve.wait_ge(S("ht_hi"), NT * L + i + 1)
                    dve.tensor_tensor(HT[i % 2][1], ps[:, 4, 0:4 * T], f(HT[i % 2][0]), ALU.subtract).then_inc(S("ht_lo"), 1)

                h_lo(0)
                dve.wait_ge(S("rows_in"), 32 + 64 * L)
                for i in range(NT + 2):
                    n = NT * L + i
                    if i + 1 < NT:
                        h_lo(i + 1)
                    if i < NT:
                        dve.wait_ge(S("w1_ps"), n + 1)
                        if n >= 2:
                            dve.wait_ge(S("y_tr"), n - 1)
                        v1(dve.tensor_tensor(YY[i % 2].rearrange("p (a b) -> p a b", a=2), ps[0:T, 0:2, :],
                                             BC1.rearrange("p (a b) -> p a b", a=2), ALU.add))
                        dve.sem_inc(S("y_sb"), 1)
                        dve.bn_stats(st_m[:, 0, :], YY[i % 2][:, 0:D])
                        v1(dve.bn_stats(st_m[:, 1, :], YY[i % 2][:, D:H]))
                        if n >= 1:
                            dve.wait_ge(S("y_norm"), n)
                        v1(dve.bn_aggr(mv_m[:, 0:2], st_m[:].rearrange("p a b -> p (a b)")))
                        dve.tensor_scalar(mv_m[:, 1:2], mv_m[:, 1:2], 1e-5, None, ALU.add).then_inc(S("mlp_var"), 1)
                    if i == 0:
                        split_lo(f"w2_{L}0")
                        split_lo(f"w2_{L}1")
                    if i >= 2:
                        dve.wait_ge(S("xi_hi"), n - 1)
                        dve.tensor_tensor(XI[1], ps[:, 6, 0:4 * T], f(XI[0]), ALU.subtract).then_inc(S("xi_lo"), 1)
                    if i < NT:
                        dve.wait_ge(S("mlp_rstd"), n + 1)
                        dve.scalar_tensor_tensor(out=mv_m[:, 3:4], in0=mv_m[:, 0:1], scalar=-1.0, in1=mv_m[:, 2:3],
                                                 op0=ALU.mult, op1=ALU.mult).then_inc(S("mlp_nmr"), 1)
                    if 1 <= i <= NT:
                        t = i - 1
                        dve.wait_ge(S("w2_ps"), n)
                        if L == 0:
                            v1(dve.tensor_tensor(XC[:, t, :], ps[0:T, 5, :], BC2, ALU.add))
                            dve.sem_inc(S("w2_sb"), 1)
                            dve.sem_inc(S("x_next"), 1)
                        else:
                            m = NT * (L - 1) + t + 1
                            v1(dve.tensor_tensor(LN, ps[0:T, 5, :], BC2, ALU.add))
                            dve.sem_inc(S("w2_sb"), 1)
                            v1(dve.bn_stats(st_o[:, 0, :], LN))
                            v1(dve.bn_aggr(mv_o[:, 0:2], st_o[:, 0, :]))
                            dve.tensor_scalar(mv_o[:, 1:2], mv_o[:, 1:2], 1e-5, None, ALU.add).then_inc(S("out_var"), 1)
                            dve.wait_ge(S("out_rstd"), m)
                            dve.tensor_scalar(LN, LN, mv_o[:, 0:1], mv_o[:, 2:3], ALU.subtract, ALU.mult).then_inc(S("out_norm"), 1)
                            dve.wait_ge(S("out_affine"), m)
                            v1(dve.scalar_tensor_tensor(out=XC[:, t, :], in0=LN2, scalar=0.0, in1=XC[:, t, :], op0=ALU.max, op1=ALU.add))
                            dve.sem_inc(S("x_next"), 1)
                        if L + 1 < NL:
                            message(L + 1, t)
                    if i >= 2:
                        dve.wait_ge(S("cw_ps"), n - 1)
                        dve.tensor_tensor(XO[:, i - 2, :], XO[:, i - 2, :], ps[0:T, 7, :], ALU.add).then_inc(S("cw_add"), 1)
                    if i < NT:
                        for h in range(2):
                            dve.wait_ge(S("r_hi"), 2 * n + h + 1)
                            dve.tensor_tensor(RT[1][:, cut(500 * h, 500)], RR[:, cut(500 * h, 500)], f(RT[0][:, cut(500 * h, 500)]),
                                              ALU.subtract).then_inc(S("r_lo"), 1)

            row_stats("fin_var", "fin_rstd", "fin_norm")
            split_lo("rw")
            tr_lo("fin")
            for nme in ("sg0", "sd0", "sg1", "sd1"):
                split_lo(nme)
            dve.wait_ge(S("rbias_in"), 16)
            for t in range(NT):
                dve.wait_ge(S("router_ps"), t + 1)
                v1(dve.tensor_tensor(LOG[:, t, :], ps[0:T, 2 + t % 2, 0:E], RBC, ALU.add))
                dve.sem_inc(S("log_sb"), 1)
                v1(dve.tensor_reduce(rsm[:, 0, cut(t, 1)], LOG[:, t, :], axis=AX.X, op=ALU.max))
                dve.tensor_scalar(rsm[:, 0, cut(t, 1)], rsm[:, 0, cut(t, 1)], -1.0, None, ALU.mult).then_inc(S("log_max"), 1)
            dve.wait_ge(S("log_exp"), NT)
            v1(dve.reciprocal(rsm[:, 2, :], rsm[:, 1, :]))
            for t in range(NT):
                last = dve.tensor_scalar(PRB[:, t, :], PRB[:, t, :], rsm[:, 2, cut(t, 1)], None, ALU.mult)
            v1(last)
            for t in range(NT):
                last = dve.max(r8[:, t, :], PRB[:, t, :])
            v1(last)
            v1(dve.tensor_reduce(rsm[:, 3, :], r8[:, :, 0:TOPK], axis=AX.X, op=ALU.add))
            v1(dve.tensor_scalar(rsm[:, 3, :], rsm[:, 3, :], 1e-9, None, ALU.add))
            v1(dve.reciprocal(rsm[:, 3, :], rsm[:, 3, :]))
            v1(dve.memset(r8[:, :, TOPK:8], -5.0))
            for t in range(NT):
                last = dve.match_replace(MSK[:, t, :], r8[:, t, :], PRB[:, t, :], -1.0)
            v1(last)
            v1(dve.tensor_scalar(MSK, MSK, -1.0, None, ALU.is_equal))
            dve.tensor_copy(MSKB, MSK).then_inc(S("mask"), 1)
            for t in range(NT):
                last = dve.scalar_tensor_tensor(out=GAT[:, t, :], in0=PRB[:, t, :], scalar=rsm[:, 3, cut(t, 1)], in1=MSK[:, t, :],
                                                op0=ALU.mult, op1=ALU.mult)
            v1(last)
            v1(dve.memset(GR[:, 2, 0:E], 1.0))
            for t in range(NT):
                last = dve.tensor_tensor_scan(KRK[:, t, :], GR[:, 2, 0:E], MSK[:, t, :], 0.0, ALU.mult, ALU.add)
            v1(last)
            v1(dve.tensor_tensor(KRK, KRK, MSK, ALU.subtract))
            dve.wait_ge(S("iota"), 3)
            v1(dve.tensor_copy(pnum, pnum_i))
            v1(dve.tensor_copy(iota_s[:], snum_i))
            dve.tensor_scalar(MTAB[:, :, :, 0], MSK, 0.0, pnum, ALU.mult, ALU.add)
            for t in range(NT):
                dve.memset(MTAB[:, t, :, 1], float(t))
            dve.tensor_copy(MTAB[:, :, :, 2], KRK)
            dve.memset(MTAB[:, :, :, 3], 1.0)
            v1(dve.tensor_copy(MTAB[:, :, :, 4], GAT))
            g0, gr = [GR[:, i, :].rearrange("p (t e) -> p t e", t=NT) for i in range(2)]
            v1(dve.tensor_tensor(g0, GAT, MTAB[:, :, :, 4], ALU.subtract))
            v1(dve.tensor_copy(MTAB[:, :, :, 5], g0))
            v1(dve.tensor_tensor(gr, g0, MTAB[:, :, :, 5], ALU.subtract))
            v1(dve.tensor_copy(MTAB[:, :, :, 6], gr))
            dve.wait_ge(S("pos_ps"), 1)
            v1(dve.tensor_copy(POS, ps[0:T, 4, 0:NT * E].rearrange("p (t e) -> p t e", t=NT)))
            v1(dve.scalar_tensor_tensor(out=LOG, in0=POS, scalar=float(CAP), in1=MSK, op0=ALU.is_lt, op1=ALU.mult))
            v1(dve.scalar_tensor_tensor(out=POS, in0=POS, scalar=-FAR, in1=LOG, op0=ALU.add, op1=ALU.mult))
            v1(dve.tensor_scalar(POSB, POS, FAR, None, ALU.add))

            def select(e, n, r):
                if not isinstance(n, int) or n >= UNROLL:
                    dve.wait_ge(S("sel_used"), n - 3)
                dve.tensor_tensor(SELT[r], iota_s[:, 0:CAP].unsqueeze(1).to_broadcast([T, NT, CAP]),
                                  POSB[:, :, e].to_broadcast([T, NT, CAP]), ALU.is_equal).then_inc(S("sel"), 1)

            for e in range(UNROLL):
                select(cut(e, 1), e, e)
            with dve.Fori(1, E // UNROLL) as i:
                for r in range(UNROLL):
                    select(bass.ds(UNROLL * i + r, 1), UNROLL * i + r, r)
            dve.wait_ge(S("sel_used"), E)
            v1(dve.tensor_copy(TAB, ps[0:CAP, 5, 0:7 * E].rearrange("p (e c) -> p e c", c=7)))
            v1(dve.tensor_tensor(gat_s[:], TAB[:, :, 4], TAB[:, :, 5], ALU.add))
            v1(dve.tensor_tensor(gat_s[:], gat_s[:], TAB[:, :, 6], ALU.add))
            v1(dve.scalar_tensor_tensor(out=tokf[:, 0, :], in0=TAB[:, :, 1], scalar=float(T), in1=TAB[:, :, 0], op0=ALU.mult, op1=ALU.add))
            v1(dve.scalar_tensor_tensor(out=tokf[:, 1, :], in0=tokf[:, 0, :], scalar=float(TOPK), in1=TAB[:, :, 2], op0=ALU.mult, op1=ALU.add))
            v1(dve.tensor_scalar(TAB[:, :, 3], TAB[:, :, 3], -SKIP, SKIP, ALU.mult, ALU.add))
            v1(dve.tensor_tensor(tokf[:, 0, :], tokf[:, 0, :], TAB[:, :, 3], ALU.add))
            v1(dve.tensor_tensor(tokf[:, 1, :], tokf[:, 1, :], TAB[:, :, 3], ALU.add))
            v1(dve.tensor_copy(tok_i[:], tokf[:, 0, :]))
            dve.tensor_copy(tok_c[:], tok_i[:, 0:UNROLL]).then_inc(S("tok_col"), UNROLL)
            dve.tensor_copy(row_i[:], tokf[:, 1, :]).then_inc(S("tables"), 1)

            def shared_hg(n):
                dve.wait_ge(S("silu"), n + 1)
                if n >= 2:
                    dve.wait_ge(S("ht_ps"), n - 1)
                dve.tensor_tensor(HG[n % 2][0:T, :], ps[0:T, 2 + n % 2, F:2 * F], SIL[n % 2][0:T, :], ALU.mult).then_inc(S("hg"), 1)

            shared_hg(0)
            for n in range(2 * NT):
                if n + 1 < 2 * NT:
                    shared_hg(n + 1)
                dve.wait_ge(S("s_t_hi"), n + 1)
                dve.tensor_tensor(ST[1], ps[:, 6, 0:2 * T], f(ST[0]), ALU.subtract).then_inc(S("s_t_lo"), 1)
                if n % 2 == 0 and n:
                    t = n // 2 - 1
                    dve.wait_ge(S("shared_ps"), t + 1)
                    dve.scalar_tensor_tensor(out=XO[:, t, :], in0=ps[0:T, 7, :], scalar=0.5, in1=XO[:, t, :],
                                             op0=ALU.mult, op1=ALU.add).then_inc(S("shared_add"), 1)
            dve.wait_ge(S("shared_ps"), NT)
            dve.scalar_tensor_tensor(out=XO[:, NT - 1, :], in0=ps[0:T, 7, :], scalar=0.5, in1=XO[:, NT - 1, :],
                                     op0=ALU.mult, op1=ALU.add).then_inc(S("shared_add"), 1)

            def after(name, value):
                if not isinstance(value, int) or value > 0:
                    dve.wait_ge(S(name), value)

            def gated(e, col, ahead, r, turn):
                dve.wait_ge(S("silu"), NSH + e + 1)
                if ahead is not None:
                    dve.tensor_copy(tok_c[:, cut(r, 1)], tok_i[:, ahead]).then_inc(S("tok_col"), 1)
                dve.wait_ge(S("ht_ps"), NSH + e - 1)
                dve.tensor_tensor(HG[r % 2][0:CAP, :], ps[0:CAP, 2 + r % 2, F:2 * F], SIL[r % 2][0:CAP, :], ALU.mult).then_inc(S("hg"), 1)
                after(f"y_out{r}", 16 * turn)
                dve.tensor_copy(row_c[:, cut(r, 1)], row_i[:, col]).then_inc(S("row_col"), 1)
                dve.wait_ge(S("ht_ps"), NSH + e + 1)
                after("o_ps", e - 1)
                dve.tensor_copy(HTF[r % 2], ps[:, 4 + r % 2, 0:2 * CAP]).then_inc(S("ht_sb"), 1)

            for r in range(UNROLL):
                gated(r, cut(r, 1), cut(r + UNROLL, 1), r, 0)
            with dve.Fori(1, E // UNROLL - 1) as i:
                for r in range(UNROLL):
                    e = UNROLL * i + r
                    gated(e, bass.ds(e, 1), bass.ds(e + UNROLL, 1), r, i)
            for r in range(UNROLL):
                e = E - UNROLL + r
                gated(e, cut(e, 1), None, r, E // UNROLL - 1)
            for t in range(NT):
                dve.wait_ge(S(f"y_in{t % 2}"), 16 * (t // 2 + 1))
                if t >= 1:
                    dve.wait_ge(S("y_sum"), t)
                v1(dve.tensor_reduce(ysum, YL[t % 2].rearrange("p a n -> p n a"), axis=AX.X, op=ALU.add))
                dve.tensor_tensor(XO[:, t, :], XO[:, t, :], ysum, ALU.add).then_inc(S("y_sum"), 1)

        @block.tensor
        def _(eng):
            def tr_x(norm, which):
                for t in range(NT):
                    pe.wait_ge(S(norm), t + 1)
                    if t >= 2:
                        pe.wait_ge(S(which + "_lo"), t - 1)
                    for k in range(KD):
                        last = pe.transpose(ps[:, t % 2, cut(k * T, T)], XC[:, t, cut(k * P, P)], ident[0:T, 0:T])
                    last.then_inc(S(which + "_tr"), 1)

            pe.wait_ge(S("ident"), 1)
            tr_x("in_norm", "in")
            weights("wv")
            for t in range(NT):
                pe.wait_ge(S("in_lo"), t + 1)
                if t >= 2:
                    pe.wait_ge(S("v_sb"), t - 1)
                for k in range(KD):
                    last = mm3(ps[0:T, 2 + t % 2, :], sub(XT, A_, k, cut(t * T, T)), sub(WMA, A_, k, A_), k == 0, k == KD - 1)
                last.then_inc(S("v_ps"), 1)

            def proj(u, w):
                c, h = divmod(u % 8, 2)
                n0, nn = HALVES[h]
                if u >= 2:
                    pe.wait_ge(S("kt_sb"), u - 1)
                for k in range(KD):
                    last = mm3(ps[:, 4 + u % 2, 0:nn], sub(w, A_, k, cut(c * P, P)), sub(XT, A_, k, cut(n0, nn)), k == 0, k == KD - 1)
                last.then_inc(S("kt_ps"), 1)

            weights("wk")
            pe.wait_ge(S("pads_zero"), 1)
            for u in range(8):
                proj(u, WMB)
            weights("g")
            pe.wait_ge(S("kt_lo"), 8)
            for u in range(4 * NT):
                t, c = divmod(u, KD)
                if u >= 2:
                    pe.wait_ge(S("pk_ab"), u - 1)
                mm3(ps[0:T, 6 + u % 2, 0:2 * P], sub(KT, A_, c, cut(t * T, T)),
                    (GM[0][:, 2:4, :], GM[1][:, 2:4, :]), True, True).then_inc(S("pk_ps"), 1)
            weights("wq")
            for u in range(8, 16):
                if u == 10:
                    pe.wait_ge(S("pk_lo"), 4 * NT)
                    pe.wait_ge(S("v_lo"), NT)
                    pe.wait_ge(S("ones_r"), 1)
                    for c in range(KD):
                        b, o = c // 2, 256 * (c % 2)
                        for t in range(NT):
                            mm3(ps[:, b, cut(o, P)], sub(PK, A_, t, cut(c * P, P)), sub(VV, A_, t, cut(c * P, P)), t == 0, t == NT - 1)
                        for t in range(NT):
                            for part in range(2):
                                last = pe.matmul(ps[:, b, cut(o + P, P)], PK[part][:, t, cut(c * P, P)], ones_r[:],
                                                 start=(t == 0 and part == 0), stop=(t == NT - 1 and part == 1))
                    last.then_inc(S("kv_ps"), 1)
                proj(u, WMA)
            pe.wait_ge(S("kt_lo"), 16)
            for u in range(8):
                c, h = divmod(u, 2)
                n0, nn = HALVES[h]
                if u >= 2:
                    pe.wait_ge(S("pk_ab"), PKU + u - 1)
                mm3(ps[:, 2 + u % 2, 0:nn], sub(GM, A_, 0, A_), sub(QT, A_, c, cut(n0, nn)), True, True)
                mm3(ps[:, 6 + u % 2, 0:nn], sub(GM, A_, 1, A_), sub(QT, A_, c, cut(n0, nn)), True, True).then_inc(S("pk_ps"), 1)
            pe.wait_ge(S("kv_lo"), 1)
            for u in range(8):
                c, h = divmod(u, 2)
                n0, nn = HALVES[h]
                pe.wait_ge(S("pk_lo"), PKU + u + 1)
                if u >= 2:
                    pe.wait_ge(S("attn"), u - 1)
                mm3(ps[:, 4 + u % 2, 0:nn], sub(KV, A_, c, cut(0, P)), sub(PQ, A_, c, cut(n0, nn)), True, True)
                mm3(ps[:, u % 2, 0:nn], sub(KV, A_, c, cut(P, P)), sub(PQ, A_, c, cut(n0, nn)), True, True).then_inc(S("attn_ps"), 1)
            weights("wp")
            pe.wait_ge(S("attn_lo"), 8)
            for t in range(NT):
                if t >= 2:
                    pe.wait_ge(S("mix_out_add"), t - 1)
                for k in range(KD):
                    last = mm3(ps[0:T, 2 + t % 2, :], sub(OT, A_, k, cut(t * T, T)), sub(WMB, A_, k, A_), k == 0, k == KD - 1)
                last.then_inc(S("mix_out_ps"), 1)

            pe.wait_ge(S("member"), 1)
            pe.wait_ge(S("consts"), 1)
            pe.wait_ge(S("mix_out_add"), NT)
            for j in range(NT):
                b, q = (6, j) if j < 3 else (7, j - 3)
                last = pe.matmul(ps[0:1, b, cut(q * CH, CH)], ones_b[:, 0:1], member[:, cut(j * CH, CH)], start=True, stop=True)
            last.then_inc(S("member_ps"), 1)
            pe.wait_ge(S("ranges"), 1)
            parts = [(0, 0, 313), (1, 313, 312)]

            def adj_transpose(j):
                pe.wait_ge(S("adj_sb"), j + 1)
                if j >= 1:
                    pe.wait_ge(S("adj_lo"), j)
                for s in range(NT):
                    b, q = (4, s) if s < 3 else (5, s - 3)
                    last = pe.transpose(ps[0:T, b, cut(q * T, T)], adj[:, j % 2, cut(s * T, T)], ident[0:T, 0:T])
                last.then_inc(S("adj_tr"), 1)

            for j in range(NT):
                steps = pe.value_load(lohi_i[0:1, 1, j:j + 1], min_val=1, max_val=NG)
                if j >= 2:
                    pe.wait_ge(S("adj_sb"), j - 1)
                for h, s0, sn in parts:
                    last = pe.matmul(ps[0:T, 2 * (j % 2) + h, 0:sn], zero_b[:, 0:T], zero_b[:, 0:sn], start=True, stop=False)
                last.then_inc(S(f"one_hot_free{j}"), G)
                with pe.Fori(0, steps) as q:
                    for i in range(G):
                        pe.wait_ge(S(f"one_hot{j}"), q * G + i + 1)
                        for h, s0, sn in parts:
                            last = pe.matmul(ps[0:T, 2 * (j % 2) + h, 0:sn], one_hot_dst[:, i, 0:T], one_hot_src[:, i, cut(s0, sn)],
                                             start=False, stop=False)
                        last.then_inc(S(f"one_hot_free{j}"), 1)
                for h, s0, sn in parts:
                    last = pe.matmul(ps[0:T, 2 * (j % 2) + h, 0:sn], zero_b[:, 0:T], zero_b[:, 0:sn], start=False, stop=True)
                last.then_inc(S("adj_ps"), 1)
                if j >= 1:
                    adj_transpose(j - 1)
            adj_transpose(NT - 1)

            pe.wait_ge(S("adj_lo"), NT)
            for L in range(NL):
                pe.wait_ge(S("e_lo"), NT * (L + 1))
                pe.wait_ge(S("em_lo"), NT * (L + 1))
                for d in range(NT):
                    n = NT * L + d
                    if d >= 2:
                        pe.wait_ge(S("h"), n - 1)
                    elif L:
                        pe.wait_ge(S("y_tr_read"), NT * L) if False else pe.wait_ge(S("relu"), 2 * NT * L)
                    b = 2 * (d % 2)
                    for s in range(NT):
                        a = (AT_hi[:, s, cut(d * T, T)], AT_lo[:, s, cut(d * T, T)])
                        mm3(ps[0:T, b, :], a, sub(EX, A_, s, A_), s == 0, s == NT - 1)
                        last = mm3(ps[0:T, b + 1, :], a, sub(EM, A_, s, A_), s == 0, s == NT - 1)
                    last.then_inc(S("agg_ps"), 1)

                def h_tr(i):
                    n = NT * L + i
                    pe.wait_ge(S("h"), n + 1)
                    if n >= 1:
                        pe.wait_ge(S("ht_lo"), n)
                    for k in range(KD):
                        last = pe.transpose(ps[:, 4, cut(k * T, T)], HN[:, i, cut(k * P, P)], ident[0:T, 0:T])
                    last.then_inc(S("h_tr"), 1)

                h_tr(0)
                weights(f"w1_{L}1")
                for i in range(NT + 2):
                    n = NT * L + i
                    if i + 1 < NT:
                        h_tr(i + 1)
                    if i == 0:
                        pe.wait_ge(S("h"), NT * (L + 1))
                    if i < NT:
                        pe.wait_ge(S("ht_lo"), n + 1)
                        if i:
                            pe.wait_ge(S("y_sb"), n)
                        for b in range(2):
                            for k in range(KD):
                                last = mm3(ps[0:T, b, :], sub(HT[i % 2], A_, cut(k * T, T)), sub(W1, A_, k, cut(b * D, D)), k == 0, k == KD - 1)
                        last.then_inc(S("w1_ps"), 1)
                    if i >= 2:
                        m = n - 2
                        pe.wait_ge(S("x_next"), m + 1)
                        if m >= 1:
                            pe.wait_ge(S("xi_lo"), m)
                        for k in range(KD):
                            last = pe.transpose(ps[:, 6, cut(k * T, T)], XC[:, i - 2, cut(k * P, P)], ident[0:T, 0:T])
                        last.then_inc(S("x_tr"), 1)
                    if 1 <= i <= NT:
                        m = n - 1
                        if i == 1:
                            weights(f"w2_{L}1")
                        pe.wait_ge(S("r_lo"), 2 * (m + 1))
                        if m >= 1:
                            pe.wait_ge(S("w2_sb"), m)
                        for k in range(KH):
                            last = mm3(ps[0:T, 5, :], sub(RT, A_, cut(k * T, T)), sub(W2, A_, k, A_), k == 0, k == KH - 1)
                        last.then_inc(S("w2_ps"), 1)
                    if i >= 2:
                        m = n - 2
                        if i == 2:
                            weights(f"cw_{L}")
                        pe.wait_ge(S("xi_lo"), m + 1)
                        if m >= 1:
                            pe.wait_ge(S("cw_add"), m)
                        for k in range(KD):
                            last = mm3(ps[0:T, 7, :], sub(XI, A_, cut(k * T, T)), sub(CW, A_, k, A_), k == 0, k == KD - 1)
                        last.then_inc(S("cw_ps"), 1)
                    if i < NT:
                        pe.wait_ge(S("y_norm"), n + 1)
                        if n >= 1:
                            pe.wait_ge(S("relu"), 2 * n)
                        for k in range(KH):
                            last = pe.transpose(ps[:, 2 + k // 4, cut((k % 4) * T, T)], YY[i % 2][:, cut(k * P, P)], ident[0:T, 0:T])
                        last.then_inc(S("y_tr"), 1)

            tr_x("fin_norm", "fin")
            weights("rw")
            for t in range(NT):
                pe.wait_ge(S("fin_lo"), t + 1)
                if t >= 2:
                    pe.wait_ge(S("log_sb"), t - 1)
                for k in range(KD):
                    last = mm3(ps[0:T, 2 + t % 2, 0:E], sub(XT, A_, k, cut(t * T, T)), sub(RW, A_, k, A_), k == 0, k == KD - 1)
                last.then_inc(S("router_ps"), 1)
            pe.wait_ge(S("mask"), 1)
            for t in range(NT):
                for q in range(t):
                    pe.matmul(ps[0:T, 4, cut(t * E, E)], ones_b[:, 0:T], MSKB[:, q, :], start=(q == 0), stop=False)
                last = pe.matmul(ps[0:T, 4, cut(t * E, E)], tri[:], MSKB[:, t, :], start=(t == 0), stop=True)
            last.then_inc(S("pos_ps"), 1)
            for e in range(E):
                pe.wait_ge(S("sel"), e + 1)
                for t in range(NT):
                    last = pe.matmul(ps[0:CAP, 5, cut(7 * e, 7)], SELT[e % UNROLL][:, t, :], MTAB[:, t, e, 0:7], start=(t == 0), stop=(t == NT - 1))
                last.then_inc(S("sel_used"), 1)

            weights("sd1")
            pe.wait_ge(S("log_sb"), NT)

            def shared_down(n):
                t, s = divmod(n, 2)
                pe.wait_ge(S("s_t_lo"), n + 1)
                if s == 0 and t >= 1:
                    pe.wait_ge(S("shared_add"), t)
                for k in range(2):
                    last = mm3(ps[0:T, 7, :], sub(ST, A_, cut(k * T, T)), sub(SD[s], A_, k, A_), s == 0 and k == 0, s == 1 and k == 1)
                if s == 1:
                    last.then_inc(S("shared_ps"), 1)

            for n in range(2 * NT):
                t, s = divmod(n, 2)
                if n >= 2:
                    pe.wait_ge(S("hg"), n - 1)
                for k in range(KD):
                    last = mm3(ps[0:T, 2 + n % 2, :], sub(XT, A_, k, cut(t * T, T)), sub(SG[s], A_, k, A_), k == 0, k == KD - 1)
                last.then_inc(S("gu_ps"), 1)
                if n >= 1:
                    shared_down(n - 1)
                pe.wait_ge(S("hg"), n + 1)
                for k in range(2):
                    last = pe.transpose(ps[:, 6, cut(k * T, T)], HG[n % 2][0:T, cut(k * P, P)], ident[0:T, 0:T])
                last.then_inc(S("ht_ps"), 1)
            shared_down(2 * NT - 1)

            def after(name, value):
                if not isinstance(value, int) or value > 0:
                    pe.wait_ge(S(name), value)

            def transpose_x(e, r, turn):
                pe.wait_ge(S(f"xg_in{r}"), 16 * turn + 16)
                after("xe_sb", e - 1)
                for k in range(KD):
                    last = pe.transpose(ps[:, r % 2, cut(k * CAP, CAP)], XG[r][:, cut(k * P, P)], ident[0:CAP, 0:CAP])
                last.then_inc(S("xe_ps"), 1)

            def gate_up(e, r, turn):
                pe.wait_ge(S(f"ring_in{r}"), 16 * turn + 16)
                pe.wait_ge(S("xe_sb"), e + 1)
                after("hg", NSH + e - 1)
                for k in range(KD):
                    last = pe.matmul(ps[0:CAP, 2 + r % 2, :], XE[r % 2][:, cut(k * CAP, CAP)], RING[r][:, cut(512 * k, 512)],
                                     start=(k == 0), stop=(k == KD - 1))
                last.then_inc(S("gu_ps"), 1)

            def down(e, r):
                pe.wait_ge(S("ht_sb"), e + 1)
                after("scaled", e - 1)
                for k in range(2):
                    last = pe.matmul(ps[0:CAP, 6 + r % 2, :], HTF[r % 2][:, cut(k * CAP, CAP)], RING[r][:, cut(2048 + 512 * k, 512)],
                                     start=(k == 0), stop=(k == 1))
                last.then_inc(S("o_ps"), 1)

            def transpose_h(e, r):
                pe.wait_ge(S("hg"), NSH + e + 1)
                after("ht_sb", e - 1)
                for k in range(2):
                    last = pe.transpose(ps[:, 4 + r % 2, cut(k * CAP, CAP)], HG[r % 2][0:CAP, cut(k * P, P)], ident[0:CAP, 0:CAP])
                last.then_inc(S("ht_ps"), 1)

            pe.wait_ge(S("shared_add"), NT)
            transpose_x(0, 0, 0)
            for r in range(UNROLL):
                transpose_x(r + 1, (r + 1) % UNROLL, (r + 1) // UNROLL)
                gate_up(r, r, 0)
                if r >= 1:
                    down(r - 1, r - 1)
                transpose_h(r, r)
            with pe.Fori(1, E // UNROLL - 1) as i:
                for r in range(UNROLL):
                    e = UNROLL * i + r
                    transpose_x(e + 1, (r + 1) % UNROLL, i + 1 if r == UNROLL - 1 else i)
                    gate_up(e, r, i)
                    down(e - 1, (r - 1) % UNROLL)
                    transpose_h(e, r)
            turn = E // UNROLL - 1
            for r in range(UNROLL):
                e = E - UNROLL + r
                if e + 1 < E:
                    transpose_x(e + 1, r + 1, turn)
                gate_up(e, r, turn)
                down(e - 1, (r - 1) % UNROLL)
                transpose_h(e, r)
            down(E - 1, UNROLL - 1)


def kernel(**inputs):
    import numpy as np
    import concourse.bacc as bacc
    from concourse import mybir as mb
    from concourse.bass_utils import run_bass_kernel_spmd as run

    g = {k: np.asarray(v) for k, v in inputs.items()}
    gn, mx, ff = (lambda n: g["L0_gnn_" + n]), (lambda n: g["L0_mix_" + n]), (lambda n: g["L0_ffn_" + n])

    def column(v):
        return v.reshape(-1, P).T

    def pack(gate, up, down):
        n = gate.shape[0]
        gu = np.concatenate([gate, up], axis=1).transpose(0, 2, 1).reshape(n, KD, P, 2 * F).transpose(0, 2, 1, 3)
        dn = down.transpose(0, 2, 1).reshape(n, 2, P, D).transpose(0, 2, 1, 3)
        return np.concatenate([gu.reshape(n, P, -1), dn.reshape(n, P, -1)], axis=2)

    scalars = [mx("gamma_q"), mx("beta_q"), mx("gamma_k"), mx("beta_k"), gn("t0"), gn("t1"), gn("t2")]
    cols = np.concatenate([column(gn(f"mlg_{L}")) for L in range(NL)] + [column(gn(f"mlb_{L}")) for L in range(NL)]
                          + [column(mx("bq")), column(mx("bk"))] + [np.broadcast_to(s, (P, 1)) for s in scalars], axis=1)
    rows = [mx("bv"), mx("bp"), gn("cb"), gn("mb1_0"), gn("mb2_0")]
    for L in range(1, NL):
        rows += [gn(f"mb1_{L}"), gn(f"mb2_{L}"), gn(f"lng_{L}"), gn(f"lnb_{L}")]
    ins = {
        "x": g["x"], "src": g["src"].reshape(CH, T).T, "dst": g["dst"].reshape(CH, T).T,
        "cols": cols, "rows": np.concatenate(rows),
        "w1": np.stack([gn(f"mw1_{L}") for L in range(NL)]), "w2": np.stack([gn(f"mw2_{L}") for L in range(NL)]),
        "cw": gn("cw"), "wmix": np.stack([mx(n) for n in ("Wq", "Wk", "Wv", "Wp")]),
        "gmix": np.stack([mx(n) for n in ("qG1", "qG2", "kG1", "kG2")]),
        "router": ff("router_w").T, "rbias": ff("bias"),
        "shared": pack(ff("shared_w_gate"), ff("shared_w_up"), ff("shared_w_down")),
        "experts": pack(ff("w_gate"), ff("w_up"), ff("w_down")),
    }
    nc = bacc.Bacc("TRN2", target_bir_lowering=False, num_devices=1)
    arrays, args = {}, []
    for name, a in ins.items():
        a = np.ascontiguousarray(a)
        arrays[name + "_in"] = a
        args.append(nc.dram_tensor(name + "_in", a.shape, mb.dt.from_np(a.dtype), kind="ExternalInput").ap())
    args.append(nc.dram_tensor("out_x", (N, D), mb.dt.float32, kind="ExternalOutput").ap())
    gps_kernel(nc, *args)
    return run(nc, [arrays], core_ids=[0]).results[0]["out_x"]
```

```python
from contextlib import ExitStack

import concourse.bass as bass
from concourse import mybir

F32 = mybir.dt.float32
F32R = mybir.dt.float32r
BF16 = mybir.dt.bfloat16
F16 = mybir.dt.float16
I32 = mybir.dt.int32
ACT = mybir.ActivationFunctionType
ALU = mybir.AluOpType
AX = mybir.AxisListType
RMAX = bass.bass_isa.ReduceOp.max

N = 625
T = 125
NT = N // T
D = 512
H = 1024
P = 128
KD = D // P
KH = H // P
TP = N + 1
HALVES = [(0, 314), (314, 312)]
NL = 3
EDGES = 20625
CH = EDGES // T
G = 5
NG = CH // G
E = 64
F = 256
TOPK = 6
CAP = int(N * TOPK * 2.0 / E)
WE = KD * 2 * F + (F // P) * D
FAR = 200.0
SKIP = 100000.0
UNROLL = 4
PKU = NT
NSH = 2 * NT
NW = 63

COL_LG, COL_LB, COL_BQ, COL_BK, COL_S = 0, 24, 48, 52, 56


def gps_kernel(nc, x, src, dst, cols, rows, w1, w2, cw, wmix, gmix, router, rbias, shared, experts, out):
    xn2 = nc.dram_tensor("xn2_scratch", (N, D), F32, kind="Internal").ap()
    yrow = nc.dram_tensor("yrow_scratch", (N * TOPK, D), F32, kind="Internal").ap()

    with ExitStack() as ctx:
        base = [16512]

        def sb(name, shape, dt, at=None):
            size = {F32: 4, F32R: 4, I32: 4, BF16: 2, F16: 2}[dt]
            for s in shape[1:]:
                size *= s
            if at is None:
                at = base[0]
                base[0] += -(-size // 32) * 32
                assert base[0] <= 229344, (name, base[0])
            return nc.alloc_sbuf_tensor_at(name, shape, dt, offset=at)

        sems = {}

        def S(name):
            if name not in sems:
                sems[name] = ctx.enter_context(nc.semaphore(name))
            return sems[name]

        RG_WORDS = 5008 + 8192 + 4096 + 10240 + 6250
        rg_at = base[0]
        RG = sb("split_operands", [P, RG_WORDS], F32R)
        o_xt, o_w1, o_cw, o_e, o_at = 0, 5008, 13200, 17296, 27536

        def rg(o, *dims, p=P):
            n = 1
            for q in dims:
                n *= q
            v = RG[0:p, o:o + n]
            if len(dims) == 2:
                v = v.rearrange("p (a b) -> p a b", a=dims[0])
            if len(dims) == 3:
                v = v.rearrange("p (a b c) -> p a b c", a=dims[0], b=dims[1])
            return v

        def pair(o, *dims, p=P):
            n = 1
            for q in dims:
                n *= q
            return rg(o, *dims, p=p), rg(o + n, *dims, p=p)

        XT = pair(o_xt, KD, TP)
        HT = [pair(o_xt + 1000 * i, 4 * T) for i in range(2)]
        RT = pair(o_xt + 2000, 8 * T)
        XI = pair(o_xt + 4000, 4 * T)
        W1 = pair(o_w1, KD, H)
        CW = pair(o_cw, KD, D)
        W2 = pair(o_e, KH, D)
        EX = pair(o_e, NT, D, p=T)
        EM = pair(o_e + 5120, NT, D, p=T)
        AT_hi = rg(o_at, NT, N, p=T)
        AT_lo = rg(o_at + 3125, NT, N, p=T)
        WMA, WMB = pair(o_cw, KD, D), pair(o_at, KD, D)
        VV = pair(o_e, NT, D, p=T)
        KT = pair(o_e + 5120, KD, TP)
        QT = KT
        PK = pair(o_w1, NT, D, p=T)
        PQ = pair(o_e, KD, TP)
        OT = pair(o_w1, KD, TP)
        KV = pair(o_w1 + 5120, KD, 256)
        GM = pair(o_w1 + 7168, 4, P)
        RW = pair(o_at + 0, KD, E)
        SG = [pair(o_w1 + 6144 * s, KD, 2 * F) for s in range(2)]
        SD = [pair(o_w1 + 6144 * s + 4096, 2, D) for s in range(2)]
        ST = pair(o_at + 3125, 2 * T)
        RING = [sb(f"expert_weights{r}", [P, WE], F32, at=rg_at + 4 * (17296 + r * WE)) for r in range(UNROLL)]

        XO = sb("x_out", [T, NT, D], F32)
        XC = sb("x_cur", [T, NT, D], F32)
        fg_at = base[0]
        FG = sb("work", [P, 13312], F32)

        def fg(o, *dims, p=P):
            n = 1
            for q in dims:
                n *= q
            v = FG[0:p, o:o + n]
            if len(dims) == 2:
                v = v.rearrange("p (a b) -> p a b", a=dims[0])
            if len(dims) == 3:
                v = v.rearrange("p (a b c) -> p a b c", a=dims[0], b=dims[1])
            return v

        HN = fg(0, NT, D, p=T)
        STG = [fg(2560 + 2048 * i, 2048) for i in range(2)]
        BC1 = fg(6656, H, p=T)
        BC2, BCG, BCB = [fg(7680 + 512 * i, D, p=T) for i in range(3)]
        YY = [fg(9216 + 1024 * i, H, p=T) for i in range(2)]
        RR = fg(11264, 8 * T)
        EE = [fg(11264 + 512 * i, D, p=T) for i in range(2)]
        EP = [fg(12288 + 512 * i, D, p=T) for i in range(2)]
        LN = fg(12288, D, p=T)
        LN2 = fg(12800, D, p=T)
        MT = [fg(9216 + 1024 * i, 512) for i in range(2)]
        MT2 = [fg(9728 + 1024 * i, 512) for i in range(2)]
        MT3 = [fg(11264 + 512 * i, 512) for i in range(2)]
        iota_i = fg(2560, N + 1, p=T).bitcast(I32)
        los, his = [fg(NT * CH * i, NT, CH, p=1) for i in range(2)]
        gidx = fg(3200, 2, CH, p=1)
        gsteps = fg(1800, NT, NG, p=1)
        gidx_i = fg(3540, CH, p=1).bitcast(I32)
        iota_h = FG[0:T, 3720:3720 + 313].bitcast(F16)
        member = FG[0:T, 4040:4040 + 413].bitcast(BF16)
        srcf = fg(4460, 2 * CH, p=T)
        dstrel = fg(4800, NT, 2 * CH, p=T)
        one_hot_src = FG[0:T, 6656:6656 + G * 313].bitcast(BF16).rearrange("p (g n) -> p g n", g=G)
        one_hot_dst = FG[0:T, 8224:8224 + G * 63].bitcast(BF16).rearrange("p (g n) -> p g n", g=G)
        srci = fg(8544, CH, p=T).bitcast(I32)
        dsti = fg(8712, CH, p=T).bitcast(I32)
        ge = fg(8880, CH, p=T)
        adj = fg(9216, 2, N, p=T)
        zero_b = FG[0:T, 10600:10856].bitcast(BF16)
        LOG, PRB, MSK, KRK, POS, GAT = [fg(320 * i, NT, E, p=T) for i in range(6)]
        SELT = [FG[0:T, 2560 + 320 * i:2560 + 320 * i + 293].bitcast(BF16)[:, 0:NT * CAP].rearrange("p (t s) -> p t s", t=NT) for i in range(4)]
        MTAB = FG[0:T, 3840:3840 + NT * E * 4].bitcast(BF16).rearrange("p (t e c) -> p t e c", t=NT, e=E)
        MSKB = FG[0:T, 5120:5120 + 160].bitcast(BF16).rearrange("p (t e) -> p t e", t=NT)
        POSB = FG[0:T, 5280:5280 + 160].bitcast(BF16).rearrange("p (t e) -> p t e", t=NT)
        TAB = fg(5440, E, 7, p=CAP)
        GR = fg(6656, 3, NT * E, p=T)
        RBC = fg(7640, E, p=T)
        SIL = [fg(7720 + 256 * i, F, p=P) for i in range(2)]
        HG = [fg(8232 + 256 * i, F, p=P) for i in range(2)]
        HTF = [fg(8744 + 256 * i, 2 * CAP) for i in range(2)]
        XE = [fg(9256 + 480 * i, KD * CAP) for i in range(2)]
        XG = [fg(10216 + 512 * i, D, p=CAP) for i in range(4)]
        OS = [fg(0 + 512 * i, D, p=CAP) for i in range(4)]
        YL = [rg(TOPK * D * i, TOPK, D, p=T).bitcast(F32) for i in range(NT)]
        ZB = fg(10216, D)

        pnum_i = fg(12300, 1, p=T).bitcast(I32)
        pnum = fg(12302, 1, p=T)
        snum_i = fg(12310, CAP + 1, p=T).bitcast(I32)
        ysum = fg(9216, D, p=T)
        ones_f = fg(12288, P, p=T)

        ident = sb("ident", [P, P], F32)
        colp = sb("colp", [P, NW], F32)
        ones_r = sb("ones_r", [T, P], F32R)
        gb = sb("gb", [P, 8], F32)
        mhalf = sb("mhalf", [T, NT], F32)
        stats = sb("stats", [T, NT, 2, 6], F32)
        mv = sb("mv", [T, NT, 2], F32)
        rstd = sb("rstd", [T, NT], F32)
        st_m = sb("st_m", [T, 2, 6], F32)
        mv_m = sb("mv_m", [T, 4], F32)
        st_o = sb("st_o", [T, 1, 6], F32)
        mv_o = sb("mv_o", [T, 4], F32)
        zmx = sb("zmx", [T, NT + 3], F32)
        lohi = sb("lohi", [1, 2, NT], F32)
        lohi_i = sb("lohi_i", [1, 2, NT], I32)
        tri = sb("tri", [T, T], BF16)
        ones_b = sb("ones_b", [T, P], BF16)
        iota_s = sb("iota_s", [T, CAP + 1], BF16)
        gat_s = sb("gat_s", [CAP, E], F32)
        tok_i = sb("tok_i", [CAP, E], I32)
        row_i = sb("row_i", [CAP, E], I32)
        tok_c = sb("tok_c", [CAP, UNROLL], I32)
        row_c = sb("row_c", [CAP, UNROLL], I32)
        r8 = sb("r8", [T, NT, 8], F32)
        rsm = sb("rsm", [T, 4, NT], F32)
        rden = sb("rden", [T, 8], F32)
        tokf = fg(12500, 2, E, p=CAP)

        ps = ctx.enter_context(nc.psum_tensor("ps", [P, 8, 512], F32))

        pe, dve, act, pool, sp = nc.tensor, nc.vector, nc.scalar, nc.gpsimd, nc.sync

        def f(ap):
            return ap.bitcast(F32)

        def mm3(o, a, b, start, stop):
            pe.matmul(o, a[1], b[0], start=start, stop=False)
            pe.matmul(o, a[0], b[1], start=False, stop=False)
            return pe.matmul(o, a[0], b[0], start=False, stop=stop)

        def sub(p, *ix):
            return (p[0][ix], p[1][ix])

        def by_pair(v):
            return v[0:T, :].rearrange("p (c n) -> p c n", c=KD)

        def two_banks(b):
            return ps[0:T, b:b + 2, :].rearrange("p b (c a n) -> p (b c) a n", c=2, a=2)

        def phi_k_banks(t):
            return two_banks(2 if t % 2 else 6)

        def attn_banks(t):
            return two_banks(4 if t % 2 else 6)

        kv_bank = ps[:, 0:2, :].rearrange("p b (c n) -> p (b c) n", c=2)

        def kv_block(v, h):
            return v[64 * h:64 * h + 64].rearrange("p c (a n) -> p c a n", a=2)[:, :, :, 64 * h:64 * h + 64]

        A_ = slice(None)

        def cut(o, n):
            return slice(o, o + n)

        vstep = [0]

        def v1(ins):
            vstep[0] += 1
            ins.then_inc(S("vector_step"), 1)
            dve.wait_ge(S("vector_step"), vstep[0])

        astep = [0]

        def a1(ins):
            astep[0] += 1
            ins.then_inc(S("scalar_step"), 1)
            act.wait_ge(S("scalar_step"), astep[0])

        gstep = [0]

        def g1(ins):
            gstep[0] += 1
            ins.then_inc(S("pool_step"), 1)
            pool.wait_ge(S("pool_step"), gstep[0])

        w1v = [w1[L].rearrange("(k p) n -> p k n", p=P) for L in range(NL)]
        w2v = [w2[L].rearrange("(k p) n -> p k n", p=P) for L in range(NL)]
        cwv = [cw[L * D:(L + 1) * D, :].rearrange("(k p) n -> p k n", p=P) for L in range(NL)]
        wmv = [wmix[i].rearrange("(k p) n -> p k n", p=P) for i in range(4)]
        plan = []

        def piece(name, source, parts, free=None):
            plan.append((name, source, parts, free))

        piece("wv", wmv[2], WMA)
        piece("wk", wmv[1], WMB)
        piece("g", None, GM)
        piece("wq", wmv[0], WMA, ("v_ps", NT))
        piece("wp", wmv[3], WMB, ("kt_ps", 8))
        for L in range(NL):
            gone = ("mix_out_ps", NT) if L == 0 else ("w1_ps", NT * L)
            for k in range(2):
                piece(f"w1_{L}{k}", w1v[L][:, 2 * k:2 * k + 2, :], sub(W1, A_, cut(2 * k, 2), A_), gone)
            piece(f"cw_{L}", cwv[L], CW, ("mix_out_ps", NT) if L == 0 else ("cw_ps", NT * L))
            for k in range(2):
                piece(f"w2_{L}{k}", w2v[L][:, 4 * k:4 * k + 4, :], sub(W2, A_, cut(4 * k, 4), A_), ("agg_ps", NT * (L + 1)))
        piece("rw", router.rearrange("(k p) n -> p k n", p=P), RW, ("agg_ps", NT * NL))
        for s in range(2):
            gone = ("cw_ps", NT * NL)
            piece(f"sg{s}", shared[s, :, 0:KD * 2 * F].rearrange("p (k n) -> p k n", k=KD), SG[s], gone)
            piece(f"sd{s}", shared[s, :, KD * 2 * F:WE].rearrange("p (k n) -> p k n", k=2), SD[s], gone)
        order = {n: i for i, (n, _, _, _) in enumerate(plan)}

        def staged(i):
            parts = plan[i][2][0]
            n = 1
            for q in parts.shape[1:]:
                n *= q
            v = STG[i % 2][:, 0:n]
            return v.rearrange("p (k n) -> p k n", k=parts.shape[1])

        def split_hi(name):
            i = order[name]
            act.wait_ge(S(f"stage_in{i % 2}"), 16 * (i // 2 + 1) + (16 if i >= order["g"] and i % 2 == order["g"] % 2 else 0))
            free = plan[i][3]
            if free:
                act.wait_ge(S(free[0]), free[1])
            act.activation(plan[i][2][0], staged(i), ACT.Copy).then_inc(S("weight_hi"), 1)

        def split_lo(name):
            i = order[name]
            dve.wait_ge(S("weight_hi"), i + 1)
            dve.tensor_tensor(plan[i][2][1], staged(i), f(plan[i][2][0]), ALU.subtract).then_inc(S("weight_lo"), 1)

        def weights(name):
            pe.wait_ge(S("weight_lo"), order[name] + 1)


        block = ctx.enter_context(nc.Block())

        @block.sync
        def _(eng):
            sp.dma_start(XO[:], x.rearrange("(t p) f -> p t f", p=T)).then_inc(S("x_in"), 16)
            sp.dma_start(colp[:], cols).then_inc(S("cols_in"), 16)
            sp.dma_start(BC1[:, 0:D], rows[0:D].partition_broadcast(T)).then_inc(S("mixrow_in"), 16)
            sp.dma_start(BC1[:, D:H], rows[D:2 * D].partition_broadcast(T)).then_inc(S("mixrow_in"), 16)
            sp.dma_start(BC2, rows[2 * D:3 * D].partition_broadcast(T)).then_inc(S("mixrow_in"), 16)

            def load(name):
                i = order[name]
                if i >= 2:
                    sp.wait_ge(S("weight_lo"), i - 1)
                if name == "g":
                    sp.wait_ge(S("stage_zero"), 1)
                    gv = staged(i)
                    sp.dma_start(gv[0:64, :, 0:64], gmix.rearrange("g p n -> p g n")).then_inc(S(f"stage_in{i % 2}"), 16)
                    sp.dma_start(gv[64:128, :, 64:128], gmix.rearrange("g p n -> p g n")).then_inc(S(f"stage_in{i % 2}"), 16)
                else:
                    sp.dma_start(staged(i), plan[i][1]).then_inc(S(f"stage_in{i % 2}"), 16)

            for n in ("wv", "wk"):
                load(n)
            sp.dma_start(srci, src).then_inc(S("edges_in"), 16)
            sp.dma_start(dsti, dst).then_inc(S("edges_in"), 16)
            for n in ("g", "wq", "wp"):
                load(n)
            sp.wait_ge(S("adj_lo"), NT)
            r = 3 * D
            for L in range(NL):
                if L:
                    sp.wait_ge(S("x_next"), NT * L)
                sp.dma_start(BC1, rows[r:r + H].partition_broadcast(T)).then_inc(S("rows_in"), 16)
                sp.dma_start(BC2, rows[r + H:r + H + D].partition_broadcast(T)).then_inc(S("rows_in"), 16)
                r += H + D
                if L:
                    sp.dma_start(BCG, rows[r:r + D].partition_broadcast(T)).then_inc(S("rows_in"), 16)
                    sp.dma_start(BCB, rows[r + D:r + 2 * D].partition_broadcast(T)).then_inc(S("rows_in"), 16)
                    r += 2 * D
                for n in (f"w1_{L}0", f"w1_{L}1", f"cw_{L}", f"w2_{L}0", f"w2_{L}1"):
                    load(n)
            sp.wait_ge(S("x_next"), NT * NL)
            sp.dma_start(RBC, rbias.partition_broadcast(T)).then_inc(S("rbias_in"), 16)
            sp.wait_ge(S("zeros_made"), 1)
            for q in range(NT):
                sp.dma_start(yrow[750 * q:750 * (q + 1), :].rearrange("(p a) n -> p a n", p=T),
                             ZB[0:T, :].unsqueeze(1).to_broadcast([T, TOPK, D])).then_inc(S("y_zero"), 16)
            for n in ("rw", "sg0", "sd0", "sg1", "sd1"):
                load(n)
            sp.wait_ge(S("fin_norm"), NT)
            sp.dma_start(xn2.rearrange("(t p) f -> p t f", p=T), XC[:]).then_inc(S("xn2_out"), 16)
            sp.wait_ge(S("w2_ps"), NT * NL)

            def load_expert(e, r):
                sp.dma_start(RING[r][:], experts[e].rearrange("a p n -> (a p) n")).then_inc(S(f"ring_in{r}"), 16)

            for r in range(UNROLL):
                if r == UNROLL - 1:
                    sp.wait_ge(S("router_ps"), NT)
                load_expert(cut(r, 1), r)
            with sp.Fori(1, E // UNROLL) as i:
                for r in range(UNROLL):
                    sp.wait_ge(S("o_ps"), UNROLL * i + r - 3)
                    load_expert(bass.ds(UNROLL * i + r, 1), r)
            for r in range(UNROLL):
                sp.wait_ge(S(f"y_out{r}"), 16 * (E // UNROLL))
            for t in range(NT):
                sp.dma_start(YL[t], yrow[750 * t:750 * (t + 1), :].rearrange("(p a) n -> p a n", p=T)).then_inc(S(f"y_in{t}"), 16)
            for t in range(NT):
                sp.wait_ge(S("y_sum"), t + 1)
                sp.dma_start(out[T * t:T * (t + 1), :], XO[:, t, :]).then_inc(S("out_done"), 16)
            sp.wait_ge(S("out_done"), 16 * NT)

        @block.gpsimd
        def _(eng):
            g1(pool.memset(ident[:], 0.0))
            pool.affine_select(out=ident[:], in_=ident[:], compare_op=ALU.not_equal, fill=1.0, base=0,
                               pattern=[[-1, P]], channel_multiplier=1).then_inc(S("pool_consts"), 1)
            g1(pool.memset(mhalf[:], -0.5))
            pool.memset(f(XT[0][:, :, N:TP]), 0.0)
            pool.memset(f(XT[1][:, :, N:TP]), 0.0)
            pool.memset(f(KV[0]), 0.0)
            pool.memset(f(KV[1]), 0.0).then_inc(S("pool_consts"), 1)
            g1(pool.memset(tri[:], 1.0))
            pool.affine_select(out=tri[:], in_=tri[:], compare_op=ALU.is_gt, fill=0.0, base=0,
                               pattern=[[1, T]], channel_multiplier=-1)
            pool.memset(ones_b[:], 1.0).then_inc(S("pool_consts"), 1)

            def rsqrt(o, i, n, wait, value, done):
                pool.wait_ge(S(wait), value)
                pool.tensor_tensor(o, i, mhalf[:, 0:n], ALU.pow).then_inc(S(done), 1)

            rsqrt(rstd[:], mv[:, :, 1], NT, "in_var", 1, "in_rstd")
            pool.wait_ge(S("weight_lo"), 1)
            pool.memset(STG[order["g"] % 2][:, 0:4 * P], 0.0).then_inc(S("stage_zero"), 1)
            pool.wait_ge(S("in_norm"), NT)
            pool.wait_ge(S("mixrow_in"), 48)
            for t in range(NT):
                g1(pool.tensor_tensor(XO[:, t, :], XO[:, t, :], BC1[:, D:H], ALU.add))
                pool.tensor_tensor(XO[:, t, :], XO[:, t, :], BC2, ALU.add).then_inc(S("x_rows"), 1)
            for t in range(NT):
                pool.wait_ge(S("v_hi"), t + 1)
                pool.tensor_tensor(VV[1][:, t, :], MT[t % 2][0:T, :], f(VV[0][:, t, :]), ALU.subtract).then_inc(S("v_lo"), 1)
            pool.wait_ge(S("weight_lo"), order["wp"] + 1)
            pool.iota(iota_i, pattern=[[1, N + 1]], base=0, channel_multiplier=0).then_inc(S("iota"), 1)
            pool.iota(gidx_i, pattern=[[1, CH]], base=0, channel_multiplier=0).then_inc(S("iota"), 1)
            for L in range(NL):
                pool.wait_ge(S("zmax"), L + 1)
                pool.partition_all_reduce(zmx[:, NT + 1:NT + 2], zmx[:, NT:NT + 1], T, RMAX).then_inc(S("zmax_all"), 1)
                for i in range(NT + 1):
                    n = NT * L + i
                    if i < NT:
                        rsqrt(mv_m[:, 2:3], mv_m[:, 1:2], 1, "mlp_var", n + 1, "mlp_rstd")
                    if L and i >= 1:
                        m = NT * (L - 1) + i
                        rsqrt(mv_o[:, 2:3], mv_o[:, 1:2], 1, "out_var", m, "out_rstd")
            pool.wait_ge(S("x_next"), NT * NL)
            pool.wait_ge(S("r_lo"), 2 * NT * NL)
            pool.memset(ZB, 0.0).then_inc(S("zeros_made"), 1)
            rsqrt(rstd[:], mv[:, :, 1], NT, "fin_var", 1, "fin_rstd")
            pool.iota(pnum_i, pattern=[[0, 1]], base=0, channel_multiplier=1)
            pool.iota(snum_i, pattern=[[1, CAP + 1]], base=0, channel_multiplier=0).then_inc(S("iota"), 1)
            pool.wait_ge(S("y_zero"), 16 * NT)
            for r in range(UNROLL):
                last = pool.memset(XG[r], 0.0)
            last.then_inc(S("xg_zero"), 1)
            pool.wait_ge(S("xg_zero"), 1)
            pool.wait_ge(S("xn2_out"), 16)
            pool.wait_ge(S("tables"), 1)

            last_token = pool.to_reg(N - 1)
            last_row = pool.to_reg(N * TOPK - 1)

            def gather(n, r):
                pool.wait_ge(S("tok_col"), n + 1)
                pool.sem_inc(S("pool_turns"), 1)
                pool.indirect_dma_start(XG[r], None, xn2, bass.IndirectOffsetOnAxis(ap=tok_c[:, cut(r, 1)], axis=0),
                                        bounds_check=last_token, oob_is_err=False).then_inc(S(f"xg_in{r}"), 16)

            def scatter(n, r):
                pool.wait_ge(S("scaled"), n + 1)
                pool.sem_inc(S("pool_turns"), 1)
                pool.indirect_dma_start(yrow, bass.IndirectOffsetOnAxis(ap=row_c[:, cut(r, 1)], axis=0), OS[r], None,
                                        bounds_check=last_row, oob_is_err=False).then_inc(S(f"y_out{r}"), 16)

            for e in range(UNROLL):
                gather(e, e)
            for e in range(UNROLL):
                gather(e + UNROLL, e)
                scatter(e, e)
            with pool.Fori(1, E // UNROLL - 1) as i:
                for r in range(UNROLL):
                    e = UNROLL * i + r
                    gather(e + UNROLL, r)
                    scatter(e, r)
            for r in range(UNROLL):
                scatter(E - UNROLL + r, r)

        @block.scalar
        def _(eng):
            def tr_hi(which):
                for t in range(NT):
                    act.wait_ge(S(which + "_tr"), t + 1)
                    act.activation(XT[0][:, :, cut(t * T, T)], ps[:, t % 2, 0:KD * T].rearrange("p (k n) -> p k n", k=KD),
                                   ACT.Copy).then_inc(S(which + "_hi"), 1)

            split_hi("wv")
            tr_hi("in")
            split_hi("wk")
            for t in range(NT):
                act.wait_ge(S("v_sb"), t + 1)
                act.activation(VV[0][:, t, :], MT[t % 2][0:T, :], ACT.Copy).then_inc(S("v_hi"), 1)
                if t == 1:
                    split_hi("g")
            act.wait_ge(S("cols_in"), 16)
            act.wait_ge(S("gb"), 1)

            def proj(u):
                q = u >= 8
                c, h = divmod(u % 8, 2)
                n0, nn = HALVES[h]
                act.wait_ge(S("kt_ps"), u + 1)
                if u >= 2:
                    act.wait_ge(S("kt_lo"), u - 1)
                act.activation(MT2[u % 2][:, 0:nn], ps[:, 4 + u % 2, 0:nn], ACT.Identity,
                               bias=gb[:, cut((0 if q else 4) + c, 1)],
                               scale=colp[:, cut(COL_S + (0 if q else 2), 1)]).then_inc(S("kt_sb"), 1)
                act.wait_ge(S("kt_sb"), u + 1)
                if u == 8:
                    act.wait_ge(S("pk_ps"), NT)
                act.activation(KT[0][:, c, cut(n0, nn)], MT2[u % 2][:, 0:nn], ACT.Copy).then_inc(S("kt_hi"), 1)

            for u in range(8):
                proj(u)
                if u == 3:
                    split_hi("wq")
            split_hi("wp")
            act.wait_ge(S("v_lo"), NT)

            def pk_scale(t):
                act.wait_ge(S("pk_ps"), t + 1)
                if t >= 2:
                    act.wait_ge(S("pk_lo"), t - 1)
                act.activation(by_pair(MT[t % 2]), phi_k_banks(t)[:, :, 0, :], ACT.Copy, scale=0.125).then_inc(S("pk_a"), 1)

            def pk_square(t):
                act.wait_ge(S("pk_ab"), t + 1)
                a1(act.activation(MT[t % 2][0:T, :], MT3[t % 2][0:T, :], ACT.Square))
                act.activation(PK[0][:, t, :], MT[t % 2][0:T, :], ACT.Copy).then_inc(S("pk_hi"), 1)

            pk_scale(0)
            for t in range(NT):
                if t + 1 < NT:
                    pk_scale(t + 1)
                pk_square(t)
            act.wait_ge(S("kv_ps"), 1)
            for h in range(2):
                last = act.activation(kv_block(KV[0], h), kv_block(kv_bank, h), ACT.Copy)
            last.then_inc(S("kv_hi"), 1)
            for u in range(8, 16):
                proj(u)

            def pq_scale(u):
                nn = HALVES[u % 2][1]
                act.wait_ge(S("pk_ps"), PKU + u + 1)
                if u >= 2:
                    act.wait_ge(S("pk_lo"), PKU + u - 1)
                act.activation(MT[u % 2][:, 0:nn], ps[:, 2 + u % 2, 0:nn], ACT.Copy, scale=0.125).then_inc(S("pk_a"), 1)

            def pq_square(u):
                c, h = divmod(u, 2)
                n0, nn = HALVES[h]
                act.wait_ge(S("pk_ab"), PKU + u + 1)
                a1(act.activation(MT[u % 2][:, 0:nn], MT3[u % 2][:, 0:nn], ACT.Square))
                act.activation(PQ[0][:, c, cut(n0, nn)], MT[u % 2][:, 0:nn], ACT.Copy).then_inc(S("pk_hi"), 1)

            pq_scale(0)
            for u in range(8):
                if u + 1 < 8:
                    pq_scale(u + 1)
                pq_square(u)
            for t in range(NT):
                act.wait_ge(S("attn_tr"), t + 1)
                act.activation(OT[0][:, :, cut(t * T, T)], ps[:, t % 2, 0:KD * T].rearrange("p (k n) -> p k n", k=KD),
                               ACT.Copy).then_inc(S("attn_hi"), 1)

            def adj_out(j):
                act.wait_ge(S("adj_ps"), j + 1)
                if j >= 2:
                    act.wait_ge(S("adj_tr"), j - 1)
                act.activation(adj[:, j % 2, 0:313], ps[0:T, 2 * (j % 2), 0:313], ACT.Copy)
                act.activation(adj[:, j % 2, 313:N], ps[0:T, 2 * (j % 2) + 1, 0:312], ACT.Copy).then_inc(S("adj_sb"), 1)

            adj_out(0)
            for j in range(NT):
                if j + 1 < NT:
                    adj_out(j + 1)
                act.wait_ge(S("adj_tr"), j + 1)
                act.activation(AT_hi[:, 0:3, cut(j * T, T)], ps[0:T, 4, 0:3 * T].rearrange("p (s n) -> p s n", s=3), ACT.Copy)
                act.activation(AT_hi[:, 3:5, cut(j * T, T)], ps[0:T, 5, 0:2 * T].rearrange("p (s n) -> p s n", s=2),
                               ACT.Copy).then_inc(S("adj_hi"), 1)

            for L in range(NL):
                act.wait_ge(S("zmax_neg"), L + 1)
                for t in range(NT + 1):
                    n = NT * L + t
                    if t < NT:
                        if t >= 2:
                            act.wait_ge(S("e_lo"), n - 1)
                        act.activation(EE[t % 2], HN[:, t, :], ACT.Exp, scale=colp[0:T, cut(COL_S + 4 + L, 1)],
                                       bias=zmx[:, NT + 2:NT + 3]).then_inc(S("exp"), 1)
                    if t >= 1:
                        act.wait_ge(S("em"), n)
                        act.activation(EM[0][:, t - 1, :], EP[(t - 1) % 2], ACT.Copy).then_inc(S("em_hi"), 1)
                    if t < NT:
                        act.wait_ge(S("exp"), n + 1)
                        act.activation(EX[0][:, t, :], EE[t % 2], ACT.Copy).then_inc(S("e_hi"), 1)
                for nme in (f"w1_{L}0", f"w1_{L}1", f"cw_{L}"):
                    split_hi(nme)

                def h_hi(i):
                    act.wait_ge(S("h_tr"), NT * L + i + 1)
                    act.activation(HT[i % 2][0], ps[:, 4, 0:4 * T], ACT.Copy).then_inc(S("ht_hi"), 1)

                h_hi(0)
                for i in range(NT + 2):
                    n = NT * L + i
                    if i + 1 < NT:
                        h_hi(i + 1)
                    if i == 0:
                        split_hi(f"w2_{L}0")
                        split_hi(f"w2_{L}1")
                    if i >= 2:
                        act.wait_ge(S("x_tr"), n - 1)
                        act.activation(XI[0], ps[:, 6, 0:4 * T], ACT.Copy).then_inc(S("xi_hi"), 1)
                    if i < NT:
                        act.wait_ge(S("mlp_nmr"), n + 1)
                        act.activation(YY[i % 2], YY[i % 2], ACT.Identity, bias=mv_m[:, 3:4], scale=mv_m[:, 2:3]).then_inc(S("y_norm"), 1)
                        act.wait_ge(S("y_tr"), n + 1)
                        if n >= 1:
                            act.wait_ge(S("r_lo"), 2 * n)
                        for k in range(KH):
                            last = act.activation(RR[:, cut(k * T, T)], ps[:, 2 + k // 4, cut((k % 4) * T, T)], ACT.Relu,
                                                  bias=colp[:, cut(COL_LB + 8 * L + k, 1)], scale=colp[:, cut(COL_LG + 8 * L + k, 1)])
                            if k % 4 == 3:
                                last.then_inc(S("relu"), 1)
                        if n >= 1:
                            act.wait_ge(S("w2_ps"), n)
                        for h in range(2):
                            act.wait_ge(S("relu"), 2 * n + h + 1)
                            act.activation(RT[0][:, cut(500 * h, 500)], RR[:, cut(500 * h, 500)], ACT.Copy).then_inc(S("r_hi"), 1)
            split_hi("rw")
            tr_hi("fin")
            for nme in ("sg0", "sd0", "sg1", "sd1"):
                split_hi(nme)
            for t in range(NT):
                act.wait_ge(S("log_max"), t + 1)
                act.activation(PRB[:, t, :], LOG[:, t, :], ACT.Exp, bias=rsm[:, 0, cut(t, 1)],
                               accum_out=rsm[:, 1, cut(t, 1)]).then_inc(S("log_exp"), 1)

            def shared_silu(n):
                act.wait_ge(S("gu_ps"), n + 1)
                if n >= 2:
                    act.wait_ge(S("hg"), n - 1)
                act.activation(SIL[n % 2][0:T, :], ps[0:T, 2 + n % 2, 0:F], ACT.Silu).then_inc(S("silu"), 1)

            def shared_hi(n):
                act.wait_ge(S("ht_ps"), n + 1)
                act.activation(ST[0], ps[:, 6, 0:2 * T], ACT.Copy).then_inc(S("s_t_hi"), 1)

            shared_silu(0)
            for n in range(2 * NT):
                shared_hi(n)
                if n + 1 < 2 * NT:
                    shared_silu(n + 1)

            def after(name, value):
                if not isinstance(value, int) or value > 0:
                    act.wait_ge(S(name), value)

            def xe_copy(e, r):
                act.wait_ge(S("xe_ps"), e + 1)
                after("gu_ps", NSH + e - 1)
                act.activation(XE[r % 2], ps[:, r % 2, 0:KD * CAP], ACT.Copy).then_inc(S("xe_sb"), 1)

            def silu(e, r):
                act.wait_ge(S("gu_ps"), NSH + e + 1)
                after("hg", NSH + e - 1)
                act.activation(SIL[r % 2][0:CAP, :], ps[0:CAP, 2 + r % 2, 0:F], ACT.Silu).then_inc(S("silu"), 1)

            def scale(e, col, r):
                act.wait_ge(S("o_ps"), e + 1)
                act.wait_ge(S("row_col"), e + 1)
                act.activation(OS[r], ps[0:CAP, 6 + r % 2, 0:D], ACT.Copy, scale=gat_s[:, col]).then_inc(S("scaled"), 1)

            act.wait_ge(S("tables"), 1)
            xe_copy(0, 0)
            for r in range(UNROLL):
                xe_copy(r + 1, (r + 1) % UNROLL)
                silu(r, r)
                if r >= 1:
                    scale(r - 1, cut(r - 1, 1), r - 1)
            with act.Fori(1, E // UNROLL - 1) as i:
                for r in range(UNROLL):
                    e = UNROLL * i + r
                    xe_copy(e + 1, (r + 1) % UNROLL)
                    silu(e, r)
                    scale(e - 1, bass.ds(e - 1, 1), (r - 1) % UNROLL)
            for r in range(UNROLL):
                e = E - UNROLL + r
                if e + 1 < E:
                    xe_copy(e + 1, (r + 1) % UNROLL)
                silu(e, r)
                scale(e - 1, cut(e - 1, 1), (r - 1) % UNROLL)
            scale(E - 1, cut(E - 1, 1), UNROLL - 1)

        @block.vector
        def _(eng):
            def row_stats(var, rs, norm):
                for t in range(NT):
                    if var == "fin_var":
                        dve.wait_ge(S("cw_add"), NT * (NL - 1) + t + 1)
                    last = dve.bn_stats(stats[:, t, 0, :], XO[:, t, :])
                v1(last)
                for t in range(NT):
                    last = dve.bn_aggr(mv[:, t, :], stats[:, t, 0, :])
                v1(last)
                dve.tensor_scalar(mv[:, :, 1], mv[:, :, 1], 1e-5, None, ALU.add).then_inc(S(var), 1)
                dve.wait_ge(S(rs), 1)
                for t in range(NT):
                    dve.tensor_scalar(XC[:, t, :], XO[:, t, :], mv[:, t, 0:1], rstd[:, cut(t, 1)],
                                      ALU.subtract, ALU.mult).then_inc(S(norm), 1)

            def tr_lo(which):
                for t in range(NT):
                    dve.wait_ge(S(which + "_hi"), t + 1)
                    dve.tensor_tensor(XT[1][:, :, cut(t * T, T)], ps[:, t % 2, 0:KD * T].rearrange("p (k n) -> p k n", k=KD),
                                      f(XT[0][:, :, cut(t * T, T)]), ALU.subtract).then_inc(S(which + "_lo"), 1)

            def message(L, t):
                v1(dve.tensor_scalar(HN[:, t, :], XC[:, t, :], 0.0, 1e-7, ALU.max, ALU.add))
                v1(dve.tensor_scalar(LN2, HN[:, t, :], colp[0:T, cut(COL_S + 4 + L, 1)], -3.0e38, ALU.mult, ALU.max,
                                     accum_out=zmx[:, cut(t, 1)]))
                if t == NT - 1:
                    dve.tensor_reduce(zmx[:, NT:NT + 1], zmx[:, 0:NT], axis=AX.X, op=ALU.max).then_inc(S("zmax"), 1)

            v1(dve.memset(ones_f, 1.0))
            dve.tensor_copy(ones_r[:], ones_f).then_inc(S("vector_consts"), 1)
            dve.wait_ge(S("x_in"), 16)
            row_stats("in_var", "in_rstd", "in_norm")
            split_lo("wv")
            tr_lo("in")
            split_lo("wk")
            dve.wait_ge(S("cols_in"), 16)
            dve.tensor_scalar(gb[:, 0:4], colp[:, COL_BQ:COL_BQ + 4], colp[:, COL_S:COL_S + 1], colp[:, COL_S + 1:COL_S + 2], ALU.mult, ALU.add)
            dve.tensor_scalar(gb[:, 4:8], colp[:, COL_BK:COL_BK + 4], colp[:, COL_S + 2:COL_S + 3], colp[:, COL_S + 3:COL_S + 4],
                              ALU.mult, ALU.add).then_inc(S("gb"), 1)
            dve.wait_ge(S("mixrow_in"), 48)
            for t in range(NT):
                dve.wait_ge(S("v_ps"), t + 1)
                if t >= 2:
                    dve.wait_ge(S("v_lo"), t - 1)
                dve.tensor_tensor(MT[t % 2][0:T, :], ps[0:T, 2 + t % 2, :], BC1[:, 0:D], ALU.add).then_inc(S("v_sb"), 1)
                if t == 1:
                    split_lo("g")

            def proj_lo(u):
                c, h = divmod(u % 8, 2)
                n0, nn = HALVES[h]
                dve.wait_ge(S("kt_hi"), u + 1)
                dve.tensor_tensor(KT[1][:, c, cut(n0, nn)], MT2[u % 2][:, 0:nn], f(KT[0][:, c, cut(n0, nn)]),
                                  ALU.subtract).then_inc(S("kt_lo"), 1)

            for u in range(8):
                proj_lo(u)
                if u == 3:
                    split_lo("wq")

            def pk_mul(t):
                dve.wait_ge(S("pk_a"), t + 1)
                dve.tensor_tensor(by_pair(MT3[t % 2]), phi_k_banks(t)[:, :, 1, :], by_pair(MT[t % 2]), ALU.mult).then_inc(S("pk_ab"), 1)

            pk_mul(0)
            split_lo("wp")
            for t in range(NT):
                if t + 1 < NT:
                    pk_mul(t + 1)
                dve.wait_ge(S("pk_hi"), t + 1)
                dve.tensor_tensor(PK[1][:, t, :], MT[t % 2][0:T, :], f(PK[0][:, t, :]), ALU.subtract).then_inc(S("pk_lo"), 1)
            dve.wait_ge(S("iota"), 2)
            v1(dve.tensor_copy(iota_h, iota_i))
            v1(dve.tensor_copy(gidx[:, 0, :], gidx_i))
            v1(dve.tensor_scalar(gidx[:, 1, :], gidx[:, 0, :], 1.0, None, ALU.add))
            v1(dve.tensor_scalar(gidx[:, 0, :], gidx[:, 0, :], -FAR, None, ALU.add))
            dve.wait_ge(S("edges_in"), 32)
            dve.memset(srcf[:, CH:2 * CH], 0.0)
            for j in range(NT):
                dve.memset(dstrel[:, j, CH:2 * CH], -1.0)
            dve.tensor_copy(srcf[:, 0:CH], srci)
            v1(dve.tensor_copy(dstrel[:, 0, 0:CH], dsti))
            for j in range(1, NT):
                last = dve.tensor_scalar(dstrel[:, j, 0:CH], dstrel[:, 0, 0:CH], float(-T * j), None, ALU.add)
            v1(last)
            for j in range(NT):
                v1(dve.tensor_scalar(ge, dstrel[:, j, 0:CH], 0.0, None, ALU.is_ge))
                v1(dve.scalar_tensor_tensor(out=member[:, cut(j * CH, CH)], in0=dstrel[:, j, 0:CH], scalar=float(T), in1=ge,
                                            op0=ALU.is_lt, op1=ALU.mult))
            dve.sem_inc(S("member"), 1)
            dve.wait_ge(S("kv_hi"), 1)
            for h in range(2):
                last = dve.tensor_tensor(kv_block(KV[1], h), kv_block(kv_bank, h), f(kv_block(KV[0], h)), ALU.subtract)
            last.then_inc(S("kv_lo"), 1)
            for u in range(8, 10):
                proj_lo(u)
            dve.wait_ge(S("member_ps"), 1)
            for j in range(NT):
                b, q = (6, j) if j < 3 else (7, j - 3)
                for v, k in ((los, 0), (his, 1)):
                    last = dve.scalar_tensor_tensor(out=v[:, j, :], in0=ps[0:1, b, cut(q * CH, CH)], scalar=0.5, in1=gidx[:, k, :],
                                                    op0=ALU.is_gt, op1=ALU.mult)
            v1(last)
            dve.tensor_reduce(lohi[:, 0, :], los, axis=AX.X, op=ALU.min)
            v1(dve.tensor_reduce(lohi[:, 1, :], his, axis=AX.X, op=ALU.max))
            v1(dve.tensor_scalar(lohi[:, 0, :], lohi[:, 0, :], FAR, float(CH - 1), ALU.add, ALU.min))
            v1(dve.tensor_tensor(lohi[:, 1, :], lohi[:, 1, :], lohi[:, 0, :], ALU.subtract))
            for j in range(NT):
                last = dve.tensor_scalar(gsteps[:, j, :], gidx[:, 1, 0:NG], float(G), None, ALU.mult)
            v1(last)
            v1(dve.tensor_tensor(gsteps, gsteps, lohi[:, 1, :].unsqueeze(2).to_broadcast([1, NT, NG]), ALU.is_lt))
            v1(dve.tensor_reduce(lohi[:, 1, :], gsteps, axis=AX.X, op=ALU.add))
            v1(dve.tensor_scalar(lohi[:, 1, :], lohi[:, 1, :], 1.0, None, ALU.add))
            dve.tensor_copy(lohi_i[:], lohi[:]).then_inc(S("ranges"), 1)
            dve.wait_ge(S("ranges"), 1)

            for u in range(10, 16):
                proj_lo(u)
                if u < 15:
                    message(0, u - 10)

            def pq_mul(u):
                nn = HALVES[u % 2][1]
                dve.wait_ge(S("pk_a"), PKU + u + 1)
                dve.tensor_tensor(MT3[u % 2][:, 0:nn], ps[:, 6 + u % 2, 0:nn], MT[u % 2][:, 0:nn], ALU.mult).then_inc(S("pk_ab"), 1)

            pq_mul(0)
            for u in range(8):
                c, h = divmod(u, 2)
                n0, nn = HALVES[h]
                if u + 1 < 8:
                    pq_mul(u + 1)
                dve.wait_ge(S("pk_hi"), PKU + u + 1)
                dve.tensor_tensor(PQ[1][:, c, cut(n0, nn)], MT[u % 2][:, 0:nn], f(PQ[0][:, c, cut(n0, nn)]),
                                  ALU.subtract).then_inc(S("pk_lo"), 1)
            def mix_add(t):
                dve.wait_ge(S("mix_out_ps"), t + 1)
                dve.wait_ge(S("x_rows"), t + 1)
                dve.tensor_tensor(XO[:, t, :], XO[:, t, :], ps[0:T, 2 + t % 2, :], ALU.add).then_inc(S("mix_out_add"), 1)

            for t in range(NT + 1):
                if t < NT:
                    dve.wait_ge(S("attn_ps"), t + 1)
                    dens = attn_banks(t)[:, :, 1, :].rearrange("p c (h n) -> p c h n", h=2)
                    nums = attn_banks(t)[:, :, 0, :].rearrange("p c (h n) -> p c h n", h=2)
                    den = rden[:].rearrange("p (c h) -> p c h", c=KD)
                    v1(dve.tensor_scalar(den, dens[:, :, :, 0], 1e-6, None, ALU.add))
                    v1(dve.reciprocal(rden[:], rden[:]))
                    if t >= 2:
                        dve.wait_ge(S("attn_tr"), t - 1)
                    v1(dve.tensor_tensor(MT3[t % 2][0:T, :].rearrange("p (c h n) -> p c h n", c=KD, h=2), nums,
                                         den.unsqueeze(3).to_broadcast([T, KD, 2, 64]), ALU.mult))
                    dve.sem_inc(S("attn"), 1)
                if t >= 1:
                    dve.wait_ge(S("attn_hi"), t)
                    dve.tensor_tensor(OT[1][:, :, cut((t - 1) * T, T)], ps[:, (t - 1) % 2, 0:KD * T].rearrange("p (k n) -> p k n", k=KD),
                                      f(OT[0][:, :, cut((t - 1) * T, T)]), ALU.subtract).then_inc(S("attn_lo"), 1)
                if t >= 2:
                    mix_add(t - 2)
            mix_add(NT - 1)

            dve.memset(zero_b, 0.0).then_inc(S("vector_consts"), 1)
            def adj_low(j):
                dve.wait_ge(S("adj_hi"), j + 1)
                dve.tensor_tensor(AT_lo[:, 0:3, cut(j * T, T)], ps[0:T, 4, 0:3 * T].rearrange("p (s n) -> p s n", s=3),
                                  f(AT_hi[:, 0:3, cut(j * T, T)]), ALU.subtract)
                dve.tensor_tensor(AT_lo[:, 3:5, cut(j * T, T)], ps[0:T, 5, 0:2 * T].rearrange("p (s n) -> p s n", s=2),
                                  f(AT_hi[:, 3:5, cut(j * T, T)]), ALU.subtract).then_inc(S("adj_lo"), 1)

            for j in range(NT):
                lo = dve.value_load(lohi_i[0:1, 0, j:j + 1], min_val=0, max_val=CH - 1)
                steps = dve.value_load(lohi_i[0:1, 1, j:j + 1], min_val=1, max_val=NG)
                with dve.Fori(0, steps) as q:
                    for i in range(G):
                        dve.wait_ge(S(f"one_hot_free{j}"), q * G + i + 1)
                        dve.tensor_scalar(one_hot_src[:, i, :], iota_h, srcf[:, bass.ds(lo + q * G + i, 1)], None, ALU.is_equal)
                        dve.tensor_scalar(one_hot_dst[:, i, :], iota_h[:, 0:T + 1], dstrel[:, j, bass.ds(lo + q * G + i, 1)], None,
                                          ALU.is_equal).then_inc(S(f"one_hot{j}"), 1)
                if j >= 2:
                    adj_low(j - 2)
            adj_low(NT - 2)
            adj_low(NT - 1)

            for L in range(NL):
                dve.wait_ge(S("zmax_all"), L + 1)
                dve.tensor_scalar(zmx[:, NT + 2:NT + 3], zmx[:, NT + 1:NT + 2], -1.0, None, ALU.mult).then_inc(S("zmax_neg"), 1)
                for t in range(NT + 1):
                    n = NT * L + t
                    if t < NT:
                        dve.wait_ge(S("exp"), n + 1)
                        if t >= 2:
                            dve.wait_ge(S("em_lo"), n - 1)
                        dve.tensor_tensor(EP[t % 2], EE[t % 2], HN[:, t, :], ALU.mult).then_inc(S("em"), 1)
                    if t >= 1:
                        dve.wait_ge(S("em_hi"), n)
                        dve.tensor_tensor(EM[1][:, t - 1, :], EP[(t - 1) % 2], f(EM[0][:, t - 1, :]), ALU.subtract).then_inc(S("em_lo"), 1)
                    if t < NT:
                        dve.wait_ge(S("e_hi"), n + 1)
                        dve.tensor_tensor(EX[1][:, t, :], EE[t % 2], f(EX[0][:, t, :]), ALU.subtract).then_inc(S("e_lo"), 1)
                for d in range(NT):
                    n = NT * L + d
                    dve.wait_ge(S("agg_ps"), n + 1)
                    v1(dve.tensor_scalar(LN, ps[0:T, 2 * (d % 2), :], 1e-30, None, ALU.max))
                    v1(dve.reciprocal(LN, LN))
                    v1(dve.tensor_tensor(LN2, ps[0:T, 2 * (d % 2) + 1, :], LN, ALU.mult))
                    dve.tensor_tensor(HN[:, d, :], LN2, XC[:, d, :], ALU.add).then_inc(S("h"), 1)
                    if d < 3:
                        split_lo((f"w1_{L}0", f"w1_{L}1", f"cw_{L}")[d])

                def h_lo(i):
                    dve.wait_ge(S("ht_hi"), NT * L + i + 1)
                    dve.tensor_tensor(HT[i % 2][1], ps[:, 4, 0:4 * T], f(HT[i % 2][0]), ALU.subtract).then_inc(S("ht_lo"), 1)

                h_lo(0)
                dve.wait_ge(S("rows_in"), 32 + 64 * L)
                for i in range(NT + 2):
                    n = NT * L + i
                    if i + 1 < NT:
                        h_lo(i + 1)
                    if i < NT:
                        dve.wait_ge(S("w1_ps"), n + 1)
                        if n >= 2:
                            dve.wait_ge(S("y_tr"), n - 1)
                        v1(dve.tensor_tensor(YY[i % 2].rearrange("p (a b) -> p a b", a=2), ps[0:T, 0:2, :],
                                             BC1.rearrange("p (a b) -> p a b", a=2), ALU.add))
                        dve.sem_inc(S("y_sb"), 1)
                        dve.bn_stats(st_m[:, 0, :], YY[i % 2][:, 0:D])
                        v1(dve.bn_stats(st_m[:, 1, :], YY[i % 2][:, D:H]))
                        if n >= 1:
                            dve.wait_ge(S("y_norm"), n)
                        v1(dve.bn_aggr(mv_m[:, 0:2], st_m[:].rearrange("p a b -> p (a b)")))
                        dve.tensor_scalar(mv_m[:, 1:2], mv_m[:, 1:2], 1e-5, None, ALU.add).then_inc(S("mlp_var"), 1)
                    if i == 0:
                        split_lo(f"w2_{L}0")
                        split_lo(f"w2_{L}1")
                    if i >= 2:
                        dve.wait_ge(S("xi_hi"), n - 1)
                        dve.tensor_tensor(XI[1], ps[:, 6, 0:4 * T], f(XI[0]), ALU.subtract).then_inc(S("xi_lo"), 1)
                    if i < NT:
                        dve.wait_ge(S("mlp_rstd"), n + 1)
                        dve.scalar_tensor_tensor(out=mv_m[:, 3:4], in0=mv_m[:, 0:1], scalar=-1.0, in1=mv_m[:, 2:3],
                                                 op0=ALU.mult, op1=ALU.mult).then_inc(S("mlp_nmr"), 1)
                    if 1 <= i <= NT:
                        t = i - 1
                        dve.wait_ge(S("w2_ps"), n)
                        if L == 0:
                            v1(dve.tensor_tensor(XC[:, t, :], ps[0:T, 5, :], BC2, ALU.add))
                            dve.sem_inc(S("w2_sb"), 1)
                            dve.sem_inc(S("x_next"), 1)
                        else:
                            m = NT * (L - 1) + t + 1
                            v1(dve.tensor_tensor(LN, ps[0:T, 5, :], BC2, ALU.add))
                            dve.sem_inc(S("w2_sb"), 1)
                            v1(dve.bn_stats(st_o[:, 0, :], LN))
                            v1(dve.bn_aggr(mv_o[:, 0:2], st_o[:, 0, :]))
                            dve.tensor_scalar(mv_o[:, 1:2], mv_o[:, 1:2], 1e-5, None, ALU.add).then_inc(S("out_var"), 1)
                            dve.wait_ge(S("out_rstd"), m)
                            v1(dve.scalar_tensor_tensor(out=LN, in0=LN, scalar=mv_o[:, 0:1], in1=BCG, op0=ALU.subtract, op1=ALU.mult))
                            v1(dve.scalar_tensor_tensor(out=LN2, in0=LN, scalar=mv_o[:, 2:3], in1=BCB, op0=ALU.mult, op1=ALU.add))
                            v1(dve.scalar_tensor_tensor(out=XC[:, t, :], in0=LN2, scalar=0.0, in1=XC[:, t, :], op0=ALU.max, op1=ALU.add))
                            dve.sem_inc(S("x_next"), 1)
                        if L + 1 < NL:
                            message(L + 1, t)
                    if i >= 2:
                        dve.wait_ge(S("cw_ps"), n - 1)
                        dve.tensor_tensor(XO[:, i - 2, :], XO[:, i - 2, :], ps[0:T, 7, :], ALU.add).then_inc(S("cw_add"), 1)
                    if i < NT:
                        for h in range(2):
                            dve.wait_ge(S("r_hi"), 2 * n + h + 1)
                            dve.tensor_tensor(RT[1][:, cut(500 * h, 500)], RR[:, cut(500 * h, 500)], f(RT[0][:, cut(500 * h, 500)]),
                                              ALU.subtract).then_inc(S("r_lo"), 1)

            row_stats("fin_var", "fin_rstd", "fin_norm")
            split_lo("rw")
            tr_lo("fin")
            for nme in ("sg0", "sd0", "sg1", "sd1"):
                split_lo(nme)
            dve.wait_ge(S("rbias_in"), 16)
            for t in range(NT):
                dve.wait_ge(S("router_ps"), t + 1)
                v1(dve.tensor_tensor(LOG[:, t, :], ps[0:T, 2 + t % 2, 0:E], RBC, ALU.add))
                dve.sem_inc(S("log_sb"), 1)
                v1(dve.tensor_reduce(rsm[:, 0, cut(t, 1)], LOG[:, t, :], axis=AX.X, op=ALU.max))
                dve.tensor_scalar(rsm[:, 0, cut(t, 1)], rsm[:, 0, cut(t, 1)], -1.0, None, ALU.mult).then_inc(S("log_max"), 1)
            dve.wait_ge(S("log_exp"), NT)
            v1(dve.reciprocal(rsm[:, 2, :], rsm[:, 1, :]))
            for t in range(NT):
                last = dve.tensor_scalar(PRB[:, t, :], PRB[:, t, :], rsm[:, 2, cut(t, 1)], None, ALU.mult)
            v1(last)
            for t in range(NT):
                last = dve.max(r8[:, t, :], PRB[:, t, :])
            v1(last)
            v1(dve.tensor_reduce(rsm[:, 3, :], r8[:, :, 0:TOPK], axis=AX.X, op=ALU.add))
            v1(dve.tensor_scalar(rsm[:, 3, :], rsm[:, 3, :], 1e-9, None, ALU.add))
            v1(dve.reciprocal(rsm[:, 3, :], rsm[:, 3, :]))
            v1(dve.memset(r8[:, :, TOPK:8], -5.0))
            for t in range(NT):
                last = dve.match_replace(MSK[:, t, :], r8[:, t, :], PRB[:, t, :], -1.0)
            v1(last)
            v1(dve.tensor_scalar(MSK, MSK, -1.0, None, ALU.is_equal))
            dve.tensor_copy(MSKB, MSK).then_inc(S("mask"), 1)
            for t in range(NT):
                last = dve.scalar_tensor_tensor(out=GAT[:, t, :], in0=PRB[:, t, :], scalar=rsm[:, 3, cut(t, 1)], in1=MSK[:, t, :],
                                                op0=ALU.mult, op1=ALU.mult)
            v1(last)
            v1(dve.memset(GR[:, 2, 0:E], 1.0))
            for t in range(NT):
                last = dve.tensor_tensor_scan(KRK[:, t, :], GR[:, 2, 0:E], MSK[:, t, :], 0.0, ALU.mult, ALU.add)
            v1(last)
            v1(dve.tensor_tensor(KRK, KRK, MSK, ALU.subtract))
            dve.wait_ge(S("iota"), 3)
            v1(dve.tensor_copy(pnum, pnum_i))
            v1(dve.tensor_copy(iota_s[:], snum_i))
            dve.tensor_scalar(MTAB[:, :, :, 0], MSK, 0.0, pnum, ALU.mult, ALU.add)
            for t in range(NT):
                dve.memset(MTAB[:, t, :, 1], float(t))
            dve.tensor_copy(MTAB[:, :, :, 2], KRK)
            dve.memset(MTAB[:, :, :, 3], 1.0)
            v1(dve.tensor_copy(MTAB[:, :, :, 4], GAT))
            g0, gr = [GR[:, i, :].rearrange("p (t e) -> p t e", t=NT) for i in range(2)]
            v1(dve.tensor_tensor(g0, GAT, MTAB[:, :, :, 4], ALU.subtract))
            v1(dve.tensor_copy(MTAB[:, :, :, 5], g0))
            v1(dve.tensor_tensor(gr, g0, MTAB[:, :, :, 5], ALU.subtract))
            v1(dve.tensor_copy(MTAB[:, :, :, 6], gr))
            dve.wait_ge(S("pos_ps"), 1)
            v1(dve.tensor_copy(POS, ps[0:T, 4, 0:NT * E].rearrange("p (t e) -> p t e", t=NT)))
            v1(dve.scalar_tensor_tensor(out=LOG, in0=POS, scalar=float(CAP), in1=MSK, op0=ALU.is_lt, op1=ALU.mult))
            v1(dve.scalar_tensor_tensor(out=POS, in0=POS, scalar=-FAR, in1=LOG, op0=ALU.add, op1=ALU.mult))
            v1(dve.tensor_scalar(POSB, POS, FAR, None, ALU.add))

            def select(e, n, r):
                if not isinstance(n, int) or n >= UNROLL:
                    dve.wait_ge(S("sel_used"), n - 3)
                dve.tensor_tensor(SELT[r], iota_s[:, 0:CAP].unsqueeze(1).to_broadcast([T, NT, CAP]),
                                  POSB[:, :, e].to_broadcast([T, NT, CAP]), ALU.is_equal).then_inc(S("sel"), 1)

            def shared_add(t):
                dve.wait_ge(S("shared_ps"), t + 1)
                dve.scalar_tensor_tensor(out=XO[:, t, :], in0=ps[0:T, 7, :], scalar=0.5, in1=XO[:, t, :],
                                         op0=ALU.mult, op1=ALU.add).then_inc(S("shared_add"), 1)

            def shared_lo(n):
                dve.wait_ge(S("s_t_hi"), n + 1)
                dve.tensor_tensor(ST[1], ps[:, 6, 0:2 * T], f(ST[0]), ALU.subtract).then_inc(S("s_t_lo"), 1)

            for n in range(2 * NT):
                for q in range(2):
                    for r in range(UNROLL):
                        e = 2 * UNROLL * n + UNROLL * q + r
                        if e < E:
                            select(cut(e, 1), e, r)
                    if q == 0 and n >= 1:
                        shared_lo(n - 1)
                        if n % 2 == 0:
                            shared_add(n // 2 - 1)
                dve.wait_ge(S("silu"), n + 1)
                dve.tensor_tensor(HG[n % 2][0:T, :], ps[0:T, 2 + n % 2, F:2 * F], SIL[n % 2][0:T, :], ALU.mult).then_inc(S("hg"), 1)
            shared_lo(2 * NT - 1)
            shared_add(NT - 1)
            dve.wait_ge(S("sel_used"), E)
            v1(dve.tensor_copy(TAB, ps[0:CAP, 5, 0:7 * E].rearrange("p (e c) -> p e c", c=7)))
            v1(dve.tensor_tensor(gat_s[:], TAB[:, :, 4], TAB[:, :, 5], ALU.add))
            v1(dve.tensor_tensor(gat_s[:], gat_s[:], TAB[:, :, 6], ALU.add))
            v1(dve.scalar_tensor_tensor(out=tokf[:, 0, :], in0=TAB[:, :, 1], scalar=float(T), in1=TAB[:, :, 0], op0=ALU.mult, op1=ALU.add))
            v1(dve.scalar_tensor_tensor(out=tokf[:, 1, :], in0=tokf[:, 0, :], scalar=float(TOPK), in1=TAB[:, :, 2], op0=ALU.mult, op1=ALU.add))
            v1(dve.tensor_scalar(TAB[:, :, 3], TAB[:, :, 3], -SKIP, SKIP, ALU.mult, ALU.add))
            v1(dve.tensor_tensor(tokf[:, 0, :], tokf[:, 0, :], TAB[:, :, 3], ALU.add))
            v1(dve.tensor_tensor(tokf[:, 1, :], tokf[:, 1, :], TAB[:, :, 3], ALU.add))
            v1(dve.tensor_copy(tok_i[:], tokf[:, 0, :]))
            dve.tensor_copy(tok_c[:], tok_i[:, 0:UNROLL]).then_inc(S("tok_col"), UNROLL)
            dve.tensor_copy(row_i[:], tokf[:, 1, :]).then_inc(S("tables"), 1)


            def after(name, value):
                if not isinstance(value, int) or value > 0:
                    dve.wait_ge(S(name), value)

            def gated(e, col, ahead, r, turn):
                dve.wait_ge(S("silu"), NSH + e + 1)
                if ahead is not None:
                    dve.tensor_copy(tok_c[:, cut(r, 1)], tok_i[:, ahead]).then_inc(S("tok_col"), 1)
                dve.wait_ge(S("ht_ps"), NSH + e - 1)
                dve.tensor_tensor(HG[r % 2][0:CAP, :], ps[0:CAP, 2 + r % 2, F:2 * F], SIL[r % 2][0:CAP, :], ALU.mult).then_inc(S("hg"), 1)
                after(f"y_out{r}", 16 * turn)
                dve.tensor_copy(row_c[:, cut(r, 1)], row_i[:, col]).then_inc(S("row_col"), 1)
                dve.wait_ge(S("ht_ps"), NSH + e + 1)
                after("o_ps", e - 1)
                dve.tensor_copy(HTF[r % 2], ps[:, 4 + r % 2, 0:2 * CAP]).then_inc(S("ht_sb"), 1)

            for r in range(UNROLL):
                gated(r, cut(r, 1), cut(r + UNROLL, 1), r, 0)
            with dve.Fori(1, E // UNROLL - 1) as i:
                for r in range(UNROLL):
                    e = UNROLL * i + r
                    gated(e, bass.ds(e, 1), bass.ds(e + UNROLL, 1), r, i)
            for r in range(UNROLL):
                e = E - UNROLL + r
                gated(e, cut(e, 1), None, r, E // UNROLL - 1)
            for t in range(NT):
                dve.wait_ge(S(f"y_in{t}"), 16)
                if t >= 1:
                    dve.wait_ge(S("y_sum"), t)
                v1(dve.tensor_reduce(ysum, YL[t].rearrange("p a n -> p n a"), axis=AX.X, op=ALU.add))
                dve.tensor_tensor(XO[:, t, :], XO[:, t, :], ysum, ALU.add).then_inc(S("y_sum"), 1)

        @block.tensor
        def _(eng):
            def tr_x(norm, which):
                for t in range(NT):
                    pe.wait_ge(S(norm), t + 1)
                    if t >= 2:
                        pe.wait_ge(S(which + "_lo"), t - 1)
                    for k in range(KD):
                        last = pe.transpose(ps[:, t % 2, cut(k * T, T)], XC[:, t, cut(k * P, P)], ident[0:T, 0:T])
                    last.then_inc(S(which + "_tr"), 1)

            pe.wait_ge(S("pool_consts"), 1)
            tr_x("in_norm", "in")
            weights("wv")
            for t in range(NT):
                pe.wait_ge(S("in_lo"), t + 1)
                if t >= 2:
                    pe.wait_ge(S("v_sb"), t - 1)
                for k in range(KD):
                    last = mm3(ps[0:T, 2 + t % 2, :], sub(XT, A_, k, cut(t * T, T)), sub(WMA, A_, k, A_), k == 0, k == KD - 1)
                last.then_inc(S("v_ps"), 1)

            def proj(u, w):
                c, h = divmod(u % 8, 2)
                n0, nn = HALVES[h]
                if u >= 2:
                    pe.wait_ge(S("kt_sb"), u - 1)
                for k in range(KD):
                    last = mm3(ps[:, 4 + u % 2, 0:nn], sub(w, A_, k, cut(c * P, P)), sub(XT, A_, k, cut(n0, nn)), k == 0, k == KD - 1)
                last.then_inc(S("kt_ps"), 1)

            weights("wk")
            pe.wait_ge(S("pool_consts"), 2)
            for u in range(8):
                proj(u, WMB)
            weights("g")
            pe.wait_ge(S("kt_lo"), 8)
            for t in range(NT):
                if t >= 2:
                    pe.wait_ge(S("pk_ab"), t - 1)
                for c in range(KD):
                    last = mm3(phi_k_banks(t)[:, c, :, :].rearrange("p a n -> p (a n)"), sub(KT, A_, c, cut(t * T, T)),
                               (GM[0][:, 2:4, :], GM[1][:, 2:4, :]), True, True)
                last.then_inc(S("pk_ps"), 1)
            weights("wq")
            for u in range(8, 16):
                if u == 10:
                    pe.wait_ge(S("pk_lo"), NT)
                    pe.wait_ge(S("v_lo"), NT)
                    pe.wait_ge(S("vector_consts"), 1)
                    for c in range(KD):
                        b, o = c // 2, 256 * (c % 2)
                        for t in range(NT):
                            mm3(ps[:, b, cut(o, P)], sub(PK, A_, t, cut(c * P, P)), sub(VV, A_, t, cut(c * P, P)), t == 0, t == NT - 1)
                        for t in range(NT):
                            for part in range(2):
                                last = pe.matmul(ps[:, b, cut(o + P, P)], PK[part][:, t, cut(c * P, P)], ones_r[:],
                                                 start=(t == 0 and part == 0), stop=(t == NT - 1 and part == 1))
                    last.then_inc(S("kv_ps"), 1)
                    pe.wait_ge(S("member"), 1)
                    pe.wait_ge(S("pool_consts"), 3)
                    for j in range(NT):
                        b, q = (6, j) if j < 3 else (7, j - 3)
                        last = pe.matmul(ps[0:1, b, cut(q * CH, CH)], ones_b[:, 0:1], member[:, cut(j * CH, CH)], start=True, stop=True)
                    last.then_inc(S("member_ps"), 1)
                proj(u, WMA)
            pe.wait_ge(S("kt_lo"), 16)
            pe.wait_ge(S("ranges"), 1)
            for u in range(8):
                c, h = divmod(u, 2)
                n0, nn = HALVES[h]
                if u >= 2:
                    pe.wait_ge(S("pk_ab"), PKU + u - 1)
                mm3(ps[:, 2 + u % 2, 0:nn], sub(GM, A_, 0, A_), sub(QT, A_, c, cut(n0, nn)), True, True)
                mm3(ps[:, 6 + u % 2, 0:nn], sub(GM, A_, 1, A_), sub(QT, A_, c, cut(n0, nn)), True, True).then_inc(S("pk_ps"), 1)
            pe.wait_ge(S("kv_lo"), 1)
            pe.wait_ge(S("pk_ab"), PKU + 8)
            pe.wait_ge(S("pk_lo"), PKU + 8)
            pe.wait_ge(S("kt_sb"), 16)
            weights("wp")

            def attend(t):
                if t >= 2:
                    pe.wait_ge(S("attn"), t - 1)
                for c in range(KD):
                    last = mm3(attn_banks(t)[:, c, :, :].rearrange("p a n -> p (a n)"), sub(PQ, A_, c, cut(t * T, T)),
                               sub(KV, A_, c, A_), True, True)
                last.then_inc(S("attn_ps"), 1)

            def attn_transpose(t):
                pe.wait_ge(S("attn"), t + 1)
                if t >= 2:
                    pe.wait_ge(S("attn_lo"), t - 1)
                for k in range(KD):
                    last = pe.transpose(ps[:, t % 2, cut(k * T, T)], MT3[t % 2][0:T, cut(k * P, P)], ident[0:T, 0:T])
                last.then_inc(S("attn_tr"), 1)

            def mix_out(t):
                pe.wait_ge(S("attn_lo"), t + 1)
                if t >= 2:
                    pe.wait_ge(S("mix_out_add"), t - 1)
                for k in range(KD):
                    last = mm3(ps[0:T, 2 + t % 2, :], sub(OT, A_, k, cut(t * T, T)), sub(WMB, A_, k, A_), k == 0, k == KD - 1)
                last.then_inc(S("mix_out_ps"), 1)

            attend(0)
            for t in range(NT + 1):
                if t + 1 < NT:
                    attend(t + 1)
                if t < NT:
                    attn_transpose(t)
                if t >= 1:
                    mix_out(t - 1)

            pe.wait_ge(S("mix_out_add"), NT)
            pe.wait_ge(S("vector_consts"), 2)
            parts = [(0, 0, 313), (1, 313, 312)]

            def adj_transpose(j):
                pe.wait_ge(S("adj_sb"), j + 1)
                if j >= 1:
                    pe.wait_ge(S("adj_lo"), j)
                for s in range(NT):
                    b, q = (4, s) if s < 3 else (5, s - 3)
                    last = pe.transpose(ps[0:T, b, cut(q * T, T)], adj[:, j % 2, cut(s * T, T)], ident[0:T, 0:T])
                last.then_inc(S("adj_tr"), 1)

            for j in range(NT):
                steps = pe.value_load(lohi_i[0:1, 1, j:j + 1], min_val=1, max_val=NG)
                if j >= 2:
                    pe.wait_ge(S("adj_sb"), j - 1)
                for h, s0, sn in parts:
                    last = pe.matmul(ps[0:T, 2 * (j % 2) + h, 0:sn], zero_b[:, 0:T], zero_b[:, 0:sn], start=True, stop=False)
                last.then_inc(S(f"one_hot_free{j}"), G)
                with pe.Fori(0, steps) as q:
                    for i in range(G):
                        pe.wait_ge(S(f"one_hot{j}"), q * G + i + 1)
                        for h, s0, sn in parts:
                            last = pe.matmul(ps[0:T, 2 * (j % 2) + h, 0:sn], one_hot_dst[:, i, 0:T], one_hot_src[:, i, cut(s0, sn)],
                                             start=False, stop=False)
                        last.then_inc(S(f"one_hot_free{j}"), 1)
                for h, s0, sn in parts:
                    last = pe.matmul(ps[0:T, 2 * (j % 2) + h, 0:sn], zero_b[:, 0:T], zero_b[:, 0:sn], start=False, stop=True)
                last.then_inc(S("adj_ps"), 1)
                if j >= 1:
                    adj_transpose(j - 1)
            adj_transpose(NT - 1)

            pe.wait_ge(S("adj_lo"), NT)
            for L in range(NL):
                def aggregate(d, s):
                    b = 2 * (d % 2)
                    a = (AT_hi[:, s, cut(d * T, T)], AT_lo[:, s, cut(d * T, T)])
                    mm3(ps[0:T, b, :], a, sub(EX, A_, s, A_), s == 0, s == NT - 1)
                    last = mm3(ps[0:T, b + 1, :], a, sub(EM, A_, s, A_), s == 0, s == NT - 1)
                    if s == NT - 1:
                        last.then_inc(S("agg_ps"), 1)

                if L:
                    pe.wait_ge(S("relu"), 2 * NT * L)
                for s in range(NT):
                    pe.wait_ge(S("e_lo"), NT * L + s + 1)
                    pe.wait_ge(S("em_lo"), NT * L + s + 1)
                    for d in range(2):
                        aggregate(d, s)
                for d in range(2, NT):
                    pe.wait_ge(S("h"), NT * L + d - 1)
                    for s in range(NT):
                        aggregate(d, s)

                def h_tr(i):
                    n = NT * L + i
                    pe.wait_ge(S("h"), n + 1)
                    if n >= 1:
                        pe.wait_ge(S("ht_lo"), n)
                    for k in range(KD):
                        last = pe.transpose(ps[:, 4, cut(k * T, T)], HN[:, i, cut(k * P, P)], ident[0:T, 0:T])
                    last.then_inc(S("h_tr"), 1)

                h_tr(0)
                weights(f"w1_{L}1")
                for i in range(NT + 2):
                    n = NT * L + i
                    if i + 1 < NT:
                        h_tr(i + 1)
                    if i == 0:
                        pe.wait_ge(S("h"), NT * (L + 1))
                    if i < NT:
                        pe.wait_ge(S("ht_lo"), n + 1)
                        if i:
                            pe.wait_ge(S("y_sb"), n)
                        for b in range(2):
                            for k in range(KD):
                                last = mm3(ps[0:T, b, :], sub(HT[i % 2], A_, cut(k * T, T)), sub(W1, A_, k, cut(b * D, D)), k == 0, k == KD - 1)
                        last.then_inc(S("w1_ps"), 1)
                    if i >= 2:
                        m = n - 2
                        pe.wait_ge(S("x_next"), m + 1)
                        if m >= 1:
                            pe.wait_ge(S("xi_lo"), m)
                        for k in range(KD):
                            last = pe.transpose(ps[:, 6, cut(k * T, T)], XC[:, i - 2, cut(k * P, P)], ident[0:T, 0:T])
                        last.then_inc(S("x_tr"), 1)
                    if 1 <= i <= NT:
                        m = n - 1
                        if i == 1:
                            weights(f"w2_{L}1")
                        pe.wait_ge(S("r_lo"), 2 * (m + 1))
                        if m >= 1:
                            pe.wait_ge(S("w2_sb"), m)
                        for k in range(KH):
                            last = mm3(ps[0:T, 5, :], sub(RT, A_, cut(k * T, T)), sub(W2, A_, k, A_), k == 0, k == KH - 1)
                        last.then_inc(S("w2_ps"), 1)
                    if i >= 2:
                        m = n - 2
                        if i == 2:
                            weights(f"cw_{L}")
                        pe.wait_ge(S("xi_lo"), m + 1)
                        if m >= 1:
                            pe.wait_ge(S("cw_add"), m)
                        for k in range(KD):
                            last = mm3(ps[0:T, 7, :], sub(XI, A_, cut(k * T, T)), sub(CW, A_, k, A_), k == 0, k == KD - 1)
                        last.then_inc(S("cw_ps"), 1)
                    if i < NT:
                        pe.wait_ge(S("y_norm"), n + 1)
                        if n >= 1:
                            pe.wait_ge(S("relu"), 2 * n)
                        for k in range(KH):
                            last = pe.transpose(ps[:, 2 + k // 4, cut((k % 4) * T, T)], YY[i % 2][:, cut(k * P, P)], ident[0:T, 0:T])
                        last.then_inc(S("y_tr"), 1)

            tr_x("fin_norm", "fin")
            weights("rw")
            for t in range(NT):
                pe.wait_ge(S("fin_lo"), t + 1)
                if t >= 2:
                    pe.wait_ge(S("log_sb"), t - 1)
                for k in range(KD):
                    last = mm3(ps[0:T, 2 + t % 2, 0:E], sub(XT, A_, k, cut(t * T, T)), sub(RW, A_, k, A_), k == 0, k == KD - 1)
                last.then_inc(S("router_ps"), 1)
            pe.wait_ge(S("mask"), 1)
            for t in range(NT):
                for q in range(t):
                    pe.matmul(ps[0:T, 4, cut(t * E, E)], ones_b[:, 0:T], MSKB[:, q, :], start=(q == 0), stop=False)
                last = pe.matmul(ps[0:T, 4, cut(t * E, E)], tri[:], MSKB[:, t, :], start=(t == 0), stop=True)
            last.then_inc(S("pos_ps"), 1)
            def table(e):
                pe.wait_ge(S("sel"), e + 1)
                for t in range(NT):
                    last = pe.matmul(ps[0:CAP, 5, cut(7 * e, 7)], SELT[e % UNROLL][:, t, :], MTAB[:, t, e, 0:7], start=(t == 0), stop=(t == NT - 1))
                last.then_inc(S("sel_used"), 1)

            weights("sd1")
            pe.wait_ge(S("log_sb"), NT)

            def shared_down(n):
                t, s = divmod(n, 2)
                pe.wait_ge(S("s_t_lo"), n + 1)
                if s == 0 and t >= 1:
                    pe.wait_ge(S("shared_add"), t)
                for k in range(2):
                    last = mm3(ps[0:T, 7, :], sub(ST, A_, cut(k * T, T)), sub(SD[s], A_, k, A_), s == 0 and k == 0, s == 1 and k == 1)
                if s == 1:
                    last.then_inc(S("shared_ps"), 1)

            for n in range(2 * NT):
                t, s = divmod(n, 2)
                if n >= 2:
                    pe.wait_ge(S("hg"), n - 1)
                for k in range(KD):
                    last = mm3(ps[0:T, 2 + n % 2, :], sub(XT, A_, k, cut(t * T, T)), sub(SG[s], A_, k, A_), k == 0, k == KD - 1)
                last.then_inc(S("gu_ps"), 1)
                if n >= 1:
                    shared_down(n - 1)
                for e in range(2 * UNROLL * n, min(2 * UNROLL * (n + 1), E)):
                    table(e)
                pe.wait_ge(S("hg"), n + 1)
                for k in range(2):
                    last = pe.transpose(ps[:, 6, cut(k * T, T)], HG[n % 2][0:T, cut(k * P, P)], ident[0:T, 0:T])
                last.then_inc(S("ht_ps"), 1)
            shared_down(2 * NT - 1)

            def after(name, value):
                if not isinstance(value, int) or value > 0:
                    pe.wait_ge(S(name), value)

            def transpose_x(e, r, turn):
                pe.wait_ge(S(f"xg_in{r}"), 16 * turn + 16)
                after("xe_sb", e - 1)
                for k in range(KD):
                    last = pe.transpose(ps[:, r % 2, cut(k * CAP, CAP)], XG[r][:, cut(k * P, P)], ident[0:CAP, 0:CAP])
                last.then_inc(S("xe_ps"), 1)

            def gate_up(e, r, turn):
                pe.wait_ge(S(f"ring_in{r}"), 16 * turn + 16)
                pe.wait_ge(S("xe_sb"), e + 1)
                after("hg", NSH + e - 1)
                for k in range(KD):
                    last = pe.matmul(ps[0:CAP, 2 + r % 2, :], XE[r % 2][:, cut(k * CAP, CAP)], RING[r][:, cut(512 * k, 512)],
                                     start=(k == 0), stop=(k == KD - 1))
                last.then_inc(S("gu_ps"), 1)

            def down(e, r):
                pe.wait_ge(S("ht_sb"), e + 1)
                after("scaled", e - 1)
                for k in range(2):
                    last = pe.matmul(ps[0:CAP, 6 + r % 2, :], HTF[r % 2][:, cut(k * CAP, CAP)], RING[r][:, cut(2048 + 512 * k, 512)],
                                     start=(k == 0), stop=(k == 1))
                last.then_inc(S("o_ps"), 1)

            def transpose_h(e, r):
                pe.wait_ge(S("hg"), NSH + e + 1)
                after("ht_sb", e - 1)
                for k in range(2):
                    last = pe.transpose(ps[:, 4 + r % 2, cut(k * CAP, CAP)], HG[r % 2][0:CAP, cut(k * P, P)], ident[0:CAP, 0:CAP])
                last.then_inc(S("ht_ps"), 1)

            pe.wait_ge(S("shared_add"), NT)
            transpose_x(0, 0, 0)
            for r in range(UNROLL):
                transpose_x(r + 1, (r + 1) % UNROLL, (r + 1) // UNROLL)
                gate_up(r, r, 0)
                if r >= 1:
                    down(r - 1, r - 1)
                transpose_h(r, r)
            with pe.Fori(1, E // UNROLL - 1) as i:
                for r in range(UNROLL):
                    e = UNROLL * i + r
                    transpose_x(e + 1, (r + 1) % UNROLL, i + 1 if r == UNROLL - 1 else i)
                    gate_up(e, r, i)
                    down(e - 1, (r - 1) % UNROLL)
                    transpose_h(e, r)
            turn = E // UNROLL - 1
            for r in range(UNROLL):
                e = E - UNROLL + r
                if e + 1 < E:
                    transpose_x(e + 1, r + 1, turn)
                gate_up(e, r, turn)
                down(e - 1, (r - 1) % UNROLL)
                transpose_h(e, r)
            down(E - 1, UNROLL - 1)


def kernel(**inputs):
    import numpy as np
    import concourse.bacc as bacc
    from concourse import mybir as mb
    from concourse.bass_utils import run_bass_kernel_spmd as run

    g = {k: np.asarray(v) for k, v in inputs.items()}
    gn, mx, ff = (lambda n: g["L0_gnn_" + n]), (lambda n: g["L0_mix_" + n]), (lambda n: g["L0_ffn_" + n])

    def column(v):
        return v.reshape(-1, P).T

    def pack(gate, up, down):
        n = gate.shape[0]
        gu = np.concatenate([gate, up], axis=1).transpose(0, 2, 1).reshape(n, KD, P, 2 * F).transpose(0, 2, 1, 3)
        dn = down.transpose(0, 2, 1).reshape(n, 2, P, D).transpose(0, 2, 1, 3)
        return np.concatenate([gu.reshape(n, P, -1), dn.reshape(n, P, -1)], axis=2)

    scalars = [mx("gamma_q"), mx("beta_q"), mx("gamma_k"), mx("beta_k"), gn("t0"), gn("t1"), gn("t2")]
    cols = np.concatenate([column(gn(f"mlg_{L}")) for L in range(NL)] + [column(gn(f"mlb_{L}")) for L in range(NL)]
                          + [column(mx("bq")), column(mx("bk"))] + [np.broadcast_to(s, (P, 1)) for s in scalars], axis=1)
    rows = [mx("bv"), mx("bp"), gn("cb"), gn("mb1_0"), gn("mb2_0")]
    for L in range(1, NL):
        rows += [gn(f"mb1_{L}"), gn(f"mb2_{L}"), gn(f"lng_{L}"), gn(f"lnb_{L}")]
    ins = {
        "x": g["x"], "src": g["src"].reshape(CH, T).T, "dst": g["dst"].reshape(CH, T).T,
        "cols": cols, "rows": np.concatenate(rows),
        "w1": np.stack([gn(f"mw1_{L}") for L in range(NL)]), "w2": np.stack([gn(f"mw2_{L}") for L in range(NL)]),
        "cw": gn("cw"), "wmix": np.stack([mx(n) for n in ("Wq", "Wk", "Wv", "Wp")]),
        "gmix": np.stack([mx(n) for n in ("qG1", "qG2", "kG1", "kG2")]),
        "router": ff("router_w").T, "rbias": ff("bias"),
        "shared": pack(ff("shared_w_gate"), ff("shared_w_up"), ff("shared_w_down")),
        "experts": pack(ff("w_gate"), ff("w_up"), ff("w_down")),
    }
    nc = bacc.Bacc("TRN2", target_bir_lowering=False, num_devices=1)
    arrays, args = {}, []
    for name, a in ins.items():
        a = np.ascontiguousarray(a)
        arrays[name + "_in"] = a
        args.append(nc.dram_tensor(name + "_in", a.shape, mb.dt.from_np(a.dtype), kind="ExternalInput").ap())
    args.append(nc.dram_tensor("out_x", (N, D), mb.dt.float32, kind="ExternalOutput").ap())
    gps_kernel(nc, *args)
    return run(nc, [arrays], core_ids=[0]).results[0]["out_x"]
```

```python
from contextlib import ExitStack

import concourse.bass as bass
from concourse import mybir

F32 = mybir.dt.float32
F32R = mybir.dt.float32r
BF16 = mybir.dt.bfloat16
F16 = mybir.dt.float16
I32 = mybir.dt.int32
ACT = mybir.ActivationFunctionType
ALU = mybir.AluOpType
AX = mybir.AxisListType
RMAX = bass.bass_isa.ReduceOp.max

N = 625
T = 125
NT = N // T
D = 512
H = 1024
P = 128
KD = D // P
KH = H // P
TP = N + 1
HALVES = [(0, 314), (314, 312)]
NL = 3
EDGES = 20625
CH = EDGES // T
G = 5
NG = CH // G
E = 64
F = 256
TOPK = 6
CAP = int(N * TOPK * 2.0 / E)
WE = KD * 2 * F + (F // P) * D
FAR = 200.0
SKIP = 100000.0
UNROLL = 4
PKU = NT
NSH = 2 * NT
NW = 63

LIFT = 40.0
AGG_BANK = [0, 2, 6, 0, 2]

COL_LG, COL_LB, COL_BQ, COL_BK, COL_S = 0, 24, 48, 52, 56


def gps_kernel(nc, x, src, dst, cols, rows, w1, w2, cw, wmix, gmix, router, rbias, shared, experts, out):
    xn2 = nc.dram_tensor("xn2_scratch", (N, D), F32, kind="Internal").ap()
    slot_dram = nc.dram_tensor("slot_scratch", (E * CAP, 4), I32, kind="Internal").ap()
    yrow = nc.dram_tensor("yrow_scratch", (N * TOPK, D), F32, kind="Internal").ap()

    with ExitStack() as ctx:
        base = [16512]

        def sb(name, shape, dt, at=None):
            size = {F32: 4, F32R: 4, I32: 4, BF16: 2, F16: 2}[dt]
            for s in shape[1:]:
                size *= s
            if at is None:
                at = base[0]
                base[0] += -(-size // 32) * 32
                assert base[0] <= 229344, (name, base[0])
            return nc.alloc_sbuf_tensor_at(name, shape, dt, offset=at)

        sems = {}

        def S(name):
            if name not in sems:
                sems[name] = ctx.enter_context(nc.semaphore(name))
            return sems[name]

        RG_WORDS = 5008 + 8192 + 4096 + 10240 + 6250
        rg_at = base[0]
        RG = sb("split_operands", [P, RG_WORDS], F32R)
        o_xt, o_w1, o_cw, o_e, o_at = 0, 5008, 13200, 17296, 27536

        def rg(o, *dims, p=P):
            n = 1
            for q in dims:
                n *= q
            v = RG[0:p, o:o + n]
            if len(dims) == 2:
                v = v.rearrange("p (a b) -> p a b", a=dims[0])
            if len(dims) == 3:
                v = v.rearrange("p (a b c) -> p a b c", a=dims[0], b=dims[1])
            return v

        def pair(o, *dims, p=P):
            n = 1
            for q in dims:
                n *= q
            return rg(o, *dims, p=p), rg(o + n, *dims, p=p)

        XT = pair(o_xt, KD, TP)
        HT = [pair(o_xt + 1000 * i, 4 * T) for i in range(2)]
        RT = pair(o_xt + 2000, 8 * T)
        XI = pair(o_xt + 4000, 4 * T)
        W1 = pair(o_w1, KD, H)
        CW = pair(o_cw, KD, D)
        W2 = pair(o_e, KH, D)
        EX = pair(o_e, NT, D, p=T)
        EM = pair(o_e + 5120, NT, D, p=T)
        AT_hi = rg(o_at, NT, N, p=T)
        AT_lo = rg(o_at + 3125, NT, N, p=T)
        WMA, WMB = pair(o_cw, KD, D), pair(o_at, KD, D)
        VV = pair(o_e, NT, D, p=T)
        KT = pair(o_e + 5120, KD, TP)
        QT = KT
        PK = pair(o_w1, NT, D, p=T)
        PQ = pair(o_e, KD, TP)
        OT = pair(o_w1, KD, TP)
        KV = pair(o_w1 + 5120, KD, 256)
        GM = pair(o_w1 + 7168, 4, P)
        RW = sb("router_weights", [P, KD, E], F32, at=rg_at + 4 * o_at)
        SG = [pair(o_w1 + 6144 * s, KD, 2 * F) for s in range(2)]
        SD = [pair(o_w1 + 6144 * s + 4096, 2, D) for s in range(2)]
        ST = pair(o_at + 3125, 2 * T)
        RING = [sb(f"expert_weights{r}", [P, WE], F32, at=rg_at + 4 * (17296 + r * WE)) for r in range(UNROLL)]

        XO = sb("x_out", [T, NT, D], F32)
        XC = sb("x_cur", [T, NT, D], F32)
        fg_at = base[0]
        FG = sb("work", [P, 13312], F32)

        def fg(o, *dims, p=P):
            n = 1
            for q in dims:
                n *= q
            v = FG[0:p, o:o + n]
            if len(dims) == 2:
                v = v.rearrange("p (a b) -> p a b", a=dims[0])
            if len(dims) == 3:
                v = v.rearrange("p (a b c) -> p a b c", a=dims[0], b=dims[1])
            return v

        HN = fg(0, NT, D, p=T)
        STG = [fg(2560 + 2048 * i, 2048) for i in range(2)]
        BC1 = fg(6656, H, p=T)
        BC2, BCG, BCB = [fg(7680 + 512 * i, D, p=T) for i in range(3)]
        YY = [fg(9216 + 1024 * i, H, p=T) for i in range(2)]
        RR = fg(11264, 8 * T)
        EE = [fg(11264 + 512 * i, D, p=T) for i in range(2)]
        EP = [fg(12288 + 512 * i, D, p=T) for i in range(2)]
        LN = fg(12288, D, p=T)
        LN2 = fg(12800, D, p=T)
        MT = [fg(9216 + 1024 * i, 512) for i in range(2)]
        MT2 = [fg(9728 + 1024 * i, 512) for i in range(2)]
        MT3 = [fg(11264 + 512 * i, 512) for i in range(2)]
        iota_i = fg(2560, N + 1, p=T).bitcast(I32)
        los, his = [fg(NT * CH * i, NT, CH, p=1) for i in range(2)]
        gidx = fg(3200, 2, CH, p=1)
        gsteps = fg(1800, NT, NG, p=1)
        gidx_i = fg(3540, CH, p=1).bitcast(I32)
        iota_h = FG[0:T, 3720:3720 + 313].bitcast(F16)
        member = FG[0:T, 4040:4040 + 413].bitcast(BF16)
        srcf = fg(4460, 2 * CH, p=T)
        dstrel = fg(4800, NT, 2 * CH, p=T)
        one_hot_src = FG[0:T, 6656:6656 + G * 313].bitcast(BF16).rearrange("p (g n) -> p g n", g=G)
        one_hot_dst = FG[0:T, 8224:8224 + G * 63].bitcast(BF16).rearrange("p (g n) -> p g n", g=G)
        srci = fg(8544, CH, p=T).bitcast(I32)
        dsti = fg(8712, CH, p=T).bitcast(I32)
        ge = fg(8880, CH, p=T)
        adj = fg(9216, 2, N, p=T)
        zero_b = FG[0:T, 10600:10856].bitcast(BF16)
        LOG, PRB, MSK, KRK, POS, GAT = [fg(320 * i, NT, E, p=T) for i in range(6)]
        ADR = fg(2560, NT, E, p=T)
        BYK = fg(2880, NT, TOPK, E, p=T)
        PAY = fg(4800, NT, TOPK, 4, p=T).bitcast(I32)
        adr_f = fg(4920, NT, TOPK, p=T)
        adr_i = fg(4950, NT, TOPK, p=T).bitcast(I32)
        eoff_i = fg(4980, E, p=T).bitcast(I32)
        eoff = fg(5044, E, p=T)
        MSKB = FG[0:T, 5120:5120 + 160].bitcast(BF16).rearrange("p (t e) -> p t e", t=NT)
        GR = fg(6656, 3, NT * E, p=T)
        RBC = fg(7640, E, p=T)
        SIL = [fg(7720 + 256 * i, F, p=P) for i in range(2)]
        HG = [fg(8232 + 256 * i, F, p=P) for i in range(2)]
        HTF = [fg(8744 + 256 * i, 2 * CAP) for i in range(2)]
        XE = [fg(9256 + 480 * i, KD * CAP) for i in range(2)]
        XG = [fg(10216 + 512 * i, D, p=CAP) for i in range(4)]
        OS = [fg(0 + 512 * i, D, p=CAP) for i in range(4)]
        YL = [rg(TOPK * D * i, TOPK, D, p=T).bitcast(F32) for i in range(NT)]
        ysum = fg(9216, D, p=T)
        ones_f = fg(12288, P, p=T)

        ident = sb("ident", [P, P], F32)
        colp = sb("colp", [P, NW], F32)
        ones_r = sb("ones_r", [T, P], F32R)
        gb = sb("gb", [P, 8], F32)
        mhalf = sb("mhalf", [T, NT], F32)
        stats = sb("stats", [T, NT, 2, 6], F32)
        mv = sb("mv", [T, NT, 2], F32)
        rstd = sb("rstd", [T, NT], F32)
        st_m = sb("st_m", [T, 2, 6], F32)
        mv_m = sb("mv_m", [T, 4], F32)
        st_o = sb("st_o", [T, 1, 6], F32)
        mv_o = sb("mv_o", [T, 4], F32)
        zmx = sb("zmx", [T, NT + 3], F32)
        lohi = sb("lohi", [1, 2, NT], F32)
        lohi_i = sb("lohi_i", [1, 2, NT], I32)
        tri = sb("tri", [T, T], BF16)
        ones_b = sb("ones_b", [T, P], BF16)
        slots = sb("slots", [CAP, E, 4], I32)
        tok_c = sb("tok_c", [CAP, UNROLL], I32)
        row_c = sb("row_c", [CAP, UNROLL], I32)
        r8 = sb("r8", [T, NT, 8], F32)
        rsm = sb("rsm", [T, 4, NT], F32)
        rden = sb("rden", [T, 8], F32)
        ps = ctx.enter_context(nc.psum_tensor("ps", [P, 8, 512], F32))

        pe, dve, act, pool, sp = nc.tensor, nc.vector, nc.scalar, nc.gpsimd, nc.sync

        def f(ap):
            return ap.bitcast(F32)

        def mm3(o, a, b, start, stop):
            pe.matmul(o, a[1], b[0], start=start, stop=False)
            pe.matmul(o, a[0], b[1], start=False, stop=False)
            return pe.matmul(o, a[0], b[0], start=False, stop=stop)

        def sub(p, *ix):
            return (p[0][ix], p[1][ix])

        def by_pair(v):
            return v[0:T, :].rearrange("p (c n) -> p c n", c=KD)

        def two_banks(b):
            return ps[0:T, b:b + 2, :].rearrange("p b (c a n) -> p (b c) a n", c=2, a=2)

        def phi_k_banks(t):
            return two_banks(2 if t % 2 else 6)

        def attn_banks(t):
            return two_banks(4 if t % 2 else 6)

        kv_bank = ps[:, 0:2, :].rearrange("p b (c n) -> p (b c) n", c=2)

        def kv_block(v, h):
            return v[64 * h:64 * h + 64].rearrange("p c (a n) -> p c a n", a=2)[:, :, :, 64 * h:64 * h + 64]

        A_ = slice(None)

        def cut(o, n):
            return slice(o, o + n)

        vstep = [0]

        def v1(ins):
            vstep[0] += 1
            ins.then_inc(S("vector_step"), 1)
            dve.wait_ge(S("vector_step"), vstep[0])

        astep = [0]

        def a1(ins):
            astep[0] += 1
            ins.then_inc(S("scalar_step"), 1)
            act.wait_ge(S("scalar_step"), astep[0])

        gstep = [0]

        def g1(ins):
            gstep[0] += 1
            ins.then_inc(S("pool_step"), 1)
            pool.wait_ge(S("pool_step"), gstep[0])

        w1v = [w1[L].rearrange("(k p) n -> p k n", p=P) for L in range(NL)]
        w2v = [w2[L].rearrange("(k p) n -> p k n", p=P) for L in range(NL)]
        cwv = [cw[L * D:(L + 1) * D, :].rearrange("(k p) n -> p k n", p=P) for L in range(NL)]
        wmv = [wmix[i].rearrange("(k p) n -> p k n", p=P) for i in range(4)]
        plan = []

        def piece(name, source, parts, free=None):
            plan.append((name, source, parts, free))

        piece("wv", wmv[2], WMA)
        piece("wk", wmv[1], WMB)
        piece("g", None, GM)
        piece("wq", wmv[0], WMA, ("v_ps", NT))
        piece("wp", wmv[3], WMB, ("kt_ps", 8))
        for L in range(NL):
            gone = ("mix_out_ps", NT) if L == 0 else ("w1_ps", NT * L)
            for k in range(2):
                piece(f"w1_{L}{k}", w1v[L][:, 2 * k:2 * k + 2, :], sub(W1, A_, cut(2 * k, 2), A_), gone)
            piece(f"cw_{L}", cwv[L], CW, ("mix_out_ps", NT) if L == 0 else ("cw_ps", NT * L))
            for k in range(2):
                piece(f"w2_{L}{k}", w2v[L][:, 4 * k:4 * k + 4, :], sub(W2, A_, cut(4 * k, 4), A_), ("agg_ps", NT * (L + 1)))
        for s in range(2):
            gone = ("cw_ps", NT * NL) if s else ("w1_ps", NT * NL)
            piece(f"sg{s}", shared[s, :, 0:KD * 2 * F].rearrange("p (k n) -> p k n", k=KD), SG[s], gone)
            piece(f"sd{s}", shared[s, :, KD * 2 * F:WE].rearrange("p (k n) -> p k n", k=2), SD[s], gone)
        order = {n: i for i, (n, _, _, _) in enumerate(plan)}

        def staged(i):
            parts = plan[i][2][0]
            n = 1
            for q in parts.shape[1:]:
                n *= q
            v = STG[i % 2][:, 0:n]
            return v.rearrange("p (k n) -> p k n", k=parts.shape[1])

        def split_hi(name):
            i = order[name]
            act.wait_ge(S(f"stage_in{i % 2}"), 16 * (i // 2 + 1) + (16 if i >= order["g"] and i % 2 == order["g"] % 2 else 0))
            free = plan[i][3]
            if free:
                act.wait_ge(S(free[0]), free[1])
            act.activation(plan[i][2][0], staged(i), ACT.Copy).then_inc(S("weight_hi"), 1)

        def split_lo(name):
            i = order[name]
            dve.wait_ge(S("weight_hi"), i + 1)
            dve.tensor_tensor(plan[i][2][1], staged(i), f(plan[i][2][0]), ALU.subtract).then_inc(S("weight_lo"), 1)

        def weights(name):
            pe.wait_ge(S("weight_lo"), order[name] + 1)


        block = ctx.enter_context(nc.Block())

        @block.sync
        def _(eng):
            sp.dma_start(XO[:], x.rearrange("(t p) f -> p t f", p=T)).then_inc(S("x_in"), 16)
            sp.dma_start(colp[:], cols).then_inc(S("cols_in"), 16)
            sp.dma_start(BC1[:, 0:D], rows[0:D].partition_broadcast(T)).then_inc(S("mixrow_in"), 16)
            sp.dma_start(BC1[:, D:H], rows[D:2 * D].partition_broadcast(T)).then_inc(S("mixrow_in"), 16)
            sp.dma_start(BC2, rows[2 * D:3 * D].partition_broadcast(T)).then_inc(S("mixrow_in"), 16)

            def load(name):
                i = order[name]
                if i >= 2:
                    sp.wait_ge(S("weight_lo"), i - 1)
                if name == "g":
                    sp.wait_ge(S("stage_zero"), 1)
                    gv = staged(i)
                    sp.dma_start(gv[0:64, :, 0:64], gmix.rearrange("g p n -> p g n")).then_inc(S(f"stage_in{i % 2}"), 16)
                    sp.dma_start(gv[64:128, :, 64:128], gmix.rearrange("g p n -> p g n")).then_inc(S(f"stage_in{i % 2}"), 16)
                else:
                    sp.dma_start(staged(i), plan[i][1]).then_inc(S(f"stage_in{i % 2}"), 16)

            for n in ("wv", "wk"):
                load(n)
            sp.dma_start(srci, src).then_inc(S("edges_in"), 16)
            sp.dma_start(dsti, dst).then_inc(S("edges_in"), 16)
            for n in ("g", "wq", "wp"):
                load(n)
            slots_view = slot_dram.rearrange("(e s) c -> s e c", s=CAP)
            sp.wait_ge(S("slots_empty"), 1)
            sp.dma_start(slots_view, slots[:]).then_inc(S("slots_clear"), 16)
            sp.wait_ge(S("vector_consts"), 2)
            for q in range(NT):
                sp.dma_start(yrow[750 * q:750 * (q + 1), :].rearrange("(p a) (h n) -> p (a h) n", p=T, h=2),
                             zero_b.bitcast(F32).unsqueeze(1).to_broadcast([T, 2 * TOPK, D // 2])).then_inc(S("y_zero"), 16)
            sp.wait_ge(S("adj_lo"), NT)
            r = 3 * D
            for L in range(NL):
                if L:
                    sp.wait_ge(S("x_next"), NT * L)
                sp.dma_start(BC1, rows[r:r + H].partition_broadcast(T)).then_inc(S("rows_in"), 16)
                sp.dma_start(BC2, rows[r + H:r + H + D].partition_broadcast(T)).then_inc(S("rows_in"), 16)
                r += H + D
                if L:
                    sp.dma_start(BCG, rows[r:r + D].partition_broadcast(T)).then_inc(S("rows_in"), 16)
                    sp.dma_start(BCB, rows[r + D:r + 2 * D].partition_broadcast(T)).then_inc(S("rows_in"), 16)
                    r += 2 * D
                for n in (f"w1_{L}0", f"w1_{L}1", f"cw_{L}", f"w2_{L}0", f"w2_{L}1"):
                    load(n)
            sp.wait_ge(S("agg_ps"), NT * NL)
            sp.dma_start(RW[:], router.rearrange("(k p) n -> p k n", p=P)).then_inc(S("rw_in"), 16)
            load("sg0")
            load("sd0")
            sp.wait_ge(S("x_next"), NT * NL)
            sp.dma_start(RBC, rbias.partition_broadcast(T)).then_inc(S("rbias_in"), 16)
            load("sg1")
            load("sd1")
            sp.wait_ge(S("fin_norm"), NT)
            sp.dma_start(xn2.rearrange("(t p) f -> p t f", p=T), XC[:]).then_inc(S("xn2_out"), 16)
            sp.wait_ge(S("w2_ps"), NT * NL)

            def load_expert(e, r):
                sp.dma_start(RING[r][:], experts[e].rearrange("a p n -> (a p) n")).then_inc(S(f"ring_in{r}"), 16)

            for r in range(UNROLL):
                if r == UNROLL - 1:
                    sp.wait_ge(S("router_ps"), NT)
                load_expert(cut(r, 1), r)
            sp.wait_ge(S("slots_out"), 16 * NT * TOPK)
            sp.dma_start(slots[:], slots_view).then_inc(S("tables"), 16)
            with sp.Fori(1, E // UNROLL) as i:
                for r in range(UNROLL):
                    sp.wait_ge(S("o_ps"), UNROLL * i + r - 3)
                    load_expert(bass.ds(UNROLL * i + r, 1), r)
            for r in range(UNROLL):
                sp.wait_ge(S(f"y_out{r}"), 16 * (E // UNROLL))
            for t in range(NT):
                sp.dma_start(YL[t], yrow[750 * t:750 * (t + 1), :].rearrange("(p a) n -> p a n", p=T)).then_inc(S(f"y_in{t}"), 16)
            for t in range(NT):
                sp.wait_ge(S("y_sum"), t + 1)
                sp.dma_start(out[T * t:T * (t + 1), :], XO[:, t, :]).then_inc(S("out_done"), 16)
            sp.wait_ge(S("out_done"), 16 * NT)

        @block.gpsimd
        def _(eng):
            g1(pool.memset(ident[:], 0.0))
            pool.affine_select(out=ident[:], in_=ident[:], compare_op=ALU.not_equal, fill=1.0, base=0,
                               pattern=[[-1, P]], channel_multiplier=1).then_inc(S("pool_consts"), 1)
            g1(pool.memset(mhalf[:], -0.5))
            g1(pool.memset(slots[:], int(SKIP)))
            pool.memset(slots[:, :, 2:3], 0).then_inc(S("slots_empty"), 1)
            pool.memset(f(XT[0][:, :, N:TP]), 0.0)
            pool.memset(f(XT[1][:, :, N:TP]), 0.0)
            pool.memset(f(KV[0]), 0.0)
            pool.memset(f(KV[1]), 0.0).then_inc(S("pool_consts"), 1)
            g1(pool.memset(tri[:], 1.0))
            pool.affine_select(out=tri[:], in_=tri[:], compare_op=ALU.is_gt, fill=0.0, base=0,
                               pattern=[[1, T]], channel_multiplier=-1)
            pool.memset(ones_b[:], 1.0).then_inc(S("pool_consts"), 1)

            def rsqrt(o, i, n, wait, value, done):
                pool.wait_ge(S(wait), value)
                pool.tensor_tensor(o, i, mhalf[:, 0:n], ALU.pow).then_inc(S(done), 1)

            rsqrt(rstd[:], mv[:, :, 1], NT, "in_var", 1, "in_rstd")
            pool.wait_ge(S("weight_lo"), 1)
            pool.memset(STG[order["g"] % 2][:, 0:4 * P], 0.0).then_inc(S("stage_zero"), 1)
            pool.wait_ge(S("in_norm"), NT)
            pool.wait_ge(S("mixrow_in"), 48)
            for t in range(NT):
                g1(pool.tensor_tensor(XO[:, t, :], XO[:, t, :], BC1[:, D:H], ALU.add))
                pool.tensor_tensor(XO[:, t, :], XO[:, t, :], BC2, ALU.add).then_inc(S("x_rows"), 1)
            for t in range(NT):
                pool.wait_ge(S("v_hi"), t + 1)
                pool.tensor_tensor(VV[1][:, t, :], MT[t % 2][0:T, :], f(VV[0][:, t, :]), ALU.subtract).then_inc(S("v_lo"), 1)
            pool.wait_ge(S("weight_lo"), order["wp"] + 1)
            pool.iota(iota_i, pattern=[[1, N + 1]], base=0, channel_multiplier=0).then_inc(S("iota"), 1)
            pool.iota(gidx_i, pattern=[[1, CH]], base=0, channel_multiplier=0).then_inc(S("iota"), 1)
            for L in range(NL):
                pool.wait_ge(S("zmax"), L + 1)
                pool.partition_all_reduce(zmx[:, NT + 1:NT + 2], zmx[:, NT:NT + 1], T, RMAX).then_inc(S("zmax_all"), 1)
                def mlp_rstd(i):
                    if i < NT:
                        rsqrt(mv_m[:, 2:3], mv_m[:, 1:2], 1, "mlp_var", NT * L + i + 1, "mlp_rstd")

                mlp_rstd(0)
                mlp_rstd(1)
                for i in range(NT):
                    mlp_rstd(i + 2)
                    if L:
                        rsqrt(mv_o[:, 2:3], mv_o[:, 1:2], 1, "out_var", NT * (L - 1) + i + 1, "out_rstd")
            pool.wait_ge(S("x_next"), NT * NL)
            rsqrt(rstd[:], mv[:, :, 1], NT, "fin_var", 1, "fin_rstd")
            pool.wait_ge(S("weight_lo"), order["sd1"] + 1)
            pool.iota(PAY[:, :, :, 0], pattern=[[T, NT], [0, TOPK]], base=0, channel_multiplier=1)
            pool.iota(PAY[:, :, :, 1], pattern=[[T * TOPK, NT], [1, TOPK]], base=0, channel_multiplier=TOPK)
            pool.iota(eoff_i, pattern=[[CAP, E]], base=0, channel_multiplier=0).then_inc(S("iota"), 1)
            pool.wait_ge(S("r_lo"), 2 * NT * NL)
            for r in range(UNROLL):
                last = pool.memset(XG[r], 0.0)
            last.then_inc(S("xg_zero"), 1)
            pool.wait_ge(S("slots_clear"), 16)
            pool.wait_ge(S("choices"), 1)
            pool.wait_ge(S("iota"), 3)
            last_slot = pool.to_reg(E * CAP - 1)
            for t in range(NT):
                for k in range(TOPK):
                    pool.indirect_dma_start(slot_dram, bass.IndirectOffsetOnAxis(ap=adr_i[:, t, k:k + 1], axis=0), PAY[:, t, k, :], None,
                                            bounds_check=last_slot, oob_is_err=False).then_inc(S("slots_out"), 16)
            pool.wait_ge(S("y_zero"), 16 * NT)
            pool.wait_ge(S("xg_zero"), 1)
            pool.wait_ge(S("xn2_out"), 16)
            pool.wait_ge(S("tables"), 16)
            pool.tensor_copy(tok_c[:].unsqueeze(2), slots[:, 0:UNROLL, 0:1]).then_inc(S("tok_col"), UNROLL)
            last_token = pool.to_reg(N - 1)
            last_row = pool.to_reg(N * TOPK - 1)

            def gather(n, r):
                pool.wait_ge(S("tok_col"), n + 1)
                pool.sem_inc(S("pool_turns"), 1)
                pool.indirect_dma_start(XG[r], None, xn2, bass.IndirectOffsetOnAxis(ap=tok_c[:, cut(r, 1)], axis=0),
                                        bounds_check=last_token, oob_is_err=False).then_inc(S(f"xg_in{r}"), 16)

            def scatter(n, r):
                pool.wait_ge(S("scaled"), n + 1)
                pool.sem_inc(S("pool_turns"), 1)
                pool.indirect_dma_start(yrow, bass.IndirectOffsetOnAxis(ap=row_c[:, cut(r, 1)], axis=0), OS[r], None,
                                        bounds_check=last_row, oob_is_err=False).then_inc(S(f"y_out{r}"), 16)

            for e in range(UNROLL):
                gather(e, e)
            for e in range(UNROLL):
                gather(e + UNROLL, e)
                scatter(e, e)
            with pool.Fori(1, E // UNROLL - 1) as i:
                for r in range(UNROLL):
                    e = UNROLL * i + r
                    gather(e + UNROLL, r)
                    scatter(e, r)
            for r in range(UNROLL):
                scatter(E - UNROLL + r, r)

        @block.scalar
        def _(eng):
            def tr_hi(which):
                for t in range(NT):
                    act.wait_ge(S(which + "_tr"), t + 1)
                    act.activation(XT[0][:, :, cut(t * T, T)], ps[:, t % 2, 0:KD * T].rearrange("p (k n) -> p k n", k=KD),
                                   ACT.Copy).then_inc(S(which + "_hi"), 1)

            split_hi("wv")
            tr_hi("in")
            split_hi("wk")
            for t in range(NT):
                act.wait_ge(S("v_sb"), t + 1)
                act.activation(VV[0][:, t, :], MT[t % 2][0:T, :], ACT.Copy).then_inc(S("v_hi"), 1)
                if t == 1:
                    split_hi("g")
            act.wait_ge(S("cols_in"), 16)
            act.wait_ge(S("gb"), 1)

            def proj(u):
                q = u >= 8
                c, h = divmod(u % 8, 2)
                n0, nn = HALVES[h]
                act.wait_ge(S("kt_ps"), u + 1)
                if u >= 2:
                    act.wait_ge(S("kt_lo"), u - 1)
                act.activation(MT2[u % 2][:, 0:nn], ps[:, 4 + u % 2, 0:nn], ACT.Identity,
                               bias=gb[:, cut((0 if q else 4) + c, 1)],
                               scale=colp[:, cut(COL_S + (0 if q else 2), 1)]).then_inc(S("kt_sb"), 1)
                act.wait_ge(S("kt_sb"), u + 1)
                if u == 8:
                    act.wait_ge(S("pk_ps"), NT)
                act.activation(KT[0][:, c, cut(n0, nn)], MT2[u % 2][:, 0:nn], ACT.Copy).then_inc(S("kt_hi"), 1)

            for u in range(8):
                proj(u)
                if u == 3:
                    split_hi("wq")
            split_hi("wp")
            act.wait_ge(S("v_lo"), NT)

            def pk_scale(t):
                act.wait_ge(S("pk_ps"), t + 1)
                if t >= 2:
                    act.wait_ge(S("pk_lo"), t - 1)
                act.activation(by_pair(MT[t % 2]), phi_k_banks(t)[:, :, 0, :], ACT.Copy, scale=0.125).then_inc(S("pk_a"), 1)

            def pk_square(t):
                act.wait_ge(S("pk_ab"), t + 1)
                a1(act.activation(MT[t % 2][0:T, :], MT3[t % 2][0:T, :], ACT.Square))
                act.activation(PK[0][:, t, :], MT[t % 2][0:T, :], ACT.Copy).then_inc(S("pk_hi"), 1)

            pk_scale(0)
            for t in range(NT):
                if t + 1 < NT:
                    pk_scale(t + 1)
                pk_square(t)
            act.wait_ge(S("kv_ps"), 1)
            for h in range(2):
                last = act.activation(kv_block(KV[0], h), kv_block(kv_bank, h), ACT.Copy)
            last.then_inc(S("kv_hi"), 1)
            for u in range(8, 16):
                proj(u)

            def pq_scale(u):
                nn = HALVES[u % 2][1]
                act.wait_ge(S("pk_ps"), PKU + u + 1)
                if u >= 2:
                    act.wait_ge(S("pk_lo"), PKU + u - 1)
                act.activation(MT[u % 2][:, 0:nn], ps[:, 2 + u % 2, 0:nn], ACT.Copy, scale=0.125).then_inc(S("pk_a"), 1)

            def pq_square(u):
                c, h = divmod(u, 2)
                n0, nn = HALVES[h]
                act.wait_ge(S("pk_ab"), PKU + u + 1)
                a1(act.activation(MT[u % 2][:, 0:nn], MT3[u % 2][:, 0:nn], ACT.Square))
                act.activation(PQ[0][:, c, cut(n0, nn)], MT[u % 2][:, 0:nn], ACT.Copy).then_inc(S("pk_hi"), 1)

            pq_scale(0)
            for u in range(8):
                if u + 1 < 8:
                    pq_scale(u + 1)
                pq_square(u)
            for t in range(NT):
                act.wait_ge(S("attn_tr"), t + 1)
                act.activation(OT[0][:, :, cut(t * T, T)], ps[:, t % 2, 0:KD * T].rearrange("p (k n) -> p k n", k=KD),
                               ACT.Copy).then_inc(S("attn_hi"), 1)

            def adj_out(j):
                act.wait_ge(S("adj_ps"), j + 1)
                if j >= 2:
                    act.wait_ge(S("adj_tr"), j - 1)
                act.activation(adj[:, j % 2, 0:313], ps[0:T, 2 * (j % 2), 0:313], ACT.Copy)
                act.activation(adj[:, j % 2, 313:N], ps[0:T, 2 * (j % 2) + 1, 0:312], ACT.Copy).then_inc(S("adj_sb"), 1)

            adj_out(0)
            for j in range(NT):
                if j + 1 < NT:
                    adj_out(j + 1)
                act.wait_ge(S("adj_tr"), j + 1)
                act.activation(AT_hi[:, 0:3, cut(j * T, T)], ps[0:T, 4, 0:3 * T].rearrange("p (s n) -> p s n", s=3), ACT.Copy)
                act.activation(AT_hi[:, 3:5, cut(j * T, T)], ps[0:T, 5, 0:2 * T].rearrange("p (s n) -> p s n", s=2),
                               ACT.Copy).then_inc(S("adj_hi"), 1)

            for L in range(NL):
                act.wait_ge(S("zmax_neg"), L + 1)
                for t in range(NT + 1):
                    n = NT * L + t
                    if t < NT:
                        if t >= 2:
                            act.wait_ge(S("e_lo"), n - 1)
                        act.activation(EE[t % 2], HN[:, t, :], ACT.Exp, scale=colp[0:T, cut(COL_S + 4 + L, 1)],
                                       bias=zmx[:, NT + 2:NT + 3]).then_inc(S("exp"), 1)
                    if t >= 1:
                        act.wait_ge(S("em"), n)
                        act.activation(EM[0][:, t - 1, :], EP[(t - 1) % 2], ACT.Copy).then_inc(S("em_hi"), 1)
                    if t < NT:
                        act.wait_ge(S("exp"), n + 1)
                        act.activation(EX[0][:, t, :], EE[t % 2], ACT.Copy).then_inc(S("e_hi"), 1)
                for nme in (f"w1_{L}0", f"w1_{L}1", f"cw_{L}"):
                    split_hi(nme)

                def h_hi(i):
                    act.wait_ge(S("h_tr"), NT * L + i + 1)
                    act.activation(HT[i % 2][0], ps[:, 4, 0:4 * T], ACT.Copy).then_inc(S("ht_hi"), 1)

                def y_norm(i):
                    act.wait_ge(S("mlp_nmr"), NT * L + i + 1)
                    act.activation(YY[i % 2], YY[i % 2], ACT.Identity, bias=mv_m[:, 3:4], scale=mv_m[:, 2:3]).then_inc(S("y_norm"), 1)

                h_hi(0)
                h_hi(1)
                split_hi(f"w2_{L}0")
                h_hi(2)
                split_hi(f"w2_{L}1")
                y_norm(0)
                for i in range(NT + 1):
                    n = NT * L + i
                    if i < NT:
                        act.wait_ge(S("y_tr"), n + 1)
                        if n >= 1:
                            act.wait_ge(S("r_lo"), 2 * n)
                        for k in range(KH):
                            last = act.activation(RR[:, cut(k * T, T)], ps[:, 2 + k // 4, cut((k % 4) * T, T)], ACT.Relu,
                                                  bias=colp[:, cut(COL_LB + 8 * L + k, 1)], scale=colp[:, cut(COL_LG + 8 * L + k, 1)])
                            if k % 4 == 3:
                                last.then_inc(S("relu"), 1)
                        if n >= 1:
                            act.wait_ge(S("w2_ps"), n)
                        for h in range(2):
                            act.wait_ge(S("relu"), 2 * n + h + 1)
                            act.activation(RT[0][:, cut(500 * h, 500)], RR[:, cut(500 * h, 500)], ACT.Copy).then_inc(S("r_hi"), 1)
                    if i + 1 < NT:
                        y_norm(i + 1)
                    if i + 3 < NT:
                        h_hi(i + 3)
                    if i >= 1:
                        act.wait_ge(S("x_tr"), n)
                        act.activation(XI[0], ps[:, 6, 0:4 * T], ACT.Copy).then_inc(S("xi_hi"), 1)
                    if L == NL - 1 and i == NT - 1:
                        split_hi("sg0")
                        split_hi("sd0")
            tr_hi("fin")
            for nme in ("sg1", "sd1"):
                split_hi(nme)
            for t in range(NT):
                act.wait_ge(S("log_max"), t + 1)
                act.activation(PRB[:, t, :], LOG[:, t, :], ACT.Exp, bias=rsm[:, 0, cut(t, 1)],
                               accum_out=rsm[:, 1, cut(t, 1)]).then_inc(S("log_exp"), 1)

            def shared_silu(n):
                act.wait_ge(S("gu_ps"), n + 1)
                if n >= 2:
                    act.wait_ge(S("hg"), n - 1)
                act.activation(SIL[n % 2][0:T, :], ps[0:T, 2 + n % 2, 0:F], ACT.Silu).then_inc(S("silu"), 1)

            def shared_hi(n):
                act.wait_ge(S("ht_ps"), n + 1)
                act.activation(ST[0], ps[:, 6, 0:2 * T], ACT.Copy).then_inc(S("s_t_hi"), 1)

            shared_silu(0)
            for n in range(2 * NT):
                shared_hi(n)
                if n + 1 < 2 * NT:
                    shared_silu(n + 1)

            def after(name, value):
                if not isinstance(value, int) or value > 0:
                    act.wait_ge(S(name), value)

            def xe_copy(e, r):
                act.wait_ge(S("xe_ps"), e + 1)
                after("gu_ps", NSH + e - 1)
                act.activation(XE[r % 2], ps[:, r % 2, 0:KD * CAP], ACT.Copy).then_inc(S("xe_sb"), 1)

            def silu(e, r):
                act.wait_ge(S("gu_ps"), NSH + e + 1)
                after("hg", NSH + e - 1)
                act.activation(SIL[r % 2][0:CAP, :], ps[0:CAP, 2 + r % 2, 0:F], ACT.Silu).then_inc(S("silu"), 1)

            def scale(e, col, r):
                act.wait_ge(S("o_ps"), e + 1)
                act.wait_ge(S("row_col"), e + 1)
                act.activation(OS[r], ps[0:CAP, 6 + r % 2, 0:D], ACT.Copy,
                               scale=f(slots[:, col, 2:3]).rearrange("p a b -> p (a b)")).then_inc(S("scaled"), 1)

            act.wait_ge(S("tables"), 16)
            xe_copy(0, 0)
            for r in range(UNROLL):
                xe_copy(r + 1, (r + 1) % UNROLL)
                silu(r, r)
                if r >= 1:
                    scale(r - 1, cut(r - 1, 1), r - 1)
            with act.Fori(1, E // UNROLL - 1) as i:
                for r in range(UNROLL):
                    e = UNROLL * i + r
                    xe_copy(e + 1, (r + 1) % UNROLL)
                    silu(e, r)
                    scale(e - 1, bass.ds(e - 1, 1), (r - 1) % UNROLL)
            for r in range(UNROLL):
                e = E - UNROLL + r
                if e + 1 < E:
                    xe_copy(e + 1, (r + 1) % UNROLL)
                silu(e, r)
                scale(e - 1, cut(e - 1, 1), (r - 1) % UNROLL)
            scale(E - 1, cut(E - 1, 1), UNROLL - 1)

        @block.vector
        def _(eng):
            def row_stats(var, rs, norm):
                for t in range(NT):
                    if var == "fin_var":
                        dve.wait_ge(S("cw_add"), NT * (NL - 1) + t + 1)
                    last = dve.bn_stats(stats[:, t, 0, :], XO[:, t, :])
                v1(last)
                for t in range(NT):
                    last = dve.bn_aggr(mv[:, t, :], stats[:, t, 0, :])
                v1(last)
                dve.tensor_scalar(mv[:, :, 1], mv[:, :, 1], 1e-5, None, ALU.add).then_inc(S(var), 1)
                dve.wait_ge(S(rs), 1)
                for t in range(NT):
                    dve.tensor_scalar(XC[:, t, :], XO[:, t, :], mv[:, t, 0:1], rstd[:, cut(t, 1)],
                                      ALU.subtract, ALU.mult).then_inc(S(norm), 1)

            def tr_lo(which):
                for t in range(NT):
                    dve.wait_ge(S(which + "_hi"), t + 1)
                    dve.tensor_tensor(XT[1][:, :, cut(t * T, T)], ps[:, t % 2, 0:KD * T].rearrange("p (k n) -> p k n", k=KD),
                                      f(XT[0][:, :, cut(t * T, T)]), ALU.subtract).then_inc(S(which + "_lo"), 1)

            def message(L, t):
                v1(dve.tensor_scalar(HN[:, t, :], XC[:, t, :], 0.0, 1e-7, ALU.max, ALU.add))
                v1(dve.tensor_scalar(LN2, HN[:, t, :], colp[0:T, cut(COL_S + 4 + L, 1)], -3.0e38, ALU.mult, ALU.max,
                                     accum_out=zmx[:, cut(t, 1)]))
                if t == NT - 1:
                    dve.tensor_reduce(zmx[:, NT:NT + 1], zmx[:, 0:NT], axis=AX.X, op=ALU.max).then_inc(S("zmax"), 1)

            v1(dve.memset(ones_f, 1.0))
            dve.tensor_copy(ones_r[:], ones_f).then_inc(S("vector_consts"), 1)
            dve.wait_ge(S("x_in"), 16)
            row_stats("in_var", "in_rstd", "in_norm")
            split_lo("wv")
            tr_lo("in")
            split_lo("wk")
            dve.wait_ge(S("cols_in"), 16)
            dve.tensor_scalar(gb[:, 0:4], colp[:, COL_BQ:COL_BQ + 4], colp[:, COL_S:COL_S + 1], colp[:, COL_S + 1:COL_S + 2], ALU.mult, ALU.add)
            dve.tensor_scalar(gb[:, 4:8], colp[:, COL_BK:COL_BK + 4], colp[:, COL_S + 2:COL_S + 3], colp[:, COL_S + 3:COL_S + 4],
                              ALU.mult, ALU.add).then_inc(S("gb"), 1)
            dve.wait_ge(S("mixrow_in"), 48)
            for t in range(NT):
                dve.wait_ge(S("v_ps"), t + 1)
                if t >= 2:
                    dve.wait_ge(S("v_lo"), t - 1)
                dve.tensor_tensor(MT[t % 2][0:T, :], ps[0:T, 2 + t % 2, :], BC1[:, 0:D], ALU.add).then_inc(S("v_sb"), 1)
                if t == 1:
                    split_lo("g")

            def proj_lo(u):
                c, h = divmod(u % 8, 2)
                n0, nn = HALVES[h]
                dve.wait_ge(S("kt_hi"), u + 1)
                dve.tensor_tensor(KT[1][:, c, cut(n0, nn)], MT2[u % 2][:, 0:nn], f(KT[0][:, c, cut(n0, nn)]),
                                  ALU.subtract).then_inc(S("kt_lo"), 1)

            for u in range(8):
                proj_lo(u)
                if u == 3:
                    split_lo("wq")

            def pk_mul(t):
                dve.wait_ge(S("pk_a"), t + 1)
                dve.tensor_tensor(by_pair(MT3[t % 2]), phi_k_banks(t)[:, :, 1, :], by_pair(MT[t % 2]), ALU.mult).then_inc(S("pk_ab"), 1)

            pk_mul(0)
            split_lo("wp")
            for t in range(NT):
                if t + 1 < NT:
                    pk_mul(t + 1)
                dve.wait_ge(S("pk_hi"), t + 1)
                dve.tensor_tensor(PK[1][:, t, :], MT[t % 2][0:T, :], f(PK[0][:, t, :]), ALU.subtract).then_inc(S("pk_lo"), 1)
            dve.wait_ge(S("iota"), 2)
            v1(dve.tensor_copy(iota_h, iota_i))
            v1(dve.tensor_copy(gidx[:, 0, :], gidx_i))
            v1(dve.tensor_scalar(gidx[:, 1, :], gidx[:, 0, :], 1.0, None, ALU.add))
            v1(dve.tensor_scalar(gidx[:, 0, :], gidx[:, 0, :], -FAR, None, ALU.add))
            dve.wait_ge(S("edges_in"), 32)
            dve.memset(srcf[:, CH:2 * CH], 0.0)
            for j in range(NT):
                dve.memset(dstrel[:, j, CH:2 * CH], -1.0)
            dve.tensor_copy(srcf[:, 0:CH], srci)
            v1(dve.tensor_copy(dstrel[:, 0, 0:CH], dsti))
            for j in range(1, NT):
                last = dve.tensor_scalar(dstrel[:, j, 0:CH], dstrel[:, 0, 0:CH], float(-T * j), None, ALU.add)
            v1(last)
            for j in range(NT):
                v1(dve.tensor_scalar(ge, dstrel[:, j, 0:CH], 0.0, None, ALU.is_ge))
                v1(dve.scalar_tensor_tensor(out=member[:, cut(j * CH, CH)], in0=dstrel[:, j, 0:CH], scalar=float(T), in1=ge,
                                            op0=ALU.is_lt, op1=ALU.mult))
            dve.sem_inc(S("member"), 1)
            dve.wait_ge(S("kv_hi"), 1)
            for h in range(2):
                last = dve.tensor_tensor(kv_block(KV[1], h), kv_block(kv_bank, h), f(kv_block(KV[0], h)), ALU.subtract)
            last.then_inc(S("kv_lo"), 1)
            for u in range(8, 10):
                proj_lo(u)
            dve.wait_ge(S("member_ps"), 1)
            for j in range(NT):
                b, q = (6, j) if j < 3 else (7, j - 3)
                for v, k in ((los, 0), (his, 1)):
                    last = dve.scalar_tensor_tensor(out=v[:, j, :], in0=ps[0:1, b, cut(q * CH, CH)], scalar=0.5, in1=gidx[:, k, :],
                                                    op0=ALU.is_gt, op1=ALU.mult)
            v1(last)
            dve.tensor_reduce(lohi[:, 0, :], los, axis=AX.X, op=ALU.min)
            v1(dve.tensor_reduce(lohi[:, 1, :], his, axis=AX.X, op=ALU.max))
            v1(dve.tensor_scalar(lohi[:, 0, :], lohi[:, 0, :], FAR, float(CH - 1), ALU.add, ALU.min))
            v1(dve.tensor_tensor(lohi[:, 1, :], lohi[:, 1, :], lohi[:, 0, :], ALU.subtract))
            for j in range(NT):
                last = dve.tensor_scalar(gsteps[:, j, :], gidx[:, 1, 0:NG], float(G), None, ALU.mult)
            v1(last)
            v1(dve.tensor_tensor(gsteps, gsteps, lohi[:, 1, :].unsqueeze(2).to_broadcast([1, NT, NG]), ALU.is_lt))
            v1(dve.tensor_reduce(lohi[:, 1, :], gsteps, axis=AX.X, op=ALU.add))
            v1(dve.tensor_scalar(lohi[:, 1, :], lohi[:, 1, :], 1.0, None, ALU.add))
            dve.tensor_copy(lohi_i[:], lohi[:]).then_inc(S("ranges"), 1)
            dve.wait_ge(S("ranges"), 1)

            for u in range(10, 16):
                proj_lo(u)
                if u < 15:
                    message(0, u - 10)

            def pq_mul(u):
                nn = HALVES[u % 2][1]
                dve.wait_ge(S("pk_a"), PKU + u + 1)
                dve.tensor_tensor(MT3[u % 2][:, 0:nn], ps[:, 6 + u % 2, 0:nn], MT[u % 2][:, 0:nn], ALU.mult).then_inc(S("pk_ab"), 1)

            pq_mul(0)
            for u in range(8):
                c, h = divmod(u, 2)
                n0, nn = HALVES[h]
                if u + 1 < 8:
                    pq_mul(u + 1)
                dve.wait_ge(S("pk_hi"), PKU + u + 1)
                dve.tensor_tensor(PQ[1][:, c, cut(n0, nn)], MT[u % 2][:, 0:nn], f(PQ[0][:, c, cut(n0, nn)]),
                                  ALU.subtract).then_inc(S("pk_lo"), 1)
            def mix_add(t):
                dve.wait_ge(S("mix_out_ps"), t + 1)
                dve.wait_ge(S("x_rows"), t + 1)
                dve.tensor_tensor(XO[:, t, :], XO[:, t, :], ps[0:T, 2 + t % 2, :], ALU.add).then_inc(S("mix_out_add"), 1)

            for t in range(NT + 1):
                if t < NT:
                    dve.wait_ge(S("attn_ps"), t + 1)
                    dens = attn_banks(t)[:, :, 1, :].rearrange("p c (h n) -> p c h n", h=2)
                    nums = attn_banks(t)[:, :, 0, :].rearrange("p c (h n) -> p c h n", h=2)
                    den = rden[:].rearrange("p (c h) -> p c h", c=KD)
                    v1(dve.tensor_scalar(den, dens[:, :, :, 0], 1e-6, None, ALU.add))
                    v1(dve.reciprocal(rden[:], rden[:]))
                    if t >= 2:
                        dve.wait_ge(S("attn_tr"), t - 1)
                    v1(dve.tensor_tensor(MT3[t % 2][0:T, :].rearrange("p (c h n) -> p c h n", c=KD, h=2), nums,
                                         den.unsqueeze(3).to_broadcast([T, KD, 2, 64]), ALU.mult))
                    dve.sem_inc(S("attn"), 1)
                if t >= 1:
                    dve.wait_ge(S("attn_hi"), t)
                    dve.tensor_tensor(OT[1][:, :, cut((t - 1) * T, T)], ps[:, (t - 1) % 2, 0:KD * T].rearrange("p (k n) -> p k n", k=KD),
                                      f(OT[0][:, :, cut((t - 1) * T, T)]), ALU.subtract).then_inc(S("attn_lo"), 1)
                if t >= 2:
                    mix_add(t - 2)
            mix_add(NT - 1)

            dve.memset(zero_b, 0.0).then_inc(S("vector_consts"), 1)
            def adj_low(j):
                dve.wait_ge(S("adj_hi"), j + 1)
                dve.tensor_tensor(AT_lo[:, 0:3, cut(j * T, T)], ps[0:T, 4, 0:3 * T].rearrange("p (s n) -> p s n", s=3),
                                  f(AT_hi[:, 0:3, cut(j * T, T)]), ALU.subtract)
                dve.tensor_tensor(AT_lo[:, 3:5, cut(j * T, T)], ps[0:T, 5, 0:2 * T].rearrange("p (s n) -> p s n", s=2),
                                  f(AT_hi[:, 3:5, cut(j * T, T)]), ALU.subtract).then_inc(S("adj_lo"), 1)

            for j in range(NT):
                lo = dve.value_load(lohi_i[0:1, 0, j:j + 1], min_val=0, max_val=CH - 1)
                steps = dve.value_load(lohi_i[0:1, 1, j:j + 1], min_val=1, max_val=NG)
                with dve.Fori(0, steps) as q:
                    for i in range(G):
                        dve.wait_ge(S(f"one_hot_free{j}"), q * G + i + 1)
                        dve.tensor_scalar(one_hot_src[:, i, :], iota_h, srcf[:, bass.ds(lo + q * G + i, 1)], None, ALU.is_equal)
                        dve.tensor_scalar(one_hot_dst[:, i, :], iota_h[:, 0:T + 1], dstrel[:, j, bass.ds(lo + q * G + i, 1)], None,
                                          ALU.is_equal).then_inc(S(f"one_hot{j}"), 1)
                if j >= 2:
                    adj_low(j - 2)
            adj_low(NT - 2)
            adj_low(NT - 1)

            def cw_add(L, t):
                dve.wait_ge(S("cw_ps"), NT * L + t + 1)
                dve.tensor_tensor(XO[:, t, :], XO[:, t, :], ps[0:T, 7, :], ALU.add).then_inc(S("cw_add"), 1)

            for L in range(NL):
                dve.wait_ge(S("zmax_all"), L + 1)
                dve.tensor_scalar(zmx[:, NT + 2:NT + 3], zmx[:, NT + 1:NT + 2], -1.0, LIFT, ALU.mult, ALU.add).then_inc(S("zmax_neg"), 1)
                for t in range(NT + 1):
                    n = NT * L + t
                    if t < NT:
                        dve.wait_ge(S("exp"), n + 1)
                        if t >= 2:
                            dve.wait_ge(S("em_lo"), n - 1)
                        dve.tensor_tensor(EP[t % 2], EE[t % 2], HN[:, t, :], ALU.mult).then_inc(S("em"), 1)
                    if t >= 1:
                        dve.wait_ge(S("em_hi"), n)
                        dve.tensor_tensor(EM[1][:, t - 1, :], EP[(t - 1) % 2], f(EM[0][:, t - 1, :]), ALU.subtract).then_inc(S("em_lo"), 1)
                    if t < NT:
                        dve.wait_ge(S("e_hi"), n + 1)
                        dve.tensor_tensor(EX[1][:, t, :], EE[t % 2], f(EX[0][:, t, :]), ALU.subtract).then_inc(S("e_lo"), 1)
                if L:
                    cw_add(L - 1, NT - 1)
                split_lo(f"w1_{L}0")
                split_lo(f"w1_{L}1")

                def new_h(d):
                    b = AGG_BANK[d]
                    dve.wait_ge(S("agg_ps"), NT * L + d + 1)
                    v1(dve.tensor_scalar(LN, ps[0:T, b, :], 1e-37, None, ALU.max))
                    v1(dve.reciprocal(LN, LN))
                    v1(dve.tensor_tensor(LN2, ps[0:T, b + 1, :], LN, ALU.mult))
                    dve.tensor_tensor(HN[:, d, :], LN2, XC[:, d, :], ALU.add).then_inc(S("h"), 1)

                def h_lo(i):
                    dve.wait_ge(S("ht_hi"), NT * L + i + 1)
                    dve.tensor_tensor(HT[i % 2][1], ps[:, 4, 0:4 * T], f(HT[i % 2][0]), ALU.subtract).then_inc(S("ht_lo"), 1)

                def y_stats(i):
                    n = NT * L + i
                    dve.wait_ge(S("w1_ps"), n + 1)
                    if n >= 2:
                        dve.wait_ge(S("y_tr"), n - 1)
                    if n == 1:
                        dve.wait_ge(S("y_zero"), 16 * NT)
                    v1(dve.tensor_tensor(YY[i % 2].rearrange("p (a b) -> p a b", a=2), ps[0:T, 0:2, :],
                                         BC1.rearrange("p (a b) -> p a b", a=2), ALU.add))
                    dve.sem_inc(S("y_sb"), 1)
                    dve.bn_stats(st_m[:, 0, :], YY[i % 2][:, 0:D])
                    v1(dve.bn_stats(st_m[:, 1, :], YY[i % 2][:, D:H]))
                    if n >= 1:
                        dve.wait_ge(S("y_norm"), n)
                    v1(dve.bn_aggr(mv_m[:, 0:2], st_m[:].rearrange("p a b -> p (a b)")))
                    dve.tensor_scalar(mv_m[:, 1:2], mv_m[:, 1:2], 1e-5, None, ALU.add).then_inc(S("mlp_var"), 1)

                def y_scale(i):
                    dve.wait_ge(S("mlp_rstd"), NT * L + i + 1)
                    dve.scalar_tensor_tensor(out=mv_m[:, 3:4], in0=mv_m[:, 0:1], scalar=-1.0, in1=mv_m[:, 2:3],
                                             op0=ALU.mult, op1=ALU.mult).then_inc(S("mlp_nmr"), 1)

                def new_x(t):
                    dve.wait_ge(S("w2_ps"), NT * L + t + 1)
                    if L == 0:
                        v1(dve.tensor_tensor(XC[:, t, :], ps[0:T, 5, :], BC2, ALU.add))
                        dve.sem_inc(S("w2_sb"), 1)
                    else:
                        v1(dve.tensor_tensor(LN, ps[0:T, 5, :], BC2, ALU.add))
                        dve.sem_inc(S("w2_sb"), 1)
                        v1(dve.bn_stats(st_o[:, 0, :], LN))
                        v1(dve.bn_aggr(mv_o[:, 0:2], st_o[:, 0, :]))
                        dve.tensor_scalar(mv_o[:, 1:2], mv_o[:, 1:2], 1e-5, None, ALU.add).then_inc(S("out_var"), 1)
                        dve.wait_ge(S("out_rstd"), NT * (L - 1) + t + 1)
                        v1(dve.scalar_tensor_tensor(out=LN, in0=LN, scalar=mv_o[:, 0:1], in1=BCG, op0=ALU.subtract, op1=ALU.mult))
                        v1(dve.scalar_tensor_tensor(out=LN2, in0=LN, scalar=mv_o[:, 2:3], in1=BCB, op0=ALU.mult, op1=ALU.add))
                        v1(dve.scalar_tensor_tensor(out=XC[:, t, :], in0=LN2, scalar=0.0, in1=XC[:, t, :], op0=ALU.max, op1=ALU.add))
                    dve.sem_inc(S("x_next"), 1)
                    if L + 1 < NL:
                        message(L + 1, t)

                new_h(0)
                new_h(1)
                split_lo(f"cw_{L}")
                new_h(2)
                new_h(3)
                h_lo(0)
                h_lo(1)
                new_h(4)
                dve.wait_ge(S("rows_in"), 32 + 64 * L)
                y_stats(0)
                h_lo(2)
                split_lo(f"w2_{L}0")
                y_scale(0)
                y_stats(1)
                split_lo(f"w2_{L}1")
                y_scale(1)
                for i in range(NT + 1):
                    n = NT * L + i
                    if i < NT:
                        for h in range(2):
                            dve.wait_ge(S("r_hi"), 2 * n + h + 1)
                            dve.tensor_tensor(RT[1][:, cut(500 * h, 500)], RR[:, cut(500 * h, 500)], f(RT[0][:, cut(500 * h, 500)]),
                                              ALU.subtract).then_inc(S("r_lo"), 1)
                    if i + 3 < NT:
                        h_lo(i + 3)
                    if i + 2 < NT:
                        y_stats(i + 2)
                    if i >= 1:
                        dve.wait_ge(S("xi_hi"), n)
                        dve.tensor_tensor(XI[1], ps[:, 6, 0:4 * T], f(XI[0]), ALU.subtract).then_inc(S("xi_lo"), 1)
                    if i + 2 < NT:
                        y_scale(i + 2)
                    if L == NL - 1 and i == NT - 1:
                        split_lo("sg0")
                        split_lo("sd0")
                    if i < NT:
                        new_x(i)
                    if i >= 1 and (i < NT or L == NL - 1):
                        cw_add(L, i - 1)

            def shared_add(t):
                dve.wait_ge(S("shared_ps"), t + 1)
                dve.scalar_tensor_tensor(out=XO[:, t, :], in0=ps[0:T, 7, :], scalar=0.5, in1=XO[:, t, :],
                                         op0=ALU.mult, op1=ALU.add).then_inc(S("shared_add"), 1)

            def shared_lo(n):
                dve.wait_ge(S("s_t_hi"), n + 1)
                dve.tensor_tensor(ST[1], ps[:, 6, 0:2 * T], f(ST[0]), ALU.subtract).then_inc(S("s_t_lo"), 1)

            def shared_step(n):
                if n >= 1:
                    shared_lo(n - 1)
                if n >= 3 and n % 2 == 1:
                    shared_add((n - 3) // 2)
                dve.wait_ge(S("silu"), n + 1)
                if n >= 2:
                    dve.wait_ge(S("ht_ps"), n - 1)
                dve.tensor_tensor(HG[n % 2][0:T, :], ps[0:T, 2 + n % 2, F:2 * F], SIL[n % 2][0:T, :], ALU.mult).then_inc(S("hg"), 1)

            row_stats("fin_var", "fin_rstd", "fin_norm")
            tr_lo("fin")
            for nme in ("sg1", "sd1"):
                split_lo(nme)
            dve.wait_ge(S("rbias_in"), 16)
            for t in range(NT):
                dve.wait_ge(S("router_ps"), t + 1)
                v1(dve.tensor_tensor(LOG[:, t, :], ps[0:T, 2 + t % 2, 0:E], RBC, ALU.add))
                dve.sem_inc(S("log_sb"), 1)
                v1(dve.tensor_reduce(rsm[:, 0, cut(t, 1)], LOG[:, t, :], axis=AX.X, op=ALU.max))
                dve.tensor_scalar(rsm[:, 0, cut(t, 1)], rsm[:, 0, cut(t, 1)], -1.0, None, ALU.mult).then_inc(S("log_max"), 1)
            dve.wait_ge(S("log_exp"), NT)
            v1(dve.reciprocal(rsm[:, 2, :], rsm[:, 1, :]))
            for t in range(NT):
                last = dve.tensor_scalar(PRB[:, t, :], PRB[:, t, :], rsm[:, 2, cut(t, 1)], None, ALU.mult)
            v1(last)
            for t in range(NT):
                last = dve.max(r8[:, t, :], PRB[:, t, :])
            v1(last)
            v1(dve.tensor_reduce(rsm[:, 3, :], r8[:, :, 0:TOPK], axis=AX.X, op=ALU.add))
            v1(dve.tensor_scalar(rsm[:, 3, :], rsm[:, 3, :], 1e-9, None, ALU.add))
            v1(dve.reciprocal(rsm[:, 3, :], rsm[:, 3, :]))
            v1(dve.memset(r8[:, :, TOPK:8], -5.0))
            for t in range(NT):
                last = dve.match_replace(MSK[:, t, :], r8[:, t, :], PRB[:, t, :], -1.0)
            v1(last)
            v1(dve.tensor_scalar(MSK, MSK, -1.0, None, ALU.is_equal))
            dve.tensor_copy(MSKB, MSK).then_inc(S("mask"), 1)
            for t in range(NT):
                last = dve.scalar_tensor_tensor(out=GAT[:, t, :], in0=PRB[:, t, :], scalar=rsm[:, 3, cut(t, 1)], in1=MSK[:, t, :],
                                                op0=ALU.mult, op1=ALU.mult)
            v1(last)
            shared_step(0)
            v1(dve.memset(GR[:, 2, 0:E], 1.0))
            for t in range(NT):
                last = dve.tensor_tensor_scan(KRK[:, t, :], GR[:, 2, 0:E], MSK[:, t, :], 0.0, ALU.mult, ALU.add)
            v1(last)
            v1(dve.tensor_tensor(KRK, KRK, MSK, ALU.subtract))
            dve.wait_ge(S("iota"), 3)
            v1(dve.tensor_copy(eoff, eoff_i))
            v1(dve.scalar_tensor_tensor(out=KRK, in0=MSK, scalar=-FAR, in1=KRK, op0=ALU.mult, op1=ALU.add))
            dve.wait_ge(S("pos_ps"), 1)
            v1(dve.tensor_copy(POS, ps[0:T, 4, 0:NT * E].rearrange("p (t e) -> p t e", t=NT)))
            dve.tensor_scalar(LOG, POS, float(CAP), SKIP, ALU.is_ge, ALU.mult)
            v1(dve.tensor_tensor(ADR, POS, eoff.unsqueeze(1).to_broadcast([T, NT, E]), ALU.add))
            v1(dve.tensor_tensor(ADR, ADR, LOG, ALU.add))
            for k in range(TOPK):
                last = dve.scalar_tensor_tensor(out=BYK[:, :, k, :], in0=KRK, scalar=k - FAR, in1=ADR, op0=ALU.is_equal, op1=ALU.mult)
            v1(last)
            shared_step(1)
            v1(dve.tensor_reduce(adr_f, BYK, axis=AX.X, op=ALU.add))
            dve.tensor_copy(adr_i, adr_f)
            for k in range(TOPK):
                last = dve.scalar_tensor_tensor(out=BYK[:, :, k, :], in0=KRK, scalar=k - FAR, in1=GAT, op0=ALU.is_equal, op1=ALU.mult)
            v1(last)
            shared_step(2)
            dve.tensor_reduce(f(PAY[:, :, :, 2]), BYK, axis=AX.X, op=ALU.add).then_inc(S("choices"), 1)

            for n in range(3, 2 * NT):
                shared_step(n)
            shared_lo(2 * NT - 1)
            shared_add(NT - 1)

            def after(name, value):
                if not isinstance(value, int) or value > 0:
                    dve.wait_ge(S(name), value)

            def gated(e, col, ahead, r, turn):
                dve.wait_ge(S("silu"), NSH + e + 1)
                if ahead is not None:
                    dve.tensor_copy(tok_c[:, cut(r, 1)].unsqueeze(2), slots[:, ahead, 0:1]).then_inc(S("tok_col"), 1)
                dve.wait_ge(S("ht_ps"), NSH + e - 1)
                dve.tensor_tensor(HG[r % 2][0:CAP, :], ps[0:CAP, 2 + r % 2, F:2 * F], SIL[r % 2][0:CAP, :], ALU.mult).then_inc(S("hg"), 1)
                after(f"y_out{r}", 16 * turn)
                dve.tensor_copy(row_c[:, cut(r, 1)].unsqueeze(2), slots[:, col, 1:2]).then_inc(S("row_col"), 1)
                dve.wait_ge(S("ht_ps"), NSH + e + 1)
                after("o_ps", e - 1)
                dve.tensor_copy(HTF[r % 2], ps[:, 4 + r % 2, 0:2 * CAP]).then_inc(S("ht_sb"), 1)

            dve.wait_ge(S("tables"), 16)
            for r in range(UNROLL):
                gated(r, cut(r, 1), cut(r + UNROLL, 1), r, 0)
            with dve.Fori(1, E // UNROLL - 1) as i:
                for r in range(UNROLL):
                    e = UNROLL * i + r
                    gated(e, bass.ds(e, 1), bass.ds(e + UNROLL, 1), r, i)
            for r in range(UNROLL):
                e = E - UNROLL + r
                gated(e, cut(e, 1), None, r, E // UNROLL - 1)
            for t in range(NT):
                dve.wait_ge(S(f"y_in{t}"), 16)
                if t >= 1:
                    dve.wait_ge(S("y_sum"), t)
                v1(dve.tensor_reduce(ysum, YL[t].rearrange("p a n -> p n a"), axis=AX.X, op=ALU.add))
                dve.tensor_tensor(XO[:, t, :], XO[:, t, :], ysum, ALU.add).then_inc(S("y_sum"), 1)

        @block.tensor
        def _(eng):
            def tr_x(norm, which):
                for t in range(NT):
                    pe.wait_ge(S(norm), t + 1)
                    if t >= 2:
                        pe.wait_ge(S(which + "_lo"), t - 1)
                    for k in range(KD):
                        last = pe.transpose(ps[:, t % 2, cut(k * T, T)], XC[:, t, cut(k * P, P)], ident[0:T, 0:T])
                    last.then_inc(S(which + "_tr"), 1)

            pe.wait_ge(S("pool_consts"), 1)
            tr_x("in_norm", "in")
            weights("wv")
            for t in range(NT):
                pe.wait_ge(S("in_lo"), t + 1)
                if t >= 2:
                    pe.wait_ge(S("v_sb"), t - 1)
                for k in range(KD):
                    last = mm3(ps[0:T, 2 + t % 2, :], sub(XT, A_, k, cut(t * T, T)), sub(WMA, A_, k, A_), k == 0, k == KD - 1)
                last.then_inc(S("v_ps"), 1)

            def proj(u, w):
                c, h = divmod(u % 8, 2)
                n0, nn = HALVES[h]
                if u >= 2:
                    pe.wait_ge(S("kt_sb"), u - 1)
                for k in range(KD):
                    last = mm3(ps[:, 4 + u % 2, 0:nn], sub(w, A_, k, cut(c * P, P)), sub(XT, A_, k, cut(n0, nn)), k == 0, k == KD - 1)
                last.then_inc(S("kt_ps"), 1)

            weights("wk")
            pe.wait_ge(S("pool_consts"), 2)
            for u in range(8):
                proj(u, WMB)
            weights("g")
            pe.wait_ge(S("kt_lo"), 8)
            for t in range(NT):
                if t >= 2:
                    pe.wait_ge(S("pk_ab"), t - 1)
                for c in range(KD):
                    last = mm3(phi_k_banks(t)[:, c, :, :].rearrange("p a n -> p (a n)"), sub(KT, A_, c, cut(t * T, T)),
                               (GM[0][:, 2:4, :], GM[1][:, 2:4, :]), True, True)
                last.then_inc(S("pk_ps"), 1)
            weights("wq")
            for u in range(8, 16):
                if u == 10:
                    pe.wait_ge(S("pk_lo"), NT)
                    pe.wait_ge(S("v_lo"), NT)
                    pe.wait_ge(S("vector_consts"), 1)
                    for c in range(KD):
                        b, o = c // 2, 256 * (c % 2)
                        for t in range(NT):
                            mm3(ps[:, b, cut(o, P)], sub(PK, A_, t, cut(c * P, P)), sub(VV, A_, t, cut(c * P, P)), t == 0, t == NT - 1)
                        for t in range(NT):
                            for part in range(2):
                                last = pe.matmul(ps[:, b, cut(o + P, P)], PK[part][:, t, cut(c * P, P)], ones_r[:],
                                                 start=(t == 0 and part == 0), stop=(t == NT - 1 and part == 1))
                    last.then_inc(S("kv_ps"), 1)
                    pe.wait_ge(S("member"), 1)
                    pe.wait_ge(S("pool_consts"), 3)
                    for j in range(NT):
                        b, q = (6, j) if j < 3 else (7, j - 3)
                        last = pe.matmul(ps[0:1, b, cut(q * CH, CH)], ones_b[:, 0:1], member[:, cut(j * CH, CH)], start=True, stop=True)
                    last.then_inc(S("member_ps"), 1)
                proj(u, WMA)
            pe.wait_ge(S("kt_lo"), 16)
            pe.wait_ge(S("ranges"), 1)
            for u in range(8):
                c, h = divmod(u, 2)
                n0, nn = HALVES[h]
                if u >= 2:
                    pe.wait_ge(S("pk_ab"), PKU + u - 1)
                mm3(ps[:, 2 + u % 2, 0:nn], sub(GM, A_, 0, A_), sub(QT, A_, c, cut(n0, nn)), True, True)
                mm3(ps[:, 6 + u % 2, 0:nn], sub(GM, A_, 1, A_), sub(QT, A_, c, cut(n0, nn)), True, True).then_inc(S("pk_ps"), 1)
            pe.wait_ge(S("kv_lo"), 1)
            pe.wait_ge(S("pk_ab"), PKU + 8)
            pe.wait_ge(S("pk_lo"), PKU + 8)
            pe.wait_ge(S("kt_sb"), 16)
            weights("wp")

            def attend(t):
                if t >= 2:
                    pe.wait_ge(S("attn"), t - 1)
                for c in range(KD):
                    last = mm3(attn_banks(t)[:, c, :, :].rearrange("p a n -> p (a n)"), sub(PQ, A_, c, cut(t * T, T)),
                               sub(KV, A_, c, A_), True, True)
                last.then_inc(S("attn_ps"), 1)

            def attn_transpose(t):
                pe.wait_ge(S("attn"), t + 1)
                if t >= 2:
                    pe.wait_ge(S("attn_lo"), t - 1)
                for k in range(KD):
                    last = pe.transpose(ps[:, t % 2, cut(k * T, T)], MT3[t % 2][0:T, cut(k * P, P)], ident[0:T, 0:T])
                last.then_inc(S("attn_tr"), 1)

            def mix_out(t):
                pe.wait_ge(S("attn_lo"), t + 1)
                if t >= 2:
                    pe.wait_ge(S("mix_out_add"), t - 1)
                for k in range(KD):
                    last = mm3(ps[0:T, 2 + t % 2, :], sub(OT, A_, k, cut(t * T, T)), sub(WMB, A_, k, A_), k == 0, k == KD - 1)
                last.then_inc(S("mix_out_ps"), 1)

            attend(0)
            for t in range(NT + 1):
                if t + 1 < NT:
                    attend(t + 1)
                if t < NT:
                    attn_transpose(t)
                if t >= 1:
                    mix_out(t - 1)

            pe.wait_ge(S("mix_out_add"), NT)
            pe.wait_ge(S("vector_consts"), 2)
            parts = [(0, 0, 313), (1, 313, 312)]

            def adj_transpose(j):
                pe.wait_ge(S("adj_sb"), j + 1)
                if j >= 1:
                    pe.wait_ge(S("adj_lo"), j)
                for s in range(NT):
                    b, q = (4, s) if s < 3 else (5, s - 3)
                    last = pe.transpose(ps[0:T, b, cut(q * T, T)], adj[:, j % 2, cut(s * T, T)], ident[0:T, 0:T])
                last.then_inc(S("adj_tr"), 1)

            for j in range(NT):
                steps = pe.value_load(lohi_i[0:1, 1, j:j + 1], min_val=1, max_val=NG)
                if j >= 2:
                    pe.wait_ge(S("adj_sb"), j - 1)
                for h, s0, sn in parts:
                    last = pe.matmul(ps[0:T, 2 * (j % 2) + h, 0:sn], zero_b[:, 0:T], zero_b[:, 0:sn], start=True, stop=False)
                last.then_inc(S(f"one_hot_free{j}"), G)
                with pe.Fori(0, steps) as q:
                    for i in range(G):
                        pe.wait_ge(S(f"one_hot{j}"), q * G + i + 1)
                        for h, s0, sn in parts:
                            last = pe.matmul(ps[0:T, 2 * (j % 2) + h, 0:sn], one_hot_dst[:, i, 0:T], one_hot_src[:, i, cut(s0, sn)],
                                             start=False, stop=False)
                        last.then_inc(S(f"one_hot_free{j}"), 1)
                for h, s0, sn in parts:
                    last = pe.matmul(ps[0:T, 2 * (j % 2) + h, 0:sn], zero_b[:, 0:T], zero_b[:, 0:sn], start=False, stop=True)
                last.then_inc(S("adj_ps"), 1)
                if j >= 1:
                    adj_transpose(j - 1)
            adj_transpose(NT - 1)

            pe.wait_ge(S("adj_lo"), NT)
            for L in range(NL):
                def aggregate(d, s):
                    b = AGG_BANK[d]
                    a = (AT_hi[:, s, cut(d * T, T)], AT_lo[:, s, cut(d * T, T)])
                    mm3(ps[0:T, b, :], a, sub(EX, A_, s, A_), s == 0, s == NT - 1)
                    last = mm3(ps[0:T, b + 1, :], a, sub(EM, A_, s, A_), s == 0, s == NT - 1)
                    if s == NT - 1:
                        last.then_inc(S("agg_ps"), 1)

                def h_tr(i):
                    n = NT * L + i
                    pe.wait_ge(S("h"), n + 1)
                    if n >= 1:
                        pe.wait_ge(S("ht_lo"), n)
                    for k in range(KD):
                        last = pe.transpose(ps[:, 4, cut(k * T, T)], HN[:, i, cut(k * P, P)], ident[0:T, 0:T])
                    last.then_inc(S("h_tr"), 1)

                def times_w1(i):
                    n = NT * L + i
                    pe.wait_ge(S("ht_lo"), n + 1)
                    if i:
                        pe.wait_ge(S("y_sb"), n)
                    else:
                        pe.wait_ge(S("h"), NT * L + 4)
                    for b in range(2):
                        for k in range(KD):
                            last = mm3(ps[0:T, b, :], sub(HT[i % 2], A_, cut(k * T, T)), sub(W1, A_, k, cut(b * D, D)), k == 0, k == KD - 1)
                    last.then_inc(S("w1_ps"), 1)

                if L:
                    pe.wait_ge(S("relu"), 2 * NT * L)
                for s in range(NT):
                    pe.wait_ge(S("e_lo"), NT * L + s + 1)
                    pe.wait_ge(S("em_lo"), NT * L + s + 1)
                    for d in range(2):
                        aggregate(d, s)
                if L:
                    pe.wait_ge(S("cw_add"), NT * L)
                for d in range(2, NT):
                    if d >= 3:
                        pe.wait_ge(S("h"), NT * L + d - 2)
                    for s in range(NT):
                        aggregate(d, s)

                h_tr(0)
                h_tr(1)
                weights(f"w1_{L}1")
                times_w1(0)
                h_tr(2)
                times_w1(1)
                pe.wait_ge(S("h"), NT * (L + 1))
                for i in range(NT + 1):
                    n = NT * L + i
                    if i < NT:
                        pe.wait_ge(S("y_norm"), n + 1)
                        if n >= 1:
                            pe.wait_ge(S("relu"), 2 * n)
                        for k in range(KH):
                            last = pe.transpose(ps[:, 2 + k // 4, cut((k % 4) * T, T)], YY[i % 2][:, cut(k * P, P)], ident[0:T, 0:T])
                        last.then_inc(S("y_tr"), 1)
                    if i + 2 < NT:
                        times_w1(i + 2)
                    if i + 3 < NT:
                        h_tr(i + 3)
                    if i >= 1:
                        m = n - 1
                        pe.wait_ge(S("x_next"), m + 1)
                        if m >= 1:
                            pe.wait_ge(S("xi_lo"), m)
                        for k in range(KD):
                            last = pe.transpose(ps[:, 6, cut(k * T, T)], XC[:, i - 1, cut(k * P, P)], ident[0:T, 0:T])
                        last.then_inc(S("x_tr"), 1)
                    if i < NT:
                        if i == 0:
                            weights(f"w2_{L}1")
                        pe.wait_ge(S("r_lo"), 2 * (n + 1))
                        if n >= 1:
                            pe.wait_ge(S("w2_sb"), n)
                        for k in range(KH):
                            last = mm3(ps[0:T, 5, :], sub(RT, A_, cut(k * T, T)), sub(W2, A_, k, A_), k == 0, k == KH - 1)
                        last.then_inc(S("w2_ps"), 1)
                    if i >= 1:
                        m = n - 1
                        if i == 1:
                            weights(f"cw_{L}")
                        pe.wait_ge(S("xi_lo"), m + 1)
                        if m >= 1:
                            pe.wait_ge(S("cw_add"), m)
                        for k in range(KD):
                            last = mm3(ps[0:T, 7, :], sub(XI, A_, cut(k * T, T)), sub(CW, A_, k, A_), k == 0, k == KD - 1)
                        last.then_inc(S("cw_ps"), 1)

            tr_x("fin_norm", "fin")
            pe.wait_ge(S("rw_in"), 16)
            for t in range(NT):
                pe.wait_ge(S("fin_lo"), t + 1)
                if t >= 2:
                    pe.wait_ge(S("log_sb"), t - 1)
                for k in range(KD):
                    for part in range(2):
                        last = pe.matmul(ps[0:T, 2 + t % 2, 0:E], f(XT[part][:, k, cut(t * T, T)]), RW[:, k, :],
                                         start=(k == 0 and part == 0), stop=(k == KD - 1 and part == 1))
                last.then_inc(S("router_ps"), 1)

            def ranks():
                pe.wait_ge(S("mask"), 1)
                for t in range(NT):
                    for q in range(t):
                        pe.matmul(ps[0:T, 4, cut(t * E, E)], ones_b[:, 0:T], MSKB[:, q, :], start=(q == 0), stop=False)
                    last = pe.matmul(ps[0:T, 4, cut(t * E, E)], tri[:], MSKB[:, t, :], start=(t == 0), stop=True)
                last.then_inc(S("pos_ps"), 1)

            weights("sd1")
            pe.wait_ge(S("log_sb"), NT)

            def shared_down(n):
                t, s = divmod(n, 2)
                pe.wait_ge(S("s_t_lo"), n + 1)
                if s == 0 and t >= 1:
                    pe.wait_ge(S("shared_add"), t)
                for k in range(2):
                    last = mm3(ps[0:T, 7, :], sub(ST, A_, cut(k * T, T)), sub(SD[s], A_, k, A_), s == 0 and k == 0, s == 1 and k == 1)
                if s == 1:
                    last.then_inc(S("shared_ps"), 1)

            for n in range(2 * NT):
                t, s = divmod(n, 2)
                if n >= 2:
                    pe.wait_ge(S("hg"), n - 1)
                for k in range(KD):
                    last = mm3(ps[0:T, 2 + n % 2, :], sub(XT, A_, k, cut(t * T, T)), sub(SG[s], A_, k, A_), k == 0, k == KD - 1)
                last.then_inc(S("gu_ps"), 1)
                if n == 0:
                    ranks()
                if n >= 1:
                    shared_down(n - 1)
                pe.wait_ge(S("hg"), n + 1)
                for k in range(2):
                    last = pe.transpose(ps[:, 6, cut(k * T, T)], HG[n % 2][0:T, cut(k * P, P)], ident[0:T, 0:T])
                last.then_inc(S("ht_ps"), 1)
            shared_down(2 * NT - 1)

            def after(name, value):
                if not isinstance(value, int) or value > 0:
                    pe.wait_ge(S(name), value)

            def transpose_x(e, r, turn):
                pe.wait_ge(S(f"xg_in{r}"), 16 * turn + 16)
                after("xe_sb", e - 1)
                for k in range(KD):
                    last = pe.transpose(ps[:, r % 2, cut(k * CAP, CAP)], XG[r][:, cut(k * P, P)], ident[0:CAP, 0:CAP])
                last.then_inc(S("xe_ps"), 1)

            def gate_up(e, r, turn):
                pe.wait_ge(S(f"ring_in{r}"), 16 * turn + 16)
                pe.wait_ge(S("xe_sb"), e + 1)
                after("hg", NSH + e - 1)
                for k in range(KD):
                    last = pe.matmul(ps[0:CAP, 2 + r % 2, :], XE[r % 2][:, cut(k * CAP, CAP)], RING[r][:, cut(512 * k, 512)],
                                     start=(k == 0), stop=(k == KD - 1))
                last.then_inc(S("gu_ps"), 1)

            def down(e, r):
                pe.wait_ge(S("ht_sb"), e + 1)
                after("scaled", e - 1)
                for k in range(2):
                    last = pe.matmul(ps[0:CAP, 6 + r % 2, :], HTF[r % 2][:, cut(k * CAP, CAP)], RING[r][:, cut(2048 + 512 * k, 512)],
                                     start=(k == 0), stop=(k == 1))
                last.then_inc(S("o_ps"), 1)

            def transpose_h(e, r):
                pe.wait_ge(S("hg"), NSH + e + 1)
                after("ht_sb", e - 1)
                for k in range(2):
                    last = pe.transpose(ps[:, 4 + r % 2, cut(k * CAP, CAP)], HG[r % 2][0:CAP, cut(k * P, P)], ident[0:CAP, 0:CAP])
                last.then_inc(S("ht_ps"), 1)

            pe.wait_ge(S("shared_add"), NT)
            transpose_x(0, 0, 0)
            for r in range(UNROLL):
                transpose_x(r + 1, (r + 1) % UNROLL, (r + 1) // UNROLL)
                gate_up(r, r, 0)
                if r >= 1:
                    down(r - 1, r - 1)
                transpose_h(r, r)
            with pe.Fori(1, E // UNROLL - 1) as i:
                for r in range(UNROLL):
                    e = UNROLL * i + r
                    transpose_x(e + 1, (r + 1) % UNROLL, i + 1 if r == UNROLL - 1 else i)
                    gate_up(e, r, i)
                    down(e - 1, (r - 1) % UNROLL)
                    transpose_h(e, r)
            turn = E // UNROLL - 1
            for r in range(UNROLL):
                e = E - UNROLL + r
                if e + 1 < E:
                    transpose_x(e + 1, r + 1, turn)
                gate_up(e, r, turn)
                down(e - 1, (r - 1) % UNROLL)
                transpose_h(e, r)
            down(E - 1, UNROLL - 1)


def kernel(**inputs):
    import numpy as np
    import concourse.bacc as bacc
    from concourse import mybir as mb
    from concourse.bass_utils import run_bass_kernel_spmd as run

    g = {k: np.asarray(v) for k, v in inputs.items()}
    gn, mx, ff = (lambda n: g["L0_gnn_" + n]), (lambda n: g["L0_mix_" + n]), (lambda n: g["L0_ffn_" + n])

    def column(v):
        return v.reshape(-1, P).T

    def pack(gate, up, down):
        n = gate.shape[0]
        gu = np.concatenate([gate, up], axis=1).transpose(0, 2, 1).reshape(n, KD, P, 2 * F).transpose(0, 2, 1, 3)
        dn = down.transpose(0, 2, 1).reshape(n, 2, P, D).transpose(0, 2, 1, 3)
        return np.concatenate([gu.reshape(n, P, -1), dn.reshape(n, P, -1)], axis=2)

    scalars = [mx("gamma_q"), mx("beta_q"), mx("gamma_k"), mx("beta_k"), gn("t0"), gn("t1"), gn("t2")]
    cols = np.concatenate([column(gn(f"mlg_{L}")) for L in range(NL)] + [column(gn(f"mlb_{L}")) for L in range(NL)]
                          + [column(mx("bq")), column(mx("bk"))] + [np.broadcast_to(s, (P, 1)) for s in scalars], axis=1)
    rows = [mx("bv"), mx("bp"), gn("cb"), gn("mb1_0"), gn("mb2_0")]
    for L in range(1, NL):
        rows += [gn(f"mb1_{L}"), gn(f"mb2_{L}"), gn(f"lng_{L}"), gn(f"lnb_{L}")]
    ins = {
        "x": g["x"], "src": g["src"].reshape(CH, T).T, "dst": g["dst"].reshape(CH, T).T,
        "cols": cols, "rows": np.concatenate(rows),
        "w1": np.stack([gn(f"mw1_{L}") for L in range(NL)]), "w2": np.stack([gn(f"mw2_{L}") for L in range(NL)]),
        "cw": gn("cw"), "wmix": np.stack([mx(n) for n in ("Wq", "Wk", "Wv", "Wp")]),
        "gmix": np.stack([mx(n) for n in ("qG1", "qG2", "kG1", "kG2")]),
        "router": ff("router_w").T, "rbias": ff("bias"),
        "shared": pack(ff("shared_w_gate"), ff("shared_w_up"), ff("shared_w_down")),
        "experts": pack(ff("w_gate"), ff("w_up"), ff("w_down")),
    }
    nc = bacc.Bacc("TRN2", target_bir_lowering=False, num_devices=1)
    arrays, args = {}, []
    for name, a in ins.items():
        a = np.ascontiguousarray(a)
        arrays[name + "_in"] = a
        args.append(nc.dram_tensor(name + "_in", a.shape, mb.dt.from_np(a.dtype), kind="ExternalInput").ap())
    args.append(nc.dram_tensor("out_x", (N, D), mb.dt.float32, kind="ExternalOutput").ap())
    gps_kernel(nc, *args)
    return run(nc, [arrays], core_ids=[0]).results[0]["out_x"]
```
